# Optimizing a Trainium2 kernel written in Bass

```python
import numpy as np
import jax
import jax.numpy as jnp

def _softmax(x, axis=-1):
    return jax.nn.softmax(x, axis=axis)

def _gelu(x):
    return jax.nn.gelu(x, approximate=True)

def _silu(x):
    return jax.nn.silu(x)

def _sigmoid(x):
    return jax.nn.sigmoid(x)

def _layernorm(x, axis=-1, eps=1e-05):
    m = jnp.mean(x, axis=axis, keepdims=True)
    v = jnp.var(x, axis=axis, keepdims=True)
    return (x - m) / jnp.sqrt(v + eps)

def _scatter_add(tgt, idx, src, axis=0):
    return tgt.at[idx].add(src)

def _segment_sum(src, seg, n):
    return jax.ops.segment_sum(src, seg, n)
kernel_name = 'mk_vit_tower_cls_d1_tok_img2048_r4_435e9f'

def setup_inputs(seed: int=0):
    np.random.seed(seed)
    _w = jnp.asarray

    def _rec_inputs():
        import jax
        import jax.numpy as jnp
        _rk = jax.random.key(seed)
        x = -0.00340659 + 1.00146 * jax.random.normal(jax.random.fold_in(_rk, 1), (8, 256, 64, 2), jnp.float32)
        cls_tok = 0.02 * jax.random.normal(jax.random.fold_in(_rk, 5), (1, 1, 512), jnp.float32)
        return (x, cls_tok)
    x, cls_tok = _rec_inputs()

    def _L0_tok_setup():
        import jax, jax.numpy as jnp
        import numpy as np
        CH, H, N, N_SSM, SEQ_L = (1, 256, 64, 256, 512)

        def _kernel(C_ri, log_dt, B_ri, inv_A_real, A_imag, L):
            C = C_ri[..., 0] + 1j * C_ri[..., 1]
            B = B_ri[..., 0] + 1j * B_ri[..., 1]
            A = -jnp.exp(inv_A_real) + 1j * A_imag
            rep = log_dt.shape[0] // inv_A_real.shape[0]
            B = jnp.tile(B, (rep, 1))
            A = jnp.tile(A, (rep, 1))
            dt = jnp.exp(log_dt)
            dtA = A * dt[:, None]
            Ct = B[None] * C / (1.0 - dtA / 2) * dt[:, None]
            dA = (1.0 + dtA / 2) / (1.0 - dtA / 2)
            dA_log = jnp.log(dA)
            l = jnp.arange(L, dtype=jnp.float32)
            V = jnp.exp(dA_log[:, :, None] * l)
            K = 2.0 * jnp.einsum('chn,hnl->chl', Ct, V).real
            return K
        key = jax.random.key(seed)
        ks = jax.random.split(key, 5)
        return {'C_ri': jax.random.normal(ks[0], (CH, H, N, 2), dtype=jnp.float32), 'log_dt': jax.random.normal(ks[1], (H,), dtype=jnp.float32), 'B_ri': jax.random.normal(ks[2], (N_SSM, N, 2), dtype=jnp.float32), 'inv_A_real': jax.random.normal(ks[3], (N_SSM, N), dtype=jnp.float32), 'A_imag': jax.random.normal(ks[4], (N_SSM, N), dtype=jnp.float32), 'L': SEQ_L}
    _L0_tok_all = _L0_tok_setup()
    _L0_tok_in = {k: v for k, v in _L0_tok_all.items() if k in ('log_dt', 'B_ri', 'inv_A_real', 'A_imag')}
    del _L0_tok_all

    def _L0_attn_setup():
        import jax, jax.numpy as jnp
        import numpy as np
        B, S, D, H = (4, 512, 512, 16)
        DH = D // H
        key = jax.random.key(seed)
        ks = jax.random.split(key, 11)
        p = 0.02
        return {'x': jax.random.normal(ks[0], (B, S, D), jnp.float32), 'Wq': jax.random.normal(ks[1], (D, D), jnp.float32) * p, 'bq': jax.random.normal(ks[2], (D,), jnp.float32) * p, 'Wk': jax.random.normal(ks[3], (D, D), jnp.float32) * p, 'bk': jax.random.normal(ks[4], (D,), jnp.float32) * p, 'Wv': jax.random.normal(ks[5], (D, D), jnp.float32) * p, 'bv': jax.random.normal(ks[6], (D,), jnp.float32) * p, 'Wo': jax.random.normal(ks[7], (D, D), jnp.float32) * p, 'bo': jax.random.normal(ks[8], (D,), jnp.float32) * p, 'spiral_weight': jax.random.normal(ks[9], (H,), jnp.float32), 'helix_rotation': jax.random.normal(ks[10], (D,), jnp.float32)}
    _L0_attn_all = _L0_attn_setup()
    _L0_attn_in = {k: v for k, v in _L0_attn_all.items() if k in ('Wq', 'bq', 'Wk', 'bk', 'Wv', 'bv', 'Wo', 'bo', 'spiral_weight', 'helix_rotation')}
    del _L0_attn_all

    def _L0_ffn_setup():
        import jax, jax.numpy as jnp
        import numpy as np
        B, S, H, E, D, K = (2, 512, 512, 8, 512, 2)
        key = jax.random.key(seed)
        ks = jax.random.split(key, 4)
        return {'x': jax.random.normal(ks[0], (B, S, H), jnp.float32), 'router_w': jax.random.normal(ks[1], (H, E), jnp.float32) / np.sqrt(H).astype(np.float32), 'router_b': jnp.zeros((E,), jnp.float32), 'expert_w': jax.random.normal(ks[2], (E, H, D), jnp.float32) / np.sqrt(H).astype(np.float32), 'expert_b': jnp.zeros((E, D), jnp.float32), 'out_w': jax.random.normal(ks[3], (D, D), jnp.float32) / np.sqrt(D).astype(np.float32), 'out_b': jnp.zeros((D,), jnp.float32)}
    _L0_ffn_all = _L0_ffn_setup()
    _L0_ffn_in = {k: v for k, v in _L0_ffn_all.items() if k in ('router_w', 'router_b', 'expert_w', 'expert_b', 'out_w', 'out_b')}
    del _L0_ffn_all
    return {'x': x, 'cls_tok': cls_tok, 'L0_tok_log_dt': _L0_tok_in['log_dt'], 'L0_tok_B_ri': _L0_tok_in['B_ri'], 'L0_tok_inv_A_real': _L0_tok_in['inv_A_real'], 'L0_tok_A_imag': _L0_tok_in['A_imag'], 'L0_attn_Wq': _L0_attn_in['Wq'], 'L0_attn_bq': _L0_attn_in['bq'], 'L0_attn_Wk': _L0_attn_in['Wk'], 'L0_attn_bk': _L0_attn_in['bk'], 'L0_attn_Wv': _L0_attn_in['Wv'], 'L0_attn_bv': _L0_attn_in['bv'], 'L0_attn_Wo': _L0_attn_in['Wo'], 'L0_attn_bo': _L0_attn_in['bo'], 'L0_attn_spiral_weight': _L0_attn_in['spiral_weight'], 'L0_attn_helix_rotation': _L0_attn_in['helix_rotation'], 'L0_ffn_router_w': _L0_ffn_in['router_w'], 'L0_ffn_router_b': _L0_ffn_in['router_b'], 'L0_ffn_expert_w': _L0_ffn_in['expert_w'], 'L0_ffn_expert_b': _L0_ffn_in['expert_b'], 'L0_ffn_out_w': _L0_ffn_in['out_w'], 'L0_ffn_out_b': _L0_ffn_in['out_b']}

def reference(x, cls_tok, L0_tok_log_dt, L0_tok_B_ri, L0_tok_inv_A_real, L0_tok_A_imag, L0_attn_Wq, L0_attn_bq, L0_attn_Wk, L0_attn_bk, L0_attn_Wv, L0_attn_bv, L0_attn_Wo, L0_attn_bo, L0_attn_spiral_weight, L0_attn_helix_rotation, L0_ffn_router_w, L0_ffn_router_b, L0_ffn_expert_w, L0_ffn_expert_b, L0_ffn_out_w, L0_ffn_out_b):
    import jax
    import jax.numpy as jnp

    def _L0_tok_ref(C_ri, log_dt, B_ri, inv_A_real, A_imag, L):
        import jax, jax.numpy as jnp
        import numpy as np
        CH, H, N, N_SSM, SEQ_L = (1, 256, 64, 256, 512)

        def _kernel(C_ri, log_dt, B_ri, inv_A_real, A_imag, L):
            C = C_ri[..., 0] + 1j * C_ri[..., 1]
            B = B_ri[..., 0] + 1j * B_ri[..., 1]
            A = -jnp.exp(inv_A_real) + 1j * A_imag
            rep = log_dt.shape[0] // inv_A_real.shape[0]
            B = jnp.tile(B, (rep, 1))
            A = jnp.tile(A, (rep, 1))
            dt = jnp.exp(log_dt)
            dtA = A * dt[:, None]
            Ct = B[None] * C / (1.0 - dtA / 2) * dt[:, None]
            dA = (1.0 + dtA / 2) / (1.0 - dtA / 2)
            dA_log = jnp.log(dA)
            l = jnp.arange(L, dtype=jnp.float32)
            V = jnp.exp(dA_log[:, :, None] * l)
            K = 2.0 * jnp.einsum('chn,hnl->chl', Ct, V).real
            return K
        return _kernel(C_ri, log_dt, B_ri, inv_A_real, A_imag, L)

    def _L0_attn_ref(x, Wq, bq, Wk, bk, Wv, bv, Wo, bo, spiral_weight, helix_rotation):
        import jax, jax.numpy as jnp
        import numpy as np
        B, S, D, H = (4, 512, 512, 16)
        DH = D // H
        b, s, d = x.shape
        h, dh = (H, d // H)
        q = (x @ Wq.T + bq).reshape(b, s, h, dh)
        k = (x @ Wk.T + bk).reshape(b, s, h, dh)
        v = (x @ Wv.T + bv).reshape(b, s, h, dh)
        rot = helix_rotation.reshape(h, dh)
        q = q * jnp.cos(rot)
        k = k * jnp.sin(rot)
        scores = jnp.einsum('bshd,bthd->bhst', q, k) / np.sqrt(dh).astype(np.float32)
        scores = scores * spiral_weight[None, :, None, None]
        attn = jax.nn.softmax(scores, axis=-1)
        out = jnp.einsum('bhst,bthd->bshd', attn, v).reshape(b, s, d)
        return out @ Wo.T + bo

    def _L0_ffn_ref(x, router_w, router_b, expert_w, expert_b, out_w, out_b):
        import jax, jax.numpy as jnp
        import numpy as np
        B, S, H, E, D, K = (2, 512, 512, 8, 512, 2)
        num_experts = expert_w.shape[0]
        router_logits = jnp.einsum('bsh,he->bse', x, router_w) + router_b
        router_probs = jax.nn.softmax(router_logits, axis=-1)
        top_k_probs, top_k_indices = jax.lax.top_k(router_probs, K)
        top_k_probs = top_k_probs / jnp.sum(top_k_probs, axis=-1, keepdims=True)
        onehot = jax.nn.one_hot(top_k_indices, num_experts, dtype=x.dtype)
        gates = jnp.einsum('bsk,bske->bse', top_k_probs, onehot)
        expert_out = jax.nn.gelu(jnp.einsum('bsh,ehd->ebsd', x, expert_w) + expert_b[:, None, None, :])
        combined = jnp.einsum('bse,ebsd->bsd', gates, expert_out)
        return jnp.einsum('bsd,df->bsf', combined, out_w) + out_b
    h = _L0_tok_ref(x, L0_tok_log_dt, L0_tok_B_ri, L0_tok_inv_A_real, L0_tok_A_imag, 512)
    h = jnp.concatenate([jnp.broadcast_to(cls_tok, (h.shape[0], 1, h.shape[2])), h], axis=1)
    h = h + _L0_attn_ref(_layernorm(h, axis=-1), L0_attn_Wq, L0_attn_bq, L0_attn_Wk, L0_attn_bk, L0_attn_Wv, L0_attn_bv, L0_attn_Wo, L0_attn_bo, L0_attn_spiral_weight, L0_attn_helix_rotation)
    h = h + _L0_ffn_ref(_layernorm(h, axis=-1), L0_ffn_router_w, L0_ffn_router_b, L0_ffn_expert_w, L0_ffn_expert_b, L0_ffn_out_w, L0_ffn_out_b)
    return h

_drawn_inputs = setup_inputs


def setup_inputs(seed=0):
    import zlib

    import numpy as np

    out = dict(_drawn_inputs(seed))
    spreads = {'L0_ffn_router_b': (0.0, 0.1), 'L0_ffn_expert_b': (0.0, 0.1), 'L0_ffn_out_b': (0.0, 0.1)}
    factors = {'cls_tok': 7.841, 'L0_attn_bq': 29.449, 'L0_attn_bk': 64.0, 'L0_attn_Wq': 2.683}
    for name, (base, spread) in spreads.items():
        noise = np.random.default_rng([zlib.crc32(name.encode()), seed]).standard_normal(out[name].shape)
        drawn = base * np.exp(spread * noise) if base else spread * noise
        out[name] = jnp.asarray(drawn.astype(out[name].dtype))
    for name, factor in factors.items():
        out[name] = (out[name] * factor).astype(out[name].dtype)
    return out
```

```python
from contextlib import ExitStack

import concourse.bass as bass
from concourse import mybir

F32 = mybir.dt.float32
F32R = mybir.dt.float32r
ALU = mybir.AluOpType
ACT = mybir.ActivationFunctionType
AX_X = mybir.AxisListType.X

P = 128
BANK = 512
EPS = 1e-5
TWO_PI_HI = 6.28125
TWO_PI_LO = 0.0019353071795864769
PI_SAFE = 3.1415925
ROUND_MAGIC = 12582912.0


def vit_tower_kernel(nc, x, cls_tok, log_dt, B_ri, inv_A_real, A_imag, Wq, bq, Wk, bk, Wv, bv, Wo, bo,
                     spiral, rot, router_w, router_b, expert_w, expert_b, out_w, out_b, out):
    NB, NH_SSM, NS, _ = x.shape
    D = Wq.shape[0]
    NHEAD = spiral.shape[0]
    DH = D // NHEAD
    NE = router_w.shape[1]
    KC = D // P
    HPC = P // DH
    HALVES = NH_SSM // P
    BODY = HALVES * P
    KEYS = BODY + 1
    KPAD = KEYS + 1
    S2 = 2 * NS
    NA = 8
    NBP = D // NA
    NLOW = NBP // 2
    PIECE = 8
    TILES = NB * HALVES
    CLS = TILES
    HB = 16
    NHB = P // 2 // HB
    RESTACK = 16 * 2 * 4 * HPC
    assert S2 == P and NBP * NA == D and NB * NA == 64 and HALVES == 2 and DH == 32

    with ExitStack() as whole:
        def sb(scope, name, shape, dt=F32):
            return scope.enter_context(nc.sbuf_tensor(name, shape, dt))

        def sem(name):
            return whole.enter_context(nc.semaphore(name))

        ps = whole.enter_context(nc.psum_tensor("ps", [P, 8, BANK], F32))

        ident = sb(whole, "ident", [P, P])
        tok = sb(whole, "tok", [P, TILES + 1, D])
        attn = ExitStack()
        wqT_hi = sb(attn, "wqT_hi", [P, KC, D], F32R)
        wqT_lo = sb(attn, "wqT_lo", [P, KC, D], F32R)
        wkT_hi = sb(attn, "wkT_hi", [P, KC, D], F32R)
        wkT_lo = sb(attn, "wkT_lo", [P, KC, D], F32R)
        q_scale = sb(attn, "q_scale", [P, KC])
        k_scale = sb(attn, "k_scale", [P, KC])
        q_bias = sb(attn, "q_bias", [P, KC])
        k_bias = sb(attn, "k_bias", [P, KC])
        bv_col = sb(attn, "bv_col", [P, KC])
        mk = ExitStack()
        ldt = sb(mk, "ldt", [P, HALVES])
        iar = sb(mk, "iar", [P, HALVES, NS])
        aim = sb(mk, "aim", [P, HALVES, NS])
        b_in = sb(mk, "b_in", [P, HALVES, NS, 2])
        x_in = sb(mk, "x_in", [P, NB, NS, 2])
        coef = sb(mk, "coef", [P, NB, 2, NS])
        ctmp = sb(mk, "ctmp", [P, NB, NS])
        g = sb(mk, "g", [P, HALVES, 2, NS])
        prm = sb(mk, "prm", [P, 8, HALVES, NS])
        dt2 = sb(mk, "dt2", [P, 2, HALVES])
        zs = sb(mk, "zs", [P, 9, 2, NS])
        zt = sb(mk, "zt", [P, 9, 2, NS])
        r_low = sb(mk, "r_low", [P, NLOW, 2, NS])
        w_pow = sb(mk, "w_pow", [P, NA, 2, NS])
        w_b = sb(mk, "w_b", [P, NA, 2, NS])
        ring = sb(mk, "ring", [P, 2, 2, PIECE, 2, NS])
        rT = sb(mk, "rT", [P, P, NBP])
        so = sb(mk, "so", [P, 2, HB * NBP])
        rcol = sb(mk, "rcol", [P, 4, KC])
        with ExitStack() as early:
            w_raw = sb(early, "w_raw", [P, 2, KC, D])
        lT = sb(mk, "lT", [P, P, NB * NA])
        mk.close()
        at = attn
        wvT_hi = sb(at, "wvT_hi", [P, KC, D], F32R)
        wvT_lo = sb(at, "wvT_lo", [P, KC, D], F32R)
        woT_hi = sb(at, "woT_hi", [P, KC, D], F32R)
        woT_lo = sb(at, "woT_lo", [P, KC, D], F32R)
        xT_hi = sb(at, "xT_hi", [P, KC, KPAD], F32R)
        xT_lo = sb(at, "xT_lo", [P, KC, KPAD], F32R)
        xhat = sb(at, "xhat", [P, HALVES, D])
        q_hi = sb(at, "q_hi", [P, KC, KPAD], F32R)
        q_lo = sb(at, "q_lo", [P, KC, KPAD], F32R)
        k_hi = sb(at, "k_hi", [P, KC, KPAD], F32R)
        k_lo = sb(at, "k_lo", [P, KC, KPAD], F32R)
        q4 = sb(at, "q4", [P, NHEAD, BODY], F32R)
        k4 = sb(at, "k4", [P, NHEAD, KPAD], F32R)
        v_sb = sb(at, "v_sb", [P, HALVES, D])
        oT_hi = sb(at, "oT_hi", [P, KC, BODY], F32R)
        oT_lo = sb(at, "oT_lo", [P, KC, BODY], F32R)
        u_sb = sb(at, "u_sb", [P, D])
        pclsT = sb(at, "pclsT", [P, BODY])
        pccT = sb(at, "pccT", [P, P])
        pcls = sb(at, "pcls", [P, HALVES, NHEAD])
        pc = sb(at, "pc", [NHEAD, KPAD])
        ptc = sb(at, "ptc", [P, HALVES, NHEAD])
        ocls = sb(at, "ocls", [P, KC, NB])
        negmax = sb(at, "negmax", [P, 4, HALVES])
        rowsum = sb(at, "rowsum", [P, 4, HALVES])
        rrec = sb(at, "rrec", [P, 4, HALVES])
        cstat = sb(at, "cstat", [NHEAD, 4])
        lnst = sb(at, "lnst", [P, HALVES, 6])
        lnmv = sb(at, "lnmv", [P, HALVES, 2])
        lnr = sb(at, "lnr", [P, 2, HALVES])
        mhalf = sb(at, "mhalf", [P, HALVES])
        ones = sb(at, "ones", [P, HALVES, HPC])
        qblk_hi = sb(at, "qblk_hi", [P, KC, P], F32R)
        qblk_lo = sb(at, "qblk_lo", [P, KC, P], F32R)
        late = ExitStack()
        prb = sb(late, "prb", [P, 4, HALVES, KPAD])
        pts = sb(late, "pts", [P, 8, HALVES, KPAD])
        late.close()
        setup = ExitStack()
        w_raw2 = sb(setup, "w_raw2", [P, 2, KC, D])
        mask = sb(setup, "mask", [P, KC, P])
        vblk = sb(setup, "vblk", [P, KC, 32])
        bo_row = sb(setup, "bo_row", [1, D])
        e16 = sb(setup, "e16", [1, 32])
        setup.close()
        oc_hi, oc_lo = qblk_hi, qblk_lo
        attn.close()
        ffn = whole
        ew = sb(ffn, "ew", [P, NE, KC, D])
        ow = sb(ffn, "ow", [P, KC, D])
        rw = sb(ffn, "rw", [P, KC, NE])
        eb = sb(ffn, "eb", [P, NE, D])
        ob = sb(ffn, "ob", [P, D])
        rb = sb(ffn, "rb", [P, NE])
        iota = sb(ffn, "iota", [P, NE])
        xn = sb(ffn, "xn", [P, D])
        xnT = sb(ffn, "xnT", [P, KC, P])
        pre = sb(ffn, "pre", [P, 2, D])
        act_out = sb(ffn, "act_out", [P, 2, D])
        comb = sb(ffn, "comb", [P, D])
        combT = sb(ffn, "combT", [P, KC, P])
        st2 = sb(ffn, "st2", [P, 6])
        mv2 = sb(ffn, "mv2", [P, 2])
        rs2 = sb(ffn, "rs2", [P, 2])
        mh2 = sb(ffn, "mh2", [P, 1])
        lg = sb(ffn, "lg", [P, NE])
        probs = sb(ffn, "probs", [P, NE])
        psum_ = sb(ffn, "psum_", [P, 4])
        top8 = sb(ffn, "top8", [P, 8])
        idx8 = sb(ffn, "idx8", [P, 8], mybir.dt.uint32)
        idxf = sb(ffn, "idxf", [P, 2])
        gates = sb(ffn, "gates", [P, 2, NE])

        s = {}
        for n in ("c_cls ld_par ld_x0 ld_x1 ld_w0 ld_w1 ld_cls ld_rot ld_wv ld_bo c_ident c_ones c_fix c_mask "
                  "a_exp a_sin a_wsc a_whi a_tr a_so a_expc a_v a_hiT a_hiqk a_exps a_pt a_ot a_wvhi a_fin "
                  "d_par d_coef d_pow d_rl d_up d_lp d_wlo d_so d_rot d_ln d_x d_loT d_loqk d_max d_rc d_norm "
                  "d_scm d_scn d_ptc d_tck d_ot d_res d_qb d_wvlo d_vb d_u d_fin "
                  "p_coef p_pow p_pc p_ptc p_mask "
                  "t_w t_tr t_mm t_x t_qk t_v t_sc t_tc t_op t_s t_tp t_tck t_pv t_wv t_vb t_u t_fin "
                  "m_tok m_out "
                  "f_ld f_const f_d f_pow f_dx f_tx f_ax f_tr f_dl f_ae f_te f_dp f_ag f_dg f_tc f_ac f_to f_do").split():
            s[n] = sem(n)
        s_rq = [sem(f"m_restack{i}") for i in range(KC // 2)]

        s_row = [sem(f"m_row{i}") for i in range(2)]
        tok_dram = nc.dram_tensor("tok_dram", [HALVES, P, 64, NBP], F32).ap()

        block = whole.enter_context(nc.Block())
        bc = lambda ap, shape: ap.broadcast_to(shape)

        @block.sync
        def _(sp):
            whole.enter_context(nc.allow_non_contiguous_dma(reason="a few hundred words of parameters"))
            sp.dma_start(ldt[:, :], log_dt.rearrange("(f p) -> p f", p=P)).then_inc(s["ld_par"], 16)
            sp.dma_start(iar[:, :, :], inv_A_real.rearrange("(f p) n -> p f n", p=P)).then_inc(s["ld_par"], 16)
            sp.dma_start(aim[:, :, :], A_imag.rearrange("(f p) n -> p f n", p=P)).then_inc(s["ld_par"], 16)
            sp.dma_start(b_in[:, :, :, :], B_ri.rearrange("(f p) n r -> p f n r", p=P)).then_inc(s["ld_par"], 16)
            sp.dma_start(x_in[:, :, :, :], x[:, 0:P].rearrange("c p n r -> p c n r")).then_inc(s["ld_x0"], 16)
            sp.dma_start(rcol[:, 0, :], rot.rearrange("(k p) -> p k", p=P)).then_inc(s["ld_rot"], 16)
            for j in range(HPC):
                sp.dma_start(rcol[j * DH:(j + 1) * DH, 1, :],
                             spiral.rearrange("(k j) -> j k", j=HPC)[j:j + 1, :].broadcast_to([DH, KC])
                             ).then_inc(s["ld_rot"], 16)
            sp.dma_start(q_bias[:, :], bq.rearrange("(k p) -> p k", p=P)).then_inc(s["ld_rot"], 16)
            sp.dma_start(k_bias[:, :], bk.rearrange("(k p) -> p k", p=P)).then_inc(s["ld_rot"], 16)
            sp.dma_start(w_raw[:, 0, :, :], Wq.rearrange("(o p) i -> p o i", p=P)).then_inc(s["ld_w0"], 16)
            sp.dma_start(w_raw[:, 1, :, :], Wk.rearrange("(o p) i -> p o i", p=P)).then_inc(s["ld_w1"], 16)
            sp.dma_start(bv_col[:, :], bv.rearrange("(k p) -> p k", p=P)).then_inc(s["ld_rot"], 16)
            sp.wait_ge(s["c_cls"], 1)
            sp.dma_start(tok[0:NB, CLS, :], cls_tok[0, :, :].broadcast_to([NB, D])).then_inc(s["ld_cls"], 16)
            sp.wait_ge(s["p_coef"], 1)
            sp.dma_start(x_in[:, :, :, :], x[:, P:2 * P].rearrange("c p n r -> p c n r")).then_inc(s["ld_x1"], 16)
            for hf in range(HALVES):
                for hb in range(NHB):
                    n = hf * NHB + hb
                    sp.wait_ge(s["a_so"], n + 1)
                    sp.dma_start(tok_dram[hf, :, hb * HB:(hb + 1) * HB, :],
                                 so[:, n % 2, :].rearrange("r (h b) -> r h b", h=HB)).then_inc(s_row[n % 2], 16)
                for row in s_row:
                    sp.wait_ge(row, 16 * NHB // 2 * (hf + 1))
                for hp in range(2):
                    for c in range(NB):
                        r0 = hp * 64 + c * NA
                        sp.dma_start(
                            tok[hp * 64:hp * 64 + 64, c * HALVES + hf, :].rearrange("h (a b) -> h a b", a=NA),
                            tok_dram[hf, r0:r0 + NA, :, :].rearrange("a h b -> h a b")).then_inc(s["m_tok"], 16)
            sp.wait_ge(s["t_mm"], HALVES * NHB)
            sp.wait_ge(s["m_tok"], 16 * 2 * NB * HALVES)
            sp.dma_start(w_raw2[:, 0, :, :], Wv.rearrange("(o p) i -> p o i", p=P)).then_inc(s["ld_wv"], 16)
            sp.dma_start(w_raw2[:, 1, :, :], Wo.rearrange("(o p) i -> p o i", p=P)).then_inc(s["ld_wv"], 16)
            sp.dma_start(bo_row[:, :], bo.rearrange("(a d) -> a d", a=1)).then_inc(s["ld_bo"], 16)

            def restack(c, first):
                for pair in range(KC // 2):
                    k0 = 2 * pair
                    sp.wait_ge(s["d_loqk"], c * 2 * KC + 4 * pair + 4)
                    for src2, dst, n in (((q_hi, q_lo, q_hi, q_lo), q4, BODY), ((k_hi, k_hi, k_lo, k_lo), k4, KPAD)):
                        for r, src in enumerate(src2):
                            for j in range(HPC):
                                sp.dma_start(
                                    dst[r * DH:(r + 1) * DH, k0 * HPC + j:(k0 + 2) * HPC:HPC, 0:n].bitcast(F32),
                                    src[j * DH:(j + 1) * DH, k0:k0 + 2, 0:n].bitcast(F32)).then_inc(s_rq[pair], 16)

            restack(0, True)
            with sp.Fori(1, NB) as c:
                restack(c, False)
            sp.wait_ge(s["d_fin"], 1)
            sp.dma_start(ew[:, :, :, :], expert_w.rearrange("e (k p) d -> p e k d", p=P)).then_inc(s["f_ld"], 16)
            sp.dma_start(ow[:, :, :], out_w.rearrange("(k p) d -> p k d", p=P)).then_inc(s["f_ld"], 16)
            sp.dma_start(rw[:, :, :], router_w.rearrange("(k p) e -> p k e", p=P)).then_inc(s["f_ld"], 16)
            sp.dma_start(eb[:, :, :], expert_b.rearrange("e d -> (e d)").rearrange("(a n) -> a n", a=1).broadcast_to([P, NE * D]).rearrange("p (e d) -> p e d", e=NE)).then_inc(s["f_ld"], 16)
            sp.dma_start(ob[:, :], out_b.rearrange("(a n) -> a n", a=1).broadcast_to([P, D])).then_inc(s["f_ld"], 16)
            sp.dma_start(rb[:, :], router_b.rearrange("(a n) -> a n", a=1).broadcast_to([P, NE])).then_inc(s["f_ld"], 16)
            for t in range(TILES + 1):
                sp.wait_ge(s["f_do"], t + 1)
                if t < TILES:
                    st = t % 2
                    sp.dma_start(out[t // 2, 1 + st * P:1 + st * P + P, :], tok[:, t, :]).then_inc(s["m_out"], 16)
                else:
                    sp.dma_start(out[:, 0, :], tok[0:NB, CLS, :]).then_inc(s["m_out"], 16)
            sp.wait_ge(s["m_out"], (TILES + 1) * 16)

        @block.gpsimd
        def _(pool):
            pool.memset(tok[:, CLS, :], 0.0).then_inc(s["c_cls"], 1)
            nc.gpsimd.memset(ident[:, :], 0.0).then_inc(s["c_ident"], 1)
            pool.wait_ge(s["c_ident"], 1)
            nc.gpsimd.affine_select(out=ident[:, :], in_=ident[:, :], compare_op=ALU.not_equal, fill=1.0, base=0,
                                    pattern=[[-1, P]], channel_multiplier=1).then_inc(s["c_ident"], 1)
            for hf in range(HALVES):
                pool.wait_ge(s["ld_x0" if hf == 0 else "ld_x1"], 16)
                if hf == 0:
                    pool.wait_ge(s["d_coef"], 1)
                else:
                    pool.wait_ge(s["d_lp"], NB)
                xr, xi = x_in[:, :, :, 0], x_in[:, :, :, 1]
                gr = bc(g[:, hf, 0, :].unsqueeze(1), [P, NB, NS])
                gi = bc(g[:, hf, 1, :].unsqueeze(1), [P, NB, NS])
                base = 6 * hf
                cr, cim = coef[:, :, 0, :], coef[:, :, 1, :]
                pool.tensor_tensor(ctmp[:, :, :], xi, gi, ALU.mult).then_inc(s["p_pow"], 1)
                pool.tensor_tensor(cr, xr, gr, ALU.mult).then_inc(s["p_pow"], 1)
                pool.wait_ge(s["p_pow"], base + 2)
                pool.tensor_tensor(cr, cr, ctmp[:, :, :], ALU.subtract).then_inc(s["p_pow"], 1)
                pool.wait_ge(s["p_pow"], base + 3)
                pool.tensor_tensor(ctmp[:, :, :], xi, gr, ALU.mult).then_inc(s["p_pow"], 1)
                pool.tensor_tensor(cim, xr, gi, ALU.mult).then_inc(s["p_pow"], 1)
                pool.wait_ge(s["p_pow"], base + 5)
                pool.tensor_tensor(cim, cim, ctmp[:, :, :], ALU.add).then_inc(s["p_pow"], 1)
                pool.wait_ge(s["p_pow"], base + 6)
                pool.tensor_copy(ctmp[:, 0, 0:1], ident[:, 0:1]).then_inc(s["p_coef"], 1)

            pool.wait_ge(s["t_mm"], HALVES * NHB)
            pool.wait_ge(s["m_tok"], 16 * 2 * NB * HALVES)
            pool.memset(mhalf[:, :], -0.5).then_inc(s["c_ones"], 1)
            pool.memset(ones[:, :, :], 1.0).then_inc(s["c_fix"], 1)
            pool.memset(mask[:, :, :], 1.0).then_inc(s["c_fix"], 1)
            pool.memset(pclsT[:, :], 0.0).then_inc(s["c_fix"], 1)
            pool.memset(pccT[:, :], 0.0).then_inc(s["c_fix"], 1)
            pool.memset(e16[:, :], 0.0).then_inc(s["c_fix"], 1)
            pool.memset(u_sb[:, :], 0.0).then_inc(s["c_fix"], 1)
            pool.wait_ge(s["c_fix"], 6)
            pool.affine_select(out=mask[:, :, :], in_=mask[:, :, :], compare_op=ALU.is_ge, fill=0.0, base=0,
                               pattern=[[P, KC], [-DH, P]], channel_multiplier=1).then_inc(s["p_mask"], 1)
            for t, n in ((pclsT, BODY), (pccT, P)):
                pool.affine_select(out=t[:, :], in_=t[:, :], compare_op=ALU.not_equal, fill=1.0, base=-NHEAD,
                                   pattern=[[0, n]], channel_multiplier=1).then_inc(s["c_ones"], 1)
            pool.memset(e16[:, NHEAD:NHEAD + 1], 1.0).then_inc(s["c_ones"], 1)
            pool.wait_ge(s["p_mask"], 1)
            pool.affine_select(out=mask[:, :, :], in_=mask[:, :, :], compare_op=ALU.is_ge, fill=0.0, base=DH - 1,
                               pattern=[[-P, KC], [DH, P]], channel_multiplier=-1).then_inc(s["c_mask"], 1)

            def ln_pow(n):
                pool.wait_ge(s["d_ln"], n * 5 + 5)
                pool.tensor_tensor(lnr[:, 1, :], lnr[:, 0, :], mhalf[:, :], ALU.pow).then_inc(s["p_pow"], 1)

            ln_pow(0)
            ln_pow(1)

            def keep_cls(c, j):
                pool.wait_ge(s["d_norm"], c * NHEAD + j + 1)
                column = prb[:, j % 4, :, BODY]
                pool.tensor_tensor(pcls[:, :, j], column, ones[:, :, 0], ALU.mult).then_inc(s["p_pc"], 1)

            def cls_cols(c, gr):
                if gr == 0:
                    pool.wait_ge(s["d_ptc"], c + 1)
                column = ptc[:, :, gr * HPC:(gr + 1) * HPC].rearrange("p t h -> p h t")
                pool.tensor_tensor(pts[:, (gr * HPC) % 8:(gr * HPC) % 8 + HPC, :, BODY], column, ones[:, :, :].rearrange("p t h -> p h t"), ALU.mult
                                   ).then_inc(s["p_ptc"], 1)

            def body(c, first, last):
                for j in range(NHEAD):
                    if j == 1:
                        if not first:
                            pool.wait_ge(s["t_tck"], c)
                    if j >= 1:
                        keep_cls(c, j - 1)
                    if j == 4:
                        if not first:
                            pool.wait_ge(s["t_pv"], c * KC)
                        cls_cols(c, 0)
                        cls_cols(c, 1)
                        if not last:
                            ln_pow(c + 2)
                    if j == 11:
                        pool.wait_ge(s["t_pv"], c * KC + 1)
                        cls_cols(c, 2)
                    if j == 15:
                        pool.wait_ge(s["t_pv"], c * KC + 2)
                        cls_cols(c, 3)
                keep_cls(c, NHEAD - 1)

            body(0, True, False)
            with pool.Fori(1, NB - 1) as c:
                body(c, False, False)
            body(NB - 1, False, True)
            pool.wait_ge(s["d_fin"], 1)
            pool.memset(mh2[:, :], -0.5).then_inc(s["f_const"], 1)
            pool.iota(iota[:, :], pattern=[[1, NE]], base=0, channel_multiplier=0,
                      allow_small_or_imprecise_dtypes=True).then_inc(s["f_const"], 1)
            pool.wait_ge(s["f_const"], 2)
            with pool.Fori(0, TILES + 1) as t:
                pool.wait_ge(s["f_d"], t * 3 + 3)
                pool.tensor_tensor(rs2[:, 1:2], rs2[:, 0:1], mh2[:, :], ALU.pow).then_inc(s["f_pow"], 1)

        @block.scalar
        def _(act):
            act.wait_ge(s["ld_par"], 64)
            act.activation(prm[:, 0, :, :], iar[:, :, :], ACT.Exp).then_inc(s["a_exp"], 1)
            act.activation(dt2[:, 0, :], ldt[:, :], ACT.Exp).then_inc(s["a_exp"], 1)
            act.wait_ge(s["d_rot"], 2)
            act.activation(k_scale[:, :], rcol[:, 2, :], ACT.Sin).then_inc(s["a_sin"], 1)
            act.activation(rcol[:, 0, :], rcol[:, 3, :], ACT.Sin).then_inc(s["a_sin"], 1)

            def w_scale(raw, scale):
                for o in range(KC):
                    act.activation(raw[:, o, :], raw[:, o, :], ACT.Copy, scale=scale[:, o:o + 1]
                                   ).then_inc(s["a_wsc"], 1)

            def w_hi(dst, sem_hi, sem_t, n, bank0):
                for ic in range(KC):
                    act.wait_ge(s[sem_t], n * KC + ic + 1)
                    act.activation(dst[:, ic, :], ps[:, bank0 + ic, :], ACT.Copy).then_inc(s[sem_hi], 1)

            act.wait_ge(s["ld_w0"], 16)
            act.wait_ge(s["d_rot"], 5)
            w_scale(w_raw[:, 0], q_scale)
            w_hi(wqT_hi, "a_whi", "t_w", 0, 4)
            act.wait_ge(s["ld_w1"], 16)
            w_scale(w_raw[:, 1], k_scale)
            w_hi(wkT_hi, "a_whi", "t_w", 1, 4)

            def turned(n, dst, col):
                act.wait_ge(s["t_tr"], n + 1)
                act.activation(dst[:, :, col:col + 4], ps[:, n % 4, :].rearrange("p (q h) -> p h q", q=4),
                               ACT.Copy).then_inc(s["a_tr"], 1)

            for hf in range(HALVES):
                base = hf * 32
                if hf == 1:
                    act.wait_ge(s["t_mm"], NHB)
                for q in range(16):
                    turned(base + q, rT, 4 * q)
                for c in range(NB):
                    for k in range(2):
                        turned(base + 16 + 2 * c + k, lT, c * NA + 4 * k)
                for hb in range(NHB):
                    n = hf * NHB + hb
                    act.wait_ge(s["t_mm"], n + 1)
                    if n >= 2:
                        act.wait_ge(s_row[n % 2], 16 * (n // 2))
                    for k in range(2):
                        e = act.activation(so[:, n % 2, k * BANK:(k + 1) * BANK], ps[:, 4 + 2 * (n % 2) + k, :], ACT.Copy)
                    e.then_inc(s["a_so"], 1)

            def hi_xT(n, bank, st):
                act.wait_ge(s["t_x"], n + 1)
                act.activation(xT_hi[:, :, st * P:st * P + P], ps[:, bank, :].rearrange("p (k t) -> p k t", k=KC),
                               ACT.Copy).then_inc(s["a_hiT"], 1)

            act.wait_ge(s["t_x"], 1)
            act.activation(xT_hi[:, :, BODY:KPAD], ps[:, 7, 0:KC * NB].rearrange("p (k t) -> p k t", k=KC)[:, :, 0:2],
                           ACT.Copy).then_inc(s["a_hiT"], 1)
            hi_xT(1, 6, 0)
            hi_xT(2, 7, 1)

            def hi_qk(c, m):
                dst, bias = (q_hi, q_bias) if m % 2 == 0 else (k_hi, k_bias)
                act.wait_ge(s["t_qk"], c * 2 * KC + m + 1)
                act.activation(dst[:, m // 2, :], ps[:, 6 + m % 2, 0:KPAD], ACT.Identity,
                               bias=bias[:, m // 2:m // 2 + 1]).then_inc(s["a_hiqk"], 1)

            for m in range(2 * KC):
                hi_qk(0, m)
            for i, dst in enumerate((wvT_hi, woT_hi)):
                w_hi(dst, "a_wvhi", "t_wv", i, 0)

            def exp_unit(c, j):
                act.wait_ge(s["d_max"], c * NHEAD + j + 1)
                for st in range(HALVES):
                    e = act.activation(prb[:, j % 4, st, 0:KEYS], ps[:, 2 * (j % 2) + st, 0:KEYS], ACT.Exp,
                                       bias=negmax[:, j % 4, st:st + 1], accum_out=rowsum[:, j % 4, st:st + 1])
                e.then_inc(s["a_exps"], 1)

            def keep_pt(c, j):
                act.wait_ge(s["t_tp"], c * NHEAD + j + 1)
                act.activation(pts[:, j % 8, :, 0:BODY], ps[:, 4, :].rearrange("p (t s) -> p t s", t=2),
                               ACT.Copy).then_inc(s["a_pt"], 1)

            def keep_v(c, st):
                act.wait_ge(s["t_v"], c * HALVES + st + 1)
                act.activation(v_sb[:, st, :], ps[:, 7, :], ACT.Copy).then_inc(s["a_v"], 1)

            def hi_ot(c, gr):
                act.wait_ge(s["t_pv"], c * KC + gr + 1)
                act.activation(oT_hi[:, gr, :], ps[:, 5, 0:BODY], ACT.Copy).then_inc(s["a_ot"], 1)

            def body(c, first, last):
                for j in range(NHEAD):
                    if j >= 4 or not first:
                        act.wait_ge(s["t_tp"], c * NHEAD + j - 3)
                        act.wait_ge(s["p_pc"], c * NHEAD + j - 3)
                    exp_unit(c, j)
                    if j >= 2:
                        if j == 2 and not first:
                            act.wait_ge(s["t_pv"], c * KC - 1)
                        if j == 10:
                            act.wait_ge(s["t_pv"], c * KC + 1)
                        if j == 14:
                            act.wait_ge(s["t_pv"], c * KC + 2)
                        keep_pt(c, j - 2)
                    elif not first:
                        keep_pt(c - 1, NHEAD - 2 + j)
                    if j == 0:
                        act.wait_ge(s["d_scm"], c + 1)
                        act.activation(pc[:, 0:KEYS], ps[0:NHEAD, 6, 0:KEYS], ACT.Exp, bias=cstat[:, 0:1],
                                       accum_out=cstat[:, 1:2]).then_inc(s["a_expc"], 1)
                    if j == 2:
                        if not first:
                            act.wait_ge(s["t_pv"], c * KC)
                        keep_v(c, 0)
                    if j == 3:
                        if not first:
                            hi_ot(c - 1, 3)
                        keep_v(c, 1)
                    if j == 7 and not last:
                        act.wait_ge(s["t_v"], (c + 1) * HALVES)
                        hi_xT((c + 1) * HALVES + 1, 6, 0)
                        hi_xT((c + 1) * HALVES + 2, 7, 1)
                    if j in (7, 11, 15):
                        if j == 7 and not first:
                            act.wait_ge(s["t_op"], c * HALVES)
                        hi_ot(c, (j - 7) // 4)
                    if j >= 8 and not last:
                        m = j - 8
                        if m % 4 == 0:
                            act.wait_ge(s_rq[m // 4], RESTACK * (c + 1))
                        if m == 0:
                            act.wait_ge(s["t_sc"], c + 1)
                        hi_qk(c + 1, m)

            body(0, True, False)
            with act.Fori(1, NB - 1) as c:
                body(c, False, False)
            body(NB - 1, False, True)
            last = NB - 1
            keep_pt(last, NHEAD - 2)
            keep_pt(last, NHEAD - 1)
            hi_ot(last, 3)
            act.wait_ge(s["d_fin"], 1)
            with act.Fori(0, TILES + 1) as t:
                act.wait_ge(s["f_tx"], t + 1)
                act.activation(xnT[:, :, :], ps[:, 0, :].rearrange("p (k t) -> p k t", k=KC), ACT.Copy).then_inc(s["f_ax"], 1)
                act.wait_ge(s["f_dl"], t * 8 + 2)
                act.activation(probs[:, :], lg[:, :], ACT.Exp, bias=psum_[:, 0:1], accum_out=psum_[:, 1:2]).then_inc(s["f_ae"], 1)
                for e in range(NE):
                    act.wait_ge(s["f_dp"], t * NE + e + 1)
                    act.wait_ge(s["f_dl"], t * 8 + 8)
                    act.activation(act_out[:, e % 2, :], pre[:, e % 2, :], ACT.Gelu_apprx_tanh).then_inc(s["f_ag"], 1)
                act.wait_ge(s["f_tc"], t + 1)
                act.activation(combT[:, :, :], ps[:, 4, :].rearrange("p (k t) -> p k t", k=KC), ACT.Copy).then_inc(s["f_ac"], 1)

        @block.vector
        def _(dve):
            n_par = [0]

            def link(ins):
                n_par[0] += 1
                ins.then_inc(s["d_par"], 1)
                dve.wait_ge(s["d_par"], n_par[0])

            dve.wait_ge(s["ld_rot"], 16 * (4 + HPC))
            for i, (dst, shift) in enumerate(((2, 0.0), (3, 0.25))):
                t = prm[:, 7, 0, i * 16:i * 16 + KC]
                link(dve.tensor_scalar(t, rcol[:, 0, :], 1.0 / (TWO_PI_HI + TWO_PI_LO), shift, ALU.mult, ALU.add))
                link(dve.tensor_scalar(t, t, ROUND_MAGIC, ROUND_MAGIC, ALU.add, ALU.subtract))
                link(dve.scalar_tensor_tensor(out=rcol[:, dst, :], in0=t, scalar=-TWO_PI_HI, in1=rcol[:, 0, :],
                                              op0=ALU.mult, op1=ALU.add))
                link(dve.scalar_tensor_tensor(out=rcol[:, dst, :], in0=t, scalar=-TWO_PI_LO, in1=rcol[:, dst, :],
                                              op0=ALU.mult, op1=ALU.add))
                link(dve.tensor_scalar(rcol[:, dst, :], rcol[:, dst, :], 4 * shift * 1.5707963267948966, None, ALU.add))
                dve.tensor_scalar(rcol[:, dst, :], rcol[:, dst, :], PI_SAFE, -PI_SAFE, ALU.min, ALU.max
                                  ).then_inc(s["d_rot"], 1)
            dve.wait_ge(s["a_sin"], 2)
            link(dve.scalar_tensor_tensor(out=q_scale[:, :], in0=rcol[:, 0, :], scalar=float(DH) ** -0.5,
                                          in1=rcol[:, 1, :], op0=ALU.mult, op1=ALU.mult))
            dve.tensor_tensor(q_bias[:, :], q_bias[:, :], q_scale[:, :], ALU.mult).then_inc(s["d_rot"], 1)
            dve.tensor_tensor(k_bias[:, :], k_bias[:, :], k_scale[:, :], ALU.mult).then_inc(s["d_rot"], 1)
            dve.memset(prm[:, 7, 1, 0:1], 0.0).then_inc(s["d_rot"], 1)

            dve.wait_ge(s["a_exp"], 2)
            link(dve.tensor_scalar(dt2[:, 1, :], dt2[:, 0, :], 0.5, None, ALU.mult))
            e_, q1, v_, inv, t0, t1, om = (prm[:, i, :, :] for i in range(7))
            for hf in range(HALVES):
                dve.tensor_scalar(e_[:, hf, :], e_[:, hf, :], dt2[:, 1, hf:hf + 1], None, ALU.mult).then_inc(s["d_par"], 1)
                dve.tensor_scalar(v_[:, hf, :], aim[:, hf, :], dt2[:, 1, hf:hf + 1], None, ALU.mult).then_inc(s["d_par"], 1)
            n_par[0] += 4
            dve.wait_ge(s["d_par"], n_par[0])
            link(dve.tensor_scalar(q1, e_, 1.0, None, ALU.add))
            link(dve.tensor_scalar(om, e_, -1.0, 1.0, ALU.mult, ALU.add))
            link(dve.tensor_tensor(t0, v_, v_, ALU.mult))
            link(dve.tensor_tensor(t1, q1, q1, ALU.mult))
            link(dve.tensor_tensor(t1, t1, t0, ALU.add))
            link(dve.reciprocal(inv, t1))
            link(dve.tensor_tensor(t1, om, q1, ALU.mult))
            link(dve.tensor_tensor(t1, t1, t0, ALU.subtract))
            link(dve.tensor_tensor(e_, t1, inv, ALU.mult))
            link(dve.scalar_tensor_tensor(out=om, in0=v_, scalar=2.0, in1=inv, op0=ALU.mult, op1=ALU.mult))
            br, bi = b_in[:, :, :, 0], b_in[:, :, :, 1]
            for hf in range(HALVES):
                link(dve.tensor_scalar(inv[:, hf, :], inv[:, hf, :], dt2[:, 0, hf:hf + 1], 2.0, ALU.mult, ALU.mult))
            link(dve.tensor_tensor(t0, br, q1, ALU.mult))
            link(dve.tensor_tensor(t1, bi, v_, ALU.mult))
            link(dve.tensor_tensor(t0, t0, t1, ALU.subtract))
            link(dve.tensor_tensor(g[:, :, 0, :], t0, inv, ALU.mult))
            link(dve.tensor_tensor(t0, br, v_, ALU.mult))
            link(dve.tensor_tensor(t1, bi, q1, ALU.mult))
            link(dve.tensor_tensor(t0, t0, t1, ALU.add))
            dve.tensor_tensor(g[:, :, 1, :], t0, inv, ALU.mult).then_inc(s["d_coef"], 1)

            def w_lo(dst, hi, sem_hi, sem_lo, n, bank0):
                for ic in range(KC):
                    dve.wait_ge(s[sem_hi], n * KC + ic + 1)
                    dve.tensor_tensor(dst[:, ic, :], ps[:, bank0 + ic, :], hi[:, ic, :].bitcast(F32), ALU.subtract
                                      ).then_inc(s[sem_lo], 1)

            n_pow = [0]

            def step(ins):
                n_pow[0] += 1
                ins.then_inc(s["d_pow"], 1)
                dve.wait_ge(s["d_pow"], n_pow[0])

            for hf in range(HALVES):
                step(dve.tensor_copy(zs[:, 0, 0, :], e_[:, hf, :]))
                step(dve.tensor_copy(zs[:, 0, 1, :], om[:, hf, :]))
                for k in range(9):
                    zr, zi = zs[:, k, 0, :], zs[:, k, 1, :]
                    if k < 8:
                        step(dve.tensor_tensor(t0[:, 0, :], zr, zr, ALU.mult))
                        step(dve.tensor_tensor(t1[:, 0, :], zi, zi, ALU.mult))
                        step(dve.scalar_tensor_tensor(out=zs[:, k + 1, 1, :], in0=zr, scalar=2.0, in1=zi,
                                                      op0=ALU.mult, op1=ALU.mult))
                        step(dve.tensor_tensor(zs[:, k + 1, 0, :], t0[:, 0, :], t1[:, 0, :], ALU.subtract))
                    step(dve.tensor_scalar(zt[:, k, 0, :], zi, -1.0, None, ALU.mult))
                    step(dve.tensor_copy(zt[:, k, 1, :], zr))
                if hf == 0:
                    w_lo(wqT_lo, wqT_hi, "a_whi", "d_wlo", 0, 4)
                else:
                    dve.wait_ge(s["t_tr"], 32)

                def doubled(dst, n, k, tmp):
                    shape = [P, n, 2, NS]
                    step(dve.tensor_tensor(dst[:, n:2 * n], bc(dst[:, 0:n, 0:1, :], shape),
                                           bc(zs[:, k, :, :].unsqueeze(1), shape), ALU.mult))
                    step(dve.tensor_tensor(tmp, bc(dst[:, 0:n, 1:2, :], shape),
                                           bc(zt[:, k, :, :].unsqueeze(1), shape), ALU.mult))
                    step(dve.tensor_tensor(dst[:, n:2 * n], dst[:, n:2 * n], tmp, ALU.add))

                ring_flat = ring[:, 0, :, :, :, :].rearrange("p a b s n -> p (a b) s n")
                for dst, k0, levels in ((r_low, 0, 5), (w_pow, 6, 3)):
                    step(dve.memset(dst[:, 0, 0, :], 1.0))
                    step(dve.memset(dst[:, 0, 1, :], 0.0))
                    step(dve.tensor_copy(dst[:, 1, :, :], zs[:, k0, :, :]))
                    for lv in range(1, levels):
                        doubled(dst, 1 << lv, k0 + lv, ring_flat[:, 0:1 << lv])
                    if dst is r_low:
                        dve.memset(t0[:, 0, 0:1], 0.0).then_inc(s["d_rl"], 1)
                step(dve.tensor_scalar(w_b[:, :, 0, :], w_pow[:, :, 1, :], -1.0, None, ALU.mult))
                step(dve.tensor_scalar(w_b[:, :, 1, :], w_pow[:, :, 0, :], -1.0, None, ALU.mult))
                step(dve.tensor_scalar(w_pow[:, :, 1, :], w_pow[:, :, 1, :], -1.0, None, ALU.mult))
                shape = [P, PIECE, 2, NS]
                for q in range(4):
                    n = hf * 12 + q
                    if q >= 2:
                        dve.wait_ge(s["t_tr"], hf * 32 + 8 + 2 * (q - 1))
                    dve.tensor_tensor(ring[:, n % 2, 0], bc(r_low[:, 8 * q:8 * q + 8, 0:1, :], shape),
                                      bc(zs[:, 5, :, :].unsqueeze(1), shape), ALU.mult)
                    dve.tensor_tensor(ring[:, n % 2, 1], bc(r_low[:, 8 * q:8 * q + 8, 1:2, :], shape),
                                      bc(zt[:, 5, :, :].unsqueeze(1), shape), ALU.mult).then_inc(s["d_up"], 1)
                dve.wait_ge(s["p_coef"], hf + 1)
                for c in range(NB):
                    n = hf * 12 + 4 + c
                    dve.wait_ge(s["t_tr"], hf * 32 + 8 + 2 * (4 + c - 1))
                    dve.tensor_tensor(ring[:, n % 2, 0], bc(coef[:, c, 0:1, :].unsqueeze(1), shape), w_pow[:, :, :, :],
                                      ALU.mult)
                    dve.tensor_tensor(ring[:, n % 2, 1], bc(coef[:, c, 1:2, :].unsqueeze(1), shape), w_b[:, :, :, :],
                                      ALU.mult).then_inc(s["d_lp"], 1)
                if hf == 0:
                    w_lo(wkT_lo, wkT_hi, "a_whi", "d_wlo", 1, 4)
            dve.wait_ge(s["m_tok"], 16 * 2 * NB * HALVES)
            dve.wait_ge(s["t_mm"], HALVES * NHB)

            def ln(n, tiles, rows):
                for i, t in enumerate(tiles):
                    dve.bn_stats(lnst[0:rows, i, :], tok[0:rows, t, :]).then_inc(s["d_ln"], 1)
                for i in range(2):
                    dve.wait_ge(s["d_ln"], n * 5 + 2)
                    dve.bn_aggr(lnmv[0:rows, i, :], lnst[0:rows, i, :]).then_inc(s["d_ln"], 1)
                dve.wait_ge(s["d_ln"], n * 5 + 4)
                dve.tensor_scalar(lnr[0:rows, 0, :], lnmv[0:rows, :, 1], EPS, None, ALU.add).then_inc(s["d_ln"], 1)

            def ln_apply(n, tiles, rows):
                dve.wait_ge(s["p_pow"], 12 + n + 1)
                for i, t in enumerate(tiles):
                    dve.tensor_scalar(xhat[0:rows, i, :], tok[0:rows, t, :], lnmv[0:rows, i, 0:1],
                                      lnr[0:rows, 1, i:i + 1], ALU.subtract, ALU.mult).then_inc(s["d_x"], 1)

            dve.wait_ge(s["ld_cls"], 16)
            dve.memset(lnr[:, 0, :], 1.0).then_inc(s["d_qb"], 1)
            dve.wait_ge(s["d_qb"], 1)
            ln(0, (CLS, CLS), NB)
            ln_apply(0, (CLS, CLS), NB)
            dve.wait_ge(s["t_x"], 1)
            ln(1, (0, 1), P)
            ln_apply(1, (0, 1), P)

            def lo_xT(n, bank, st):
                dve.wait_ge(s["a_hiT"], n + 1)
                dve.tensor_tensor(xT_lo[:, :, st * P:st * P + P], ps[:, bank, :].rearrange("p (k t) -> p k t", k=KC),
                                  xT_hi[:, :, st * P:st * P + P].bitcast(F32), ALU.subtract).then_inc(s["d_loT"], 1)

            dve.wait_ge(s["a_hiT"], 1)
            dve.tensor_tensor(xT_lo[:, :, BODY:KPAD],
                              ps[:, 7, 0:KC * NB].rearrange("p (k t) -> p k t", k=KC)[:, :, 0:2],
                              xT_hi[:, :, BODY:KPAD].bitcast(F32), ALU.subtract).then_inc(s["d_loT"], 1)
            lo_xT(1, 6, 0)
            lo_xT(2, 7, 1)

            def lo_qk(c, m):
                dst, hi, bias = (q_lo, q_hi, q_bias) if m % 2 == 0 else (k_lo, k_hi, k_bias)
                dve.wait_ge(s["a_hiqk"], c * 2 * KC + m + 1)
                dve.scalar_tensor_tensor(out=dst[:, m // 2, :], in0=ps[:, 6 + m % 2, 0:KPAD],
                                         scalar=bias[:, m // 2:m // 2 + 1], in1=hi[:, m // 2, :].bitcast(F32),
                                         op0=ALU.add, op1=ALU.subtract).then_inc(s["d_loqk"], 1)

            for m in range(2 * KC):
                lo_qk(0, m)
            dve.wait_ge(s["c_mask"], 1)
            dve.wait_ge(s["d_loqk"], 2 * KC)
            for ci in range(KC):
                dve.tensor_scalar(qblk_hi[:, ci, :], mask[:, ci, :], q_hi[:, ci, BODY:BODY + 1].bitcast(F32), None,
                                  ALU.mult).then_inc(s["d_qb"], 1)
                dve.tensor_scalar(qblk_lo[:, ci, :], mask[:, ci, :], q_lo[:, ci, BODY:BODY + 1].bitcast(F32), None,
                                  ALU.mult).then_inc(s["d_qb"], 1)
            for i, (dst, hi) in enumerate(((wvT_lo, wvT_hi), (woT_lo, woT_hi))):
                w_lo(dst, hi, "a_wvhi", "d_wvlo", i, 0)
            dve.wait_ge(s["t_vb"], 1)
            for ci in range(KC):
                dve.tensor_scalar(vblk[:, ci, :], mask[:, ci, 0:32], ps[:, 4, 2 * ci:2 * ci + 1], None, ALU.mult
                                  ).then_inc(s["d_vb"], 1)
            dve.wait_ge(s["d_vb"], KC)
            dve.tensor_copy(vblk[:, :, NHEAD:NHEAD + 1], bv_col[:, :].unsqueeze(2)).then_inc(s["d_vb"], 1)
            dve.wait_ge(s["t_u"], 1)
            dve.wait_ge(s["c_fix"], 6)
            dve.tensor_copy(u_sb[0:32, :], ps[0:32, 5, :]).then_inc(s["d_u"], 1)
            dve.wait_ge(s["c_ones"], 4)

            def top(c, j):
                dve.wait_ge(s["t_s"], c * NHEAD + j + 1)
                dve.tensor_reduce(negmax[:, j % 4, :], ps[:, 2 * (j % 2):2 * (j % 2) + 2, 0:KEYS], AX_X, ALU.max,
                                  negate=True).then_inc(s["d_max"], 1)

            def norm(c, j):
                dve.wait_ge(s["a_exps"], c * NHEAD + j + 1)
                dve.reciprocal(rrec[:, j % 4, :], rowsum[:, j % 4, :]).then_inc(s["d_rc"], 1)
                dve.wait_ge(s["d_rc"], c * NHEAD + j + 1)
                for st in range(HALVES):
                    e = dve.tensor_scalar(prb[:, j % 4, st, 0:KEYS], prb[:, j % 4, st, 0:KEYS],
                                          rrec[:, j % 4, st:st + 1], None, ALU.mult)
                e.then_inc(s["d_norm"], 1)

            def lo_ot(c, gr):
                dve.wait_ge(s["a_ot"], c * KC + gr + 1)
                dve.tensor_tensor(oT_lo[:, gr, :], ps[:, 5, 0:BODY], oT_hi[:, gr, :].bitcast(F32), ALU.subtract)
                dve.tensor_copy(ocls[:, gr, bass.ds(c, 1)], ps[:, 5, BODY:BODY + 1]).then_inc(s["d_ot"], 1)

            def residual(c, st, bank):
                dve.wait_ge(s["t_op"], c * HALVES + st + 1)
                t = tok[:, c * HALVES + st, :]
                dve.tensor_tensor(t, ps[:, bank, :], t, ALU.add).then_inc(s["d_res"], 1)

            def tck_copy(c):
                dve.wait_ge(s["t_tck"], c + 1)
                dve.tensor_copy(pclsT[0:NHEAD, :], ps[0:NHEAD, 4, 0:BODY]).then_inc(s["d_tck"], 1)

            def body(c, first, last):
                for j in range(NHEAD):
                    top(c, j)
                    if j >= 1:
                        norm(c, j - 1)
                    elif not first:
                        norm(c - 1, NHEAD - 1)
                    if j == 0:
                        dve.wait_ge(s["t_sc"], c + 1)
                        dve.tensor_reduce(cstat[:, 0:1], ps[0:NHEAD, 6, 0:KEYS], AX_X, ALU.max, negate=True
                                          ).then_inc(s["d_scm"], 1)
                    if j == 1:
                        dve.wait_ge(s["a_expc"], c + 1)
                        dve.reciprocal(cstat[:, 2:3], cstat[:, 1:2]).then_inc(s["d_scn"], 1)
                        dve.wait_ge(s["d_scn"], 3 * c + 1)
                        dve.tensor_scalar(pc[:, 0:KEYS], pc[:, 0:KEYS], cstat[:, 2:3], None, ALU.mult
                                          ).then_inc(s["d_scn"], 1)
                        dve.wait_ge(s["d_scn"], 3 * c + 2)
                        dve.tensor_copy(pccT[0:NHEAD, bass.ds(c, 1)], pc[:, BODY:BODY + 1]).then_inc(s["d_scn"], 1)
                    if j == 2 and not first:
                        if True:
                            dve.wait_ge(s["t_op"], (c - 1) * HALVES)
                        tck_copy(c - 1)
                    if j == 3:
                        if not first:
                            lo_ot(c - 1, 3)
                        if not last:
                            for i in range(2):
                                dve.bn_stats(lnst[:, i, :], tok[:, (c + 1) * HALVES + i, :]).then_inc(s["d_ln"], 1)
                        dve.wait_ge(s["t_tc"], c + 1)
                        if not first:
                            dve.wait_ge(s["p_ptc"], c * KC)
                        if not last:
                            dve.wait_ge(s["d_ln"], c * 5 + 12)
                        dve.tensor_copy(ptc[:, :, :], ps[:, 6, 0:2 * NHEAD].rearrange("p (t h) -> p t h", t=2)
                                        ).then_inc(s["d_ptc"], 1)
                        if not last:
                            for i in range(2):
                                dve.bn_aggr(lnmv[:, i, :], lnst[:, i, :]).then_inc(s["d_ln"], 1)
                            dve.wait_ge(s["d_ln"], c * 5 + 14)
                            dve.tensor_scalar(lnr[:, 0, :], lnmv[:, :, 1], EPS, None, ALU.add).then_inc(s["d_ln"], 1)
                    if j == 5:
                        if not first:
                            residual(c - 1, 0, 6)
                        if not last:
                            dve.wait_ge(s["p_pow"], c + 15)
                            for i in range(2):
                                dve.tensor_scalar(xhat[:, i, :],
                                                  tok[:, (c + 1) * HALVES + i, :],
                                                  lnmv[:, i, 0:1], lnr[:, 1, i:i + 1], ALU.subtract, ALU.mult
                                                  ).then_inc(s["d_x"], 1)
                    if j == 6 and not first:
                        residual(c - 1, 1, 7)
                    if j == 7 and not last:
                        lo_xT((c + 1) * HALVES + 1, 6, 0)
                        lo_xT((c + 1) * HALVES + 2, 7, 1)
                    if j in (7, 11, 15):
                        lo_ot(c, (j - 7) // 4)
                    if j >= 8 and not last:
                        lo_qk(c + 1, j - 8)

            body(0, True, False)
            with dve.Fori(1, NB - 1) as c:
                body(c, False, False)
            body(NB - 1, False, True)
            last = NB - 1
            norm(last, NHEAD - 1)
            dve.wait_ge(s["t_op"], last * HALVES)
            tck_copy(last)
            lo_ot(last, 3)
            dve.wait_ge(s["d_ot"], NB * KC)
            dve.wait_ge(s["t_sc"], NB)
            dve.memset(oc_hi[:, :, NB:P].bitcast(F32), 0.0).then_inc(s["d_qb"], 1)
            dve.memset(oc_lo[:, :, NB:P].bitcast(F32), 0.0).then_inc(s["d_qb"], 1)
            dve.tensor_copy(oc_hi[:, :, 0:NB], ocls[:, :, :]).then_inc(s["d_qb"], 1)
            dve.wait_ge(s["d_qb"], 12)
            dve.tensor_tensor(oc_lo[:, :, 0:NB], ocls[:, :, :], oc_hi[:, :, 0:NB].bitcast(F32), ALU.subtract
                              ).then_inc(s["d_qb"], 1)
            residual(last, 0, 6)
            residual(last, 1, 7)
            dve.wait_ge(s["t_fin"], 1)
            dve.tensor_tensor(tok[0:NB, CLS, :], ps[0:NB, 6, :], tok[0:NB, CLS, :], ALU.add).then_inc(s["d_fin"], 1)
            dve.wait_ge(s["d_fin"], 1)
            dve.wait_ge(s["f_const"], 2)
            dve.wait_ge(s["f_ld"], 16 * 6)
            with dve.Fori(0, TILES + 1) as t:
                dve.bn_stats(st2[:, :], tok[:, t, :]).then_inc(s["f_d"], 1)
                dve.wait_ge(s["f_d"], t * 3 + 1)
                dve.memset(idxf[:, :], 0.0)
                dve.bn_aggr(mv2[:, :], st2[:, :]).then_inc(s["f_d"], 1)
                dve.wait_ge(s["f_d"], t * 3 + 2)
                dve.tensor_scalar(rs2[:, 0:1], mv2[:, 1:2], EPS, None, ALU.add).then_inc(s["f_d"], 1)
                dve.wait_ge(s["f_pow"], t + 1)
                dve.tensor_scalar(xn[:, :], tok[:, t, :], mv2[:, 0:1], rs2[:, 1:2], ALU.subtract, ALU.mult).then_inc(s["f_dx"], 1)
                dve.tensor_tensor(tok[:, t, :], tok[:, t, :], ob[:, :], ALU.add).then_inc(s["f_dx"], 1)
                dve.wait_ge(s["f_tr"], t + 1)
                dve.tensor_tensor(lg[:, :], ps[:, 1, 0:NE], rb[:, :], ALU.add).then_inc(s["f_dl"], 1)
                dve.wait_ge(s["f_dl"], t * 8 + 1)
                dve.tensor_reduce(psum_[:, 0:1], lg[:, :], AX_X, ALU.max, negate=True).then_inc(s["f_dl"], 1)
                dve.wait_ge(s["f_ae"], t + 1)
                dve.reciprocal(psum_[:, 2:3], psum_[:, 1:2]).then_inc(s["f_dl"], 1)
                dve.wait_ge(s["f_dl"], t * 8 + 3)
                dve.tensor_scalar(probs[:, :], probs[:, :], psum_[:, 2:3], None, ALU.mult).then_inc(s["f_dl"], 1)
                dve.wait_ge(s["f_dl"], t * 8 + 4)
                dve.memset(idxf[:, :], 0.0)
                dve.max(top8[:, :], probs[:, :]).then_inc(s["f_dl"], 1)
                dve.wait_ge(s["f_dl"], t * 8 + 5)
                dve.memset(idxf[:, :], 0.0)
                dve.max_index(idx8[:, :], top8[:, :], probs[:, :]).then_inc(s["f_dl"], 1)
                dve.tensor_tensor(psum_[:, 3:4], top8[:, 0:1], top8[:, 1:2], ALU.add).then_inc(s["f_dl"], 1)
                dve.wait_ge(s["f_dl"], t * 8 + 7)
                dve.reciprocal(psum_[:, 2:3], psum_[:, 3:4]).then_inc(s["f_dl"], 1)
                dve.wait_ge(s["f_dl"], t * 8 + 8)
                dve.tensor_scalar(top8[:, 0:2], top8[:, 0:2], psum_[:, 2:3], None, ALU.mult).then_inc(s["f_dg"], 1)
                dve.tensor_copy(idxf[:, :], idx8[:, 0:2]).then_inc(s["f_dg"], 1)
                dve.wait_ge(s["f_dg"], t * 13 + 2)
                for i in range(2):
                    dve.tensor_scalar(gates[:, i, :], iota[:, :], idxf[:, i:i + 1], top8[:, i:i + 1], ALU.is_equal,
                                      ALU.mult).then_inc(s["f_dg"], 1)
                dve.wait_ge(s["f_dg"], t * 13 + 4)
                dve.tensor_tensor(gates[:, 0, :], gates[:, 0, :], gates[:, 1, :], ALU.add).then_inc(s["f_dg"], 1)
                dve.wait_ge(s["f_dg"], t * 13 + 5)

                def combine(e):
                    dve.wait_ge(s["f_ag"], t * NE + e + 1)
                    if e == 0:
                        dve.tensor_scalar(comb[:, :], act_out[:, 0, :], gates[:, 0, 0:1], None, ALU.mult).then_inc(s["f_dg"], 1)
                    else:
                        dve.wait_ge(s["f_dg"], t * 13 + 5 + e)
                        dve.scalar_tensor_tensor(out=comb[:, :], in0=act_out[:, e % 2, :], scalar=gates[:, 0, e:e + 1],
                                                 in1=comb[:, :], op0=ALU.mult, op1=ALU.add).then_inc(s["f_dg"], 1)

                for e in range(NE):
                    dve.wait_ge(s["f_te"], t * NE + e + 1)
                    dve.tensor_tensor(pre[:, e % 2, :], ps[:, 2 + e % 2, :], eb[:, e, :], ALU.add).then_inc(s["f_dp"], 1)
                    if e >= 1:
                        combine(e - 1)
                combine(NE - 1)
                dve.wait_ge(s["f_to"], t + 1)
                dve.tensor_tensor(tok[:, t, :], ps[:, 5, :], tok[:, t, :], ALU.add).then_inc(s["f_do"], 1)

        @block.tensor
        def _(pe):
            pe.wait_ge(s["c_ident"], 2)

            def w_turn(raw, sem_t, bank0):
                for ic in range(KC):
                    for o in range(KC):
                        mm = pe.transpose(ps[:, bank0 + ic, o * P:(o + 1) * P], raw[:, o, ic * P:(ic + 1) * P], ident[:, :])
                    mm.then_inc(s[sem_t], 1)

            pe.wait_ge(s["a_wsc"], KC)
            w_turn(w_raw[:, 0], "t_w", 4)
            pe.wait_ge(s["a_wsc"], 2 * KC)
            pe.wait_ge(s["d_wlo"], KC)
            w_turn(w_raw[:, 1], "t_w", 4)

            def turn(n, parts):
                if n >= 4:
                    pe.wait_ge(s["a_tr"], n - 3)
                for k, part in enumerate(parts):
                    for q in range(4):
                        mm = pe.matmul(ps[:, n % 4, q * P:(q + 1) * P], part(q), ident[:, :], is_transpose=True,
                                       start=(k == 0 and q == 0), stop=(k == len(parts) - 1 and q == 3),
                                       skip_group_check=True)
                mm.then_inc(s["t_tr"], 1)

            for hf in range(HALVES):
                base = hf * 32
                pe.wait_ge(s["d_rl"], hf + 1)
                for q in range(8):
                    turn(base + q, [lambda i, q=q: r_low[:, 4 * q + i, :, :].rearrange("p s n -> p (s n)")])
                for n in range(12):
                    if n < 4:
                        pe.wait_ge(s["d_up"], hf * 4 + n + 1)
                    else:
                        pe.wait_ge(s["d_lp"], hf * NB + n - 4 + 1)
                    for k in range(2):
                        turn(base + 8 + 2 * n + k,
                             [lambda i, w=w, n=n, k=k: ring[:, n % 2, w, 4 * k + i, :, :].rearrange("p s n -> p (s n)")
                              for w in range(2)])
                pe.wait_ge(s["a_tr"], base + 32)
                if hf == 0:
                    pe.wait_ge(s["d_wlo"], 2 * KC)
                for hb in range(NHB):
                    n = hf * NHB + hb
                    if n >= 2:
                        pe.wait_ge(s["a_so"], n - 1)
                    for i in range(HB):
                        for hp in range(2):
                            h = hp * 64 + hb * HB + i
                            bank = 4 + 2 * (n % 2) + i // 8
                            mm = pe.matmul(ps[hp * 64:hp * 64 + 64, bank, (i % 8) * NBP:(i % 8 + 1) * NBP],
                                           lT[:, h, :], rT[:, h, :], start=(i % 8 == 0), stop=(i % 8 == 7),
                                           skip_group_check=True)
                    mm.then_inc(s["t_mm"], 1)

            def split3(out_ap, lhs, rhs, start, stop, skip=False):
                (lh, ll), (rh, rl) = lhs, rhs
                for i, (a, b) in enumerate(((lh, rh), (ll, rh), (lh, rl))):
                    mm = pe.matmul(out_ap, a, b, start=start and i == 0, stop=stop and i == 2, skip_group_check=skip)
                return mm

            def x_turn(n, bank, i, rows):
                pe.wait_ge(s["d_x"], 2 * ((n + 1) // 2) + i + 1 if isinstance(n, int) and n == 0 else n + 2)
                w = rows
                for k in range(KC):
                    mm = pe.transpose(ps[:, bank, k * w:(k + 1) * w], xhat[0:rows, i, k * P:(k + 1) * P],
                                      ident[0:rows, 0:rows])
                mm.then_inc(s["t_x"], 1)

            pe.wait_ge(s["a_so"], HALVES * NHB)
            x_turn(0, 7, 0, NB)
            pe.wait_ge(s["d_x"], 2)
            x_turn(1, 6, 0, P)
            pe.wait_ge(s["d_loT"], 1)
            x_turn(2, 7, 1, P)

            def qk(c, m):
                hi, lo = (wqT_hi, wqT_lo) if m % 2 == 0 else (wkT_hi, wkT_lo)
                ci = m // 2
                for ic in range(KC):
                    w = slice(ci * P, (ci + 1) * P)
                    mm = split3(ps[:, 6 + m % 2, 0:KPAD], (hi[:, ic, w], lo[:, ic, w]),
                                (xT_hi[:, ic, :], xT_lo[:, ic, :]), ic == 0, ic == KC - 1)
                mm.then_inc(s["t_qk"], 1)

            def qk_wait(c, m):
                if m == 0:
                    pe.wait_ge(s["d_loT"], c * HALVES + 3)
                elif m >= 2:
                    pe.wait_ge(s["d_loqk"], c * 2 * KC + m - 1)

            for m in range(2 * KC):
                qk_wait(0, m)
                qk(0, m)
            pe.wait_ge(s["ld_wv"], 32)
            for i in range(2):
                if i == 1:
                    pe.wait_ge(s["d_wvlo"], KC)
                w_turn(w_raw2[:, i], "t_wv", 0)
            pe.wait_ge(s["d_wvlo"], KC)
            for ci in range(KC):
                for ic in range(KC):
                    w = slice(ci * P, (ci + 1) * P)
                    mm = split3(ps[:, 4, 2 * ci:2 * ci + 2], (wvT_hi[:, ic, w], wvT_lo[:, ic, w]),
                                (xT_hi[:, ic, BODY:KPAD], xT_lo[:, ic, BODY:KPAD]), ic == 0, ic == KC - 1, True)
            mm.then_inc(s["t_vb"], 1)
            pe.wait_ge(s["d_wvlo"], 2 * KC)
            pe.wait_ge(s["d_vb"], KC + 1)
            pe.wait_ge(s["c_ones"], 4)
            pe.wait_ge(s["ld_bo"], 16)
            for ci in range(KC):
                for part in (woT_hi, woT_lo):
                    pe.matmul(ps[0:32, 5, :], vblk[:, ci, :], part[:, ci, :].bitcast(F32),
                              start=(ci == 0 and part is woT_hi), stop=False)
            pe.matmul(ps[0:32, 5, :], e16[:, :], bo_row[:, :], start=False, stop=True).then_inc(s["t_u"], 1)

            def scores(c, j):
                if j % (2 * HPC) == 0:
                    pe.wait_ge(s_rq[j // (2 * HPC)], RESTACK * (c + 1))
                for st in range(HALVES):
                    mm = pe.matmul(ps[:, 2 * (j % 2) + st, 0:KPAD], q4[:, j, st * P:st * P + P], k4[:, j, :],
                                   start=True, stop=True)
                mm.then_inc(s["t_s"], 1)

            def turn_p(c, j):
                pe.wait_ge(s["d_norm"], c * NHEAD + j + 1)
                for tt in range(HALVES):
                    for st in range(HALVES):
                        mm = pe.transpose(ps[:, 4, tt * BODY + st * P:tt * BODY + (st + 1) * P],
                                          prb[:, j % 4, st, tt * P:(tt + 1) * P], ident[:, :])
                mm.then_inc(s["t_tp"], 1)

            def pv(c, gr):
                pe.wait_ge(s["a_pt"], c * NHEAD + (gr + 1) * HPC)
                pe.wait_ge(s["p_ptc"], c * KC + gr + 1)
                for tt in range(HALVES):
                    for j in range(HPC):
                        h = gr * HPC + j
                        mm = pe.matmul(ps[j * DH:(j + 1) * DH, 5, 0:KEYS], v_sb[:, tt, h * DH:(h + 1) * DH],
                                       pts[:, h % 8, tt, 0:KEYS], start=(tt == 0), stop=(tt == HALVES - 1))
                mm.then_inc(s["t_pv"], 1)

            def cls_scores(c):
                for ci in range(KC):
                    mm = split3(ps[:, 6, 0:KPAD], (qblk_hi[:, ci, :], qblk_lo[:, ci, :]),
                                (k_hi[:, ci, :], k_lo[:, ci, :]), ci == 0, ci == KC - 1)
                mm.then_inc(s["t_sc"], 1)

            def cls_turn(c):
                for tt in range(HALVES):
                    mm = pe.transpose(ps[:, 6, tt * NHEAD:(tt + 1) * NHEAD], pc[:, tt * P:(tt + 1) * P],
                                      ident[0:NHEAD, 0:NHEAD])
                mm.then_inc(s["t_tc"], 1)

            def values(c, st):
                for ic in range(KC):
                    w = slice(st * P, (st + 1) * P)
                    mm = split3(ps[:, 7, :], (xT_hi[:, ic, w], xT_lo[:, ic, w]),
                                (wvT_hi[:, ic, :], wvT_lo[:, ic, :]), ic == 0, ic == KC - 1)
                mm.then_inc(s["t_v"], 1)

            def key_turn(c):
                pe.wait_ge(s["p_pc"], (c + 1) * NHEAD)
                pe.wait_ge(s["a_pt"], (c + 1) * NHEAD)
                for st in range(HALVES):
                    mm = pe.transpose(ps[0:NHEAD, 4, st * P:(st + 1) * P], pcls[:, st, :], ident[:, :])
                mm.then_inc(s["t_tck"], 1)

            def project(c, st, bank):
                w = slice(st * P, (st + 1) * P)
                pe.matmul(ps[:, bank, :], pclsT[:, w], u_sb[:, :], start=True, stop=False)
                for ic in range(KC):
                    mm = split3(ps[:, bank, :], (oT_hi[:, ic, w], oT_lo[:, ic, w]),
                                (woT_hi[:, ic, :], woT_lo[:, ic, :]), False, ic == KC - 1)
                mm.then_inc(s["t_op"], 1)

            def body(c, first, last):
                for j in range(NHEAD):
                    if j >= 2 or not first:
                        pe.wait_ge(s["a_exps"], c * NHEAD + j - 1)
                    scores(c, j)
                    if j >= 3:
                        pe.wait_ge(s["a_pt"], c * NHEAD + j - 2)
                    elif j == 2:
                        if not first:
                            pe.wait_ge(s["a_pt"], c * NHEAD)
                    elif not first:
                        pe.wait_ge(s["a_pt"], c * NHEAD - 2 + j)
                    if j >= 2:
                        if j == 3 and not first:
                            pe.wait_ge(s["d_tck"], c)
                        if j == 2 and not first:
                            key_turn(c - 1)
                            pe.wait_ge(s["d_tck"], c)
                        turn_p(c, j - 2)
                    elif not first:
                        turn_p(c - 1, NHEAD - 2 + j)
                    if j == 0:
                        pe.wait_ge(s["d_loqk"], (c + 1) * 2 * KC)
                        if first:
                            pe.wait_ge(s["d_qb"], 1 + 2 * KC)
                        cls_scores(c)
                    if j == 1:
                        values(c, 0)
                    if j == 2 and not first:
                        pe.wait_ge(s["d_ot"], c * KC - 1)
                        pv(c - 1, 3)
                    if j == 3:
                        pe.wait_ge(s["d_scn"], 3 * c + 3)
                        pe.wait_ge(s["a_expc"], c + 1)
                        pe.wait_ge(s["a_v"], c * HALVES + 1)
                        values(c, 1)
                        cls_turn(c)
                    if j == 4 and not first:
                        pe.wait_ge(s["d_tck"], c)
                        pe.wait_ge(s["d_ot"], c * KC)
                        pe.wait_ge(s["d_ptc"], c + 1)
                        project(c - 1, 0, 6)
                    if j == 5 and not first:
                        pe.wait_ge(s["a_v"], c * HALVES + 2)
                        project(c - 1, 1, 7)
                    if j == 7 and not last:
                        if first:
                            pe.wait_ge(s["d_u"], 1)
                            pe.wait_ge(s["d_ptc"], c + 1)
                            pe.wait_ge(s["a_v"], c * HALVES + 2)
                        else:
                            pe.wait_ge(s["d_res"], c * HALVES - 1)
                        pe.wait_ge(s["d_x"], (c + 1) * HALVES + 3)
                        x_turn2(c + 1, 0, 6)
                        if not first:
                            pe.wait_ge(s["d_res"], c * HALVES)
                        pe.wait_ge(s["d_x"], (c + 1) * HALVES + 4)
                        x_turn2(c + 1, 1, 7)
                    if j >= 8 and not last:
                        m = j - 8
                        qk_wait(c + 1, m)
                        qk(c + 1, m)
                    if j in (6, 10, 14):
                        if j == 6:
                            pe.wait_ge(s["a_v"], (c + 1) * HALVES)
                        if j > 6 or not first:
                            pe.wait_ge(s["d_ot"], c * KC + (j - 6) // 4)
                        pv(c, (j - 6) // 4)

            def x_turn2(c, i, bank):
                for k in range(KC):
                    mm = pe.transpose(ps[:, bank, k * P:(k + 1) * P], xhat[:, i, k * P:(k + 1) * P], ident[:, :])
                mm.then_inc(s["t_x"], 1)

            body(0, True, False)
            with pe.Fori(1, NB - 1) as c:
                body(c, False, False)
            body(NB - 1, False, True)
            last = NB - 1
            pe.wait_ge(s["a_pt"], NB * NHEAD - 2)
            turn_p(last, NHEAD - 2)
            pe.wait_ge(s["a_pt"], NB * NHEAD - 1)
            turn_p(last, NHEAD - 1)
            key_turn(last)
            pe.wait_ge(s["d_ot"], NB * KC - 1)
            pv(last, 3)
            pe.wait_ge(s["d_tck"], NB)
            pe.wait_ge(s["d_ot"], NB * KC)
            project(last, 0, 6)
            project(last, 1, 7)
            pe.wait_ge(s["d_qb"], 13)
            pe.wait_ge(s["d_res"], NB * HALVES - 1)
            pe.matmul(ps[:, 6, :], pccT[:, :], u_sb[:, :], start=True, stop=False)
            for ic in range(KC):
                mm = split3(ps[:, 6, :], (oc_hi[:, ic, :], oc_lo[:, ic, :]), (woT_hi[:, ic, :], woT_lo[:, ic, :]),
                            False, ic == KC - 1)
            mm.then_inc(s["t_fin"], 1)
            pe.wait_ge(s["d_fin"], 1)
            pe.wait_ge(s["f_ld"], 16 * 6)
            with pe.Fori(0, TILES + 1) as t:
                pe.wait_ge(s["f_dx"], t * 2 + 1)
                for k in range(KC):
                    mm = pe.transpose(ps[:, 0, k * P:(k + 1) * P], xn[:, k * P:(k + 1) * P], ident[:, :])
                mm.then_inc(s["f_tx"], 1)
                pe.wait_ge(s["f_ax"], t + 1)
                for k in range(KC):
                    mm = pe.matmul(ps[:, 1, 0:NE], xnT[:, k, :], rw[:, k, :], start=(k == 0), stop=(k == KC - 1))
                mm.then_inc(s["f_tr"], 1)
                for e in range(NE):
                    if e >= 2:
                        pe.wait_ge(s["f_dp"], t * NE + e - 1)
                    for k in range(KC):
                        mm = pe.matmul(ps[:, 2 + e % 2, :], xnT[:, k, :], ew[:, e, k, :], start=(k == 0), stop=(k == KC - 1))
                    mm.then_inc(s["f_te"], 1)
                pe.wait_ge(s["f_dg"], (t + 1) * 13)
                for k in range(KC):
                    mm = pe.transpose(ps[:, 4, k * P:(k + 1) * P], comb[:, k * P:(k + 1) * P], ident[:, :])
                mm.then_inc(s["f_tc"], 1)
                pe.wait_ge(s["f_ac"], t + 1)
                for k in range(KC):
                    mm = pe.matmul(ps[:, 5, :], combT[:, k, :], ow[:, k, :], start=(k == 0), stop=(k == KC - 1))
                mm.then_inc(s["f_to"], 1)


_INS = ['x', 'cls_tok', 'L0_tok_log_dt', 'L0_tok_B_ri', 'L0_tok_inv_A_real', 'L0_tok_A_imag', 'L0_attn_Wq',
        'L0_attn_bq', 'L0_attn_Wk', 'L0_attn_bk', 'L0_attn_Wv', 'L0_attn_bv', 'L0_attn_Wo', 'L0_attn_bo',
        'L0_attn_spiral_weight', 'L0_attn_helix_rotation', 'L0_ffn_router_w', 'L0_ffn_router_b',
        'L0_ffn_expert_w', 'L0_ffn_expert_b', 'L0_ffn_out_w', 'L0_ffn_out_b']
_OUTS = [((8, 257, 512), 'float32')]


def kernel(**inputs):
    import numpy as _np
    import concourse.bacc as _bacc
    from concourse import mybir as _mybir
    from concourse.bass_utils import run_bass_kernel_spmd as _run

    nc = _bacc.Bacc("TRN2", target_bir_lowering=False, num_devices=1)
    arrays, args = {}, []
    for name in _INS:
        a = _np.ascontiguousarray(inputs[name])
        arrays[f"in_{name}_dram"] = a
        args.append(nc.dram_tensor(f"in_{name}_dram", a.shape, _mybir.dt.from_np(a.dtype), kind="ExternalInput").ap())
    for i, (shape, dtype) in enumerate(_OUTS):
        dt = _mybir.dt.from_np(_np.dtype(dtype))
        args.append(nc.dram_tensor(f"out_{i}_dram", shape, dt, kind="ExternalOutput").ap())
    vit_tower_kernel(nc, *args)
    r = _run(nc, [arrays], core_ids=[0])
    got = tuple(r.results[0][f"out_{i}_dram"] for i in range(len(_OUTS)))
    return got[0]
```

```python
from contextlib import ExitStack

import concourse.bass as bass
from concourse import mybir

F32 = mybir.dt.float32
F32R = mybir.dt.float32r
ALU = mybir.AluOpType
ACT = mybir.ActivationFunctionType
AX_X = mybir.AxisListType.X

P = 128
BANK = 512
EPS = 1e-5
TWO_PI_HI = 6.28125
TWO_PI_LO = 0.0019353071795864769
PI_SAFE = 3.1415925
ROUND_MAGIC = 12582912.0


def vit_tower_kernel(nc, x, cls_tok, log_dt, B_ri, inv_A_real, A_imag, Wq, bq, Wk, bk, Wv, bv, Wo, bo,
                     spiral, rot, router_w, router_b, expert_w, expert_b, out_w, out_b, out):
    NB, NH_SSM, NS, _ = x.shape
    D = Wq.shape[0]
    NHEAD = spiral.shape[0]
    DH = D // NHEAD
    NE = router_w.shape[1]
    KC = D // P
    HPC = P // DH
    HALVES = NH_SSM // P
    BODY = HALVES * P
    KEYS = BODY + 1
    KPAD = KEYS + 1
    S2 = 2 * NS
    NA = 8
    NBP = D // NA
    NLOW = NBP // 2
    PIECE = 8
    TILES = NB * HALVES
    CLS = TILES
    HB = 16
    NHB = P // 2 // HB
    QK_SLOT = {j: () for j in range(NHEAD)} | {9: (0,), 10: (1,), 11: (2,), 12: (3,), 13: (4,), 14: (5,), 15: (6, 7)}
    assert S2 == P and NBP * NA == D and NB * NA == 64 and HALVES == 2 and DH == 32

    with ExitStack() as whole:
        def sb(scope, name, shape, dt=F32):
            return scope.enter_context(nc.sbuf_tensor(name, shape, dt))

        def sem(name):
            return whole.enter_context(nc.semaphore(name))

        ps = whole.enter_context(nc.psum_tensor("ps", [P, 8, BANK], F32))

        ident = sb(whole, "ident", [P, P])
        tok = sb(whole, "tok", [P, TILES + 1, D])
        attn = ExitStack()
        wqT_hi = sb(attn, "wqT_hi", [P, KC, D], F32R)
        wqT_lo = sb(attn, "wqT_lo", [P, KC, D], F32R)
        wkT_hi = sb(attn, "wkT_hi", [P, KC, D], F32R)
        wkT_lo = sb(attn, "wkT_lo", [P, KC, D], F32R)
        q_scale = sb(attn, "q_scale", [P, KC])
        k_scale = sb(attn, "k_scale", [P, KC])
        q_bias = sb(attn, "q_bias", [P, KC])
        k_bias = sb(attn, "k_bias", [P, KC])
        bv_col = sb(attn, "bv_col", [P, KC])
        mk = ExitStack()
        ldt = sb(mk, "ldt", [P, HALVES])
        iar = sb(mk, "iar", [P, HALVES, NS])
        aim = sb(mk, "aim", [P, HALVES, NS])
        b_in = sb(mk, "b_in", [P, HALVES, NS, 2])
        x_in = sb(mk, "x_in", [P, NB, NS, 2])
        coef = sb(mk, "coef", [P, NB, 2, NS])
        ctmp = sb(mk, "ctmp", [P, NB, NS])
        g = sb(mk, "g", [P, HALVES, 2, NS])
        prm = sb(mk, "prm", [P, 8, HALVES, NS])
        dt2 = sb(mk, "dt2", [P, 2, HALVES])
        zs = sb(mk, "zs", [P, 9, 2, NS])
        zt = sb(mk, "zt", [P, 9, 2, NS])
        r_low = sb(mk, "r_low", [P, NLOW, 2, NS])
        w_pow = sb(mk, "w_pow", [P, NA, 2, NS])
        w_b = sb(mk, "w_b", [P, NA, 2, NS])
        ring = sb(mk, "ring", [P, 2, 2, PIECE, 2, NS])
        rT = sb(mk, "rT", [P, P, NBP])
        so = sb(mk, "so", [P, 2, HB * NBP])
        rcol = sb(mk, "rcol", [P, 4, KC])
        with ExitStack() as early:
            w_raw = sb(early, "w_raw", [P, 2, KC, D])
        lT = sb(mk, "lT", [P, P, NB * NA])
        mk.close()
        at = attn
        wvT_hi = sb(at, "wvT_hi", [P, KC, D], F32R)
        wvT_lo = sb(at, "wvT_lo", [P, KC, D], F32R)
        woT_hi = sb(at, "woT_hi", [P, KC, D], F32R)
        woT_lo = sb(at, "woT_lo", [P, KC, D], F32R)
        xT_hi = sb(at, "xT_hi", [P, KC, KPAD], F32R)
        xT_lo = sb(at, "xT_lo", [P, KC, KPAD], F32R)
        xhat = sb(at, "xhat", [P, HALVES, D])
        q_hi = sb(at, "q_hi", [P, NHEAD, BODY], F32R)
        q_lo = sb(at, "q_lo", [P, NHEAD, BODY], F32R)
        qcls_hi = sb(at, "qcls_hi", [P, KC, 2], F32R)
        qcls_lo = sb(at, "qcls_lo", [P, KC, 2], F32R)
        k_hi = sb(at, "k_hi", [P, KC, KPAD], F32R)
        k_lo = sb(at, "k_lo", [P, KC, KPAD], F32R)
        v_sb = sb(at, "v_sb", [P, HALVES, D])
        oT_hi = sb(at, "oT_hi", [P, KC, BODY], F32R)
        oT_lo = sb(at, "oT_lo", [P, KC, BODY], F32R)
        u_sb = sb(at, "u_sb", [P, D])
        pclsT = sb(at, "pclsT", [P, BODY])
        pccT = sb(at, "pccT", [P, P])
        pcls = sb(at, "pcls", [P, HALVES, NHEAD])
        pc = sb(at, "pc", [NHEAD, KPAD])
        ptc = sb(at, "ptc", [P, HALVES, NHEAD])
        ocls = sb(at, "ocls", [P, KC, NB])
        negmax = sb(at, "negmax", [P, 4, HALVES])
        rowsum = sb(at, "rowsum", [P, 4, HALVES])
        rrec = sb(at, "rrec", [P, 4, HALVES])
        cstat = sb(at, "cstat", [NHEAD, 4])
        lnst = sb(at, "lnst", [P, HALVES, 6])
        lnmv = sb(at, "lnmv", [P, HALVES, 2])
        lnr = sb(at, "lnr", [P, 2, HALVES])
        mhalf = sb(at, "mhalf", [P, HALVES])
        ones = sb(at, "ones", [P, HALVES, HPC])
        qblk_hi = sb(at, "qblk_hi", [P, KC, P], F32R)
        qblk_lo = sb(at, "qblk_lo", [P, KC, P], F32R)
        late = ExitStack()
        prb = sb(late, "prb", [P, 4, HALVES, KPAD])
        pts = sb(late, "pts", [P, 8, HALVES, KPAD])
        late.close()
        setup = ExitStack()
        w_raw2 = sb(setup, "w_raw2", [P, 2, KC, D])
        mask = sb(setup, "mask", [P, KC, P])
        vblk = sb(setup, "vblk", [P, KC, 32])
        bo_row = sb(setup, "bo_row", [1, D])
        e16 = sb(setup, "e16", [1, 32])
        setup.close()
        oc_hi, oc_lo = qblk_hi, qblk_lo
        attn.close()
        ffn = whole
        with ExitStack() as as_loaded:
            ew = sb(as_loaded, "ew", [P, NE, KC, D])
            rw = sb(as_loaded, "rw", [P, KC, NE])
        ew_lo = sb(ffn, "ew_lo", [P, NE, KC, D], F32R)
        rw_lo = sb(ffn, "rw_lo", [P, KC, NE], F32R)
        ew_hi = sb(ffn, "ew_hi", [P, NE, KC, D], F32R)
        ow = sb(ffn, "ow", [P, KC, D])
        rw_hi = sb(ffn, "rw_hi", [P, KC, NE], F32R)
        eb = sb(ffn, "eb", [P, NE, D])
        ob = sb(ffn, "ob", [P, D])
        rb = sb(ffn, "rb", [P, NE])
        iota = sb(ffn, "iota", [P, NE])
        xn = sb(ffn, "xn", [P, D])
        xnT_hi = sb(ffn, "xnT_hi", [P, KC, P], F32R)
        xnT_lo = sb(ffn, "xnT_lo", [P, KC, P], F32R)
        act_out = sb(ffn, "act_out", [P, 2, D])
        comb = sb(ffn, "comb", [P, D])
        combT = sb(ffn, "combT", [P, KC, P])
        st2 = sb(ffn, "st2", [P, 6])
        mv2 = sb(ffn, "mv2", [P, 2])
        rs2 = sb(ffn, "rs2", [P, 2])
        mh2 = sb(ffn, "mh2", [P, 1])
        lg = sb(ffn, "lg", [P, NE])
        probs = sb(ffn, "probs", [P, NE])
        rstat = sb(ffn, "rstat", [P, 4])
        top8 = sb(ffn, "top8", [P, 8])
        idx8 = sb(ffn, "idx8", [P, 8], mybir.dt.uint32)
        idxf = sb(ffn, "idxf", [P, 2])
        gates = sb(ffn, "gates", [P, 2, NE])

        s = {}
        for n in ("c_cls c_zero ld_par ld_x0 ld_x1 ld_w0 ld_w1 ld_cls ld_rot ld_wv ld_bo c_ident c_ones c_fix c_mask "
                  "a_exp a_sin a_wsc a_whi a_tr a_so a_expc a_v a_hiT a_hiqk a_exps a_pt a_ot a_wvhi a_fin "
                  "d_par d_coef d_pow d_rl d_up d_lp d_wlo d_so d_rot d_ln d_x d_loT d_loqk d_max d_rc d_norm "
                  "d_scm d_scn d_ptc d_tck d_ot d_res d_qb d_wvlo d_vb d_u d_fin "
                  "p_coef p_pow p_pc p_ptc p_mask "
                  "t_w t_tr t_mm t_x t_qk t_v t_sc t_tc t_op t_s t_tp t_tck t_pv t_wv t_vb t_u t_fin "
                  "m_tok m_out "
                  "ld_router ld_bias ld_outw p_const p_rstd p_outb d_ln2 d_xn d_rwlo d_loxn d_route d_gate d_ewlo d_pre d_comb d_out "
                  "a_rwhi a_hixn a_rexp a_ewhi a_gelu a_combT t_xn t_router t_expert t_comb t_out").split():
            s[n] = sem(n)
        ld_ew = [sem(f"ld_ew{e}") for e in range(NE)]
        s_row = [sem(f"m_row{i}") for i in range(2)]
        tok_dram = nc.dram_tensor("tok_dram", [HALVES, P, 64, NBP], F32).ap()

        block = whole.enter_context(nc.Block())
        bc = lambda ap, shape: ap.broadcast_to(shape)

        @block.sync
        def _(sp):
            whole.enter_context(nc.allow_non_contiguous_dma(reason="a few hundred words of parameters"))
            sp.dma_start(ldt[:, :], log_dt.rearrange("(f p) -> p f", p=P)).then_inc(s["ld_par"], 16)
            sp.dma_start(iar[:, :, :], inv_A_real.rearrange("(f p) n -> p f n", p=P)).then_inc(s["ld_par"], 16)
            sp.dma_start(aim[:, :, :], A_imag.rearrange("(f p) n -> p f n", p=P)).then_inc(s["ld_par"], 16)
            sp.dma_start(b_in[:, :, :, :], B_ri.rearrange("(f p) n r -> p f n r", p=P)).then_inc(s["ld_par"], 16)
            sp.dma_start(x_in[:, :, :, :], x[:, 0:P].rearrange("c p n r -> p c n r")).then_inc(s["ld_x0"], 16)
            sp.dma_start(rcol[:, 0, :], rot.rearrange("(k p) -> p k", p=P)).then_inc(s["ld_rot"], 16)
            for j in range(HPC):
                sp.dma_start(rcol[j * DH:(j + 1) * DH, 1, :],
                             spiral.rearrange("(k j) -> j k", j=HPC)[j:j + 1, :].broadcast_to([DH, KC])
                             ).then_inc(s["ld_rot"], 16)
            sp.dma_start(q_bias[:, :], bq.rearrange("(k p) -> p k", p=P)).then_inc(s["ld_rot"], 16)
            sp.dma_start(k_bias[:, :], bk.rearrange("(k p) -> p k", p=P)).then_inc(s["ld_rot"], 16)
            sp.dma_start(w_raw[:, 0, :, :], Wq.rearrange("(o p) i -> p o i", p=P)).then_inc(s["ld_w0"], 16)
            sp.dma_start(w_raw[:, 1, :, :], Wk.rearrange("(o p) i -> p o i", p=P)).then_inc(s["ld_w1"], 16)
            sp.dma_start(bv_col[:, :], bv.rearrange("(k p) -> p k", p=P)).then_inc(s["ld_rot"], 16)
            sp.wait_ge(s["c_cls"], 1)
            sp.dma_start(tok[0:NB, CLS, :], cls_tok[0, :, :].broadcast_to([NB, D])).then_inc(s["ld_cls"], 16)
            sp.wait_ge(s["p_coef"], 1)
            sp.dma_start(x_in[:, :, :, :], x[:, P:2 * P].rearrange("c p n r -> p c n r")).then_inc(s["ld_x1"], 16)
            for hf in range(HALVES):
                for hb in range(NHB):
                    n = hf * NHB + hb
                    sp.wait_ge(s["a_so"], n + 1)
                    sp.dma_start(tok_dram[hf, :, hb * HB:(hb + 1) * HB, :],
                                 so[:, n % 2, :].rearrange("r (h b) -> r h b", h=HB)).then_inc(s_row[n % 2], 16)
                for row in s_row:
                    sp.wait_ge(row, 16 * NHB // 2 * (hf + 1))
                for hp in range(2):
                    for c in range(NB):
                        r0 = hp * 64 + c * NA
                        sp.dma_start(
                            tok[hp * 64:hp * 64 + 64, c * HALVES + hf, :].rearrange("h (a b) -> h a b", a=NA),
                            tok_dram[hf, r0:r0 + NA, :, :].rearrange("a h b -> h a b")).then_inc(s["m_tok"], 16)
            sp.wait_ge(s["t_mm"], HALVES * NHB)
            sp.wait_ge(s["m_tok"], 16 * 2 * NB * HALVES)
            sp.dma_start(w_raw2[:, 0, :, :], Wv.rearrange("(o p) i -> p o i", p=P)).then_inc(s["ld_wv"], 16)
            sp.dma_start(w_raw2[:, 1, :, :], Wo.rearrange("(o p) i -> p o i", p=P)).then_inc(s["ld_wv"], 16)
            sp.dma_start(bo_row[:, :], bo.rearrange("(a d) -> a d", a=1)).then_inc(s["ld_bo"], 16)


            def load_expert(e):
                sp.dma_start(ew[:, e, :, :], expert_w[e].rearrange("(k p) d -> p k d", p=P)
                             ).then_inc(ld_ew[e], 16)

            sp.wait_ge(s["t_qk"], NB * 2 * KC)
            for e in range(NE // 2):
                load_expert(e)
            sp.wait_ge(s["d_fin"], 1)
            sp.dma_start(rw[:, :, :], router_w.rearrange("(k p) e -> p k e", p=P)
                         ).then_inc(s["ld_router"], 16)
            sp.dma_start(rb[:, :], router_b.rearrange("(a n) -> a n", a=1).broadcast_to([P, NE])
                         ).then_inc(s["ld_router"], 16)
            sp.dma_start(ob[:, :], out_b.rearrange("(a n) -> a n", a=1).broadcast_to([P, D])).then_inc(s["ld_bias"], 16)
            sp.dma_start(eb[:, :, :].rearrange("p e d -> p (e d)"),
                         expert_b.rearrange("e d -> (e d)").rearrange("(a n) -> a n", a=1).broadcast_to([P, NE * D])
                         ).then_inc(s["ld_bias"], 16)
            for e in range(NE // 2, NE):
                load_expert(e)
            sp.dma_start(ow[:, :, :], out_w.rearrange("(k p) d -> p k d", p=P)).then_inc(s["ld_outw"], 16)
            for t in range(TILES + 1):
                sp.wait_ge(s["d_out"], t + 1)
                if t < TILES:
                    st = t % 2
                    sp.dma_start(out[t // 2, 1 + st * P:1 + st * P + P, :], tok[:, t, :]).then_inc(s["m_out"], 16)
                else:
                    sp.dma_start(out[:, 0, :], tok[0:NB, CLS, :]).then_inc(s["m_out"], 16)
            sp.wait_ge(s["m_out"], (TILES + 1) * 16)

        @block.gpsimd
        def _(pool):
            pool.memset(tok[:, CLS, :], 0.0).then_inc(s["c_cls"], 1)
            nc.gpsimd.memset(ident[:, :], 0.0).then_inc(s["c_ident"], 1)
            pool.wait_ge(s["c_ident"], 1)
            nc.gpsimd.affine_select(out=ident[:, :], in_=ident[:, :], compare_op=ALU.not_equal, fill=1.0, base=0,
                                    pattern=[[-1, P]], channel_multiplier=1).then_inc(s["c_ident"], 1)
            for hf in range(HALVES):
                pool.wait_ge(s["ld_x0" if hf == 0 else "ld_x1"], 16)
                if hf == 0:
                    pool.wait_ge(s["d_coef"], 1)
                else:
                    pool.wait_ge(s["d_lp"], NB)
                xr, xi = x_in[:, :, :, 0], x_in[:, :, :, 1]
                gr = bc(g[:, hf, 0, :].unsqueeze(1), [P, NB, NS])
                gi = bc(g[:, hf, 1, :].unsqueeze(1), [P, NB, NS])
                base = 6 * hf
                cr, cim = coef[:, :, 0, :], coef[:, :, 1, :]
                pool.tensor_tensor(ctmp[:, :, :], xi, gi, ALU.mult).then_inc(s["p_pow"], 1)
                pool.tensor_tensor(cr, xr, gr, ALU.mult).then_inc(s["p_pow"], 1)
                pool.wait_ge(s["p_pow"], base + 2)
                pool.tensor_tensor(cr, cr, ctmp[:, :, :], ALU.subtract).then_inc(s["p_pow"], 1)
                pool.wait_ge(s["p_pow"], base + 3)
                pool.tensor_tensor(ctmp[:, :, :], xi, gr, ALU.mult).then_inc(s["p_pow"], 1)
                pool.tensor_tensor(cim, xr, gi, ALU.mult).then_inc(s["p_pow"], 1)
                pool.wait_ge(s["p_pow"], base + 5)
                pool.tensor_tensor(cim, cim, ctmp[:, :, :], ALU.add).then_inc(s["p_pow"], 1)
                pool.wait_ge(s["p_pow"], base + 6)
                pool.tensor_copy(ctmp[:, 0, 0:1], ident[:, 0:1]).then_inc(s["p_coef"], 1)

            pool.wait_ge(s["t_mm"], HALVES * NHB)
            pool.wait_ge(s["m_tok"], 16 * 2 * NB * HALVES)
            for part in (q_hi, q_lo):
                pool.memset(part[:, :, :].bitcast(F32), 0.0).then_inc(s["c_zero"], 1)
            pool.memset(mhalf[:, :], -0.5).then_inc(s["c_ones"], 1)
            pool.memset(ones[:, :, :], 1.0).then_inc(s["c_fix"], 1)
            pool.memset(mask[:, :, :], 1.0).then_inc(s["c_fix"], 1)
            pool.memset(pclsT[:, :], 0.0).then_inc(s["c_fix"], 1)
            pool.memset(pccT[:, :], 0.0).then_inc(s["c_fix"], 1)
            pool.memset(e16[:, :], 0.0).then_inc(s["c_fix"], 1)
            pool.memset(u_sb[:, :], 0.0).then_inc(s["c_fix"], 1)
            pool.wait_ge(s["c_fix"], 6)
            pool.affine_select(out=mask[:, :, :], in_=mask[:, :, :], compare_op=ALU.is_ge, fill=0.0, base=0,
                               pattern=[[P, KC], [-DH, P]], channel_multiplier=1).then_inc(s["p_mask"], 1)
            for t, n in ((pclsT, BODY), (pccT, P)):
                pool.affine_select(out=t[:, :], in_=t[:, :], compare_op=ALU.not_equal, fill=1.0, base=-NHEAD,
                                   pattern=[[0, n]], channel_multiplier=1).then_inc(s["c_ones"], 1)
            pool.memset(e16[:, NHEAD:NHEAD + 1], 1.0).then_inc(s["c_ones"], 1)
            pool.wait_ge(s["p_mask"], 1)
            pool.affine_select(out=mask[:, :, :], in_=mask[:, :, :], compare_op=ALU.is_ge, fill=0.0, base=DH - 1,
                               pattern=[[-P, KC], [DH, P]], channel_multiplier=-1).then_inc(s["c_mask"], 1)

            def ln_pow(n):
                pool.wait_ge(s["d_ln"], n * 5 + 5)
                pool.tensor_tensor(lnr[:, 1, :], lnr[:, 0, :], mhalf[:, :], ALU.pow).then_inc(s["p_pow"], 1)

            ln_pow(0)
            ln_pow(1)

            def keep_cls(c, j):
                pool.wait_ge(s["d_norm"], c * NHEAD + j + 1)
                column = prb[:, j % 4, :, BODY]
                pool.tensor_tensor(pcls[:, :, j], column, ones[:, :, 0], ALU.mult).then_inc(s["p_pc"], 1)

            def cls_cols(c, gr):
                if gr == 0:
                    pool.wait_ge(s["d_ptc"], c + 1)
                column = ptc[:, :, gr * HPC:(gr + 1) * HPC].rearrange("p t h -> p h t")
                pool.tensor_tensor(pts[:, (gr * HPC) % 8:(gr * HPC) % 8 + HPC, :, BODY], column, ones[:, :, :].rearrange("p t h -> p h t"), ALU.mult
                                   ).then_inc(s["p_ptc"], 1)

            def body(c, first, last):
                for j in range(NHEAD):
                    if j == 1:
                        if not first:
                            pool.wait_ge(s["t_tck"], c)
                    if j >= 1:
                        keep_cls(c, j - 1)
                    if j == 4:
                        if not first:
                            pool.wait_ge(s["t_pv"], c * KC)
                        cls_cols(c, 0)
                        cls_cols(c, 1)
                        if not last:
                            ln_pow(c + 2)
                    if j == 11:
                        pool.wait_ge(s["t_pv"], c * KC + 1)
                        cls_cols(c, 2)
                    if j == 15:
                        pool.wait_ge(s["t_pv"], c * KC + 2)
                        cls_cols(c, 3)
                keep_cls(c, NHEAD - 1)

            body(0, True, False)
            with pool.Fori(1, NB - 1) as c:
                body(c, False, False)
            body(NB - 1, False, True)
            pool.wait_ge(s["d_fin"], 1)
            pool.memset(mh2[:, :], -0.5).then_inc(s["p_const"], 1)
            pool.iota(iota[:, :], pattern=[[1, NE]], base=0, channel_multiplier=0,
                      allow_small_or_imprecise_dtypes=True).then_inc(s["p_const"], 1)
            pool.wait_ge(s["p_const"], 2)
            pool.wait_ge(s["ld_bias"], 32)
            with pool.Fori(0, TILES + 1) as t:
                pool.wait_ge(s["d_ln2"], t * 3 + 3)
                pool.tensor_tensor(rs2[:, 1:2], rs2[:, 0:1], mh2[:, :], ALU.pow).then_inc(s["p_rstd"], 1)
                pool.wait_ge(s["d_xn"], t + 1)
                pool.tensor_tensor(tok[:, t, :], tok[:, t, :], ob[:, :], ALU.add).then_inc(s["p_outb"], 1)

        @block.scalar
        def _(act):
            act.wait_ge(s["ld_par"], 64)
            act.activation(prm[:, 0, :, :], iar[:, :, :], ACT.Exp).then_inc(s["a_exp"], 1)
            act.activation(dt2[:, 0, :], ldt[:, :], ACT.Exp).then_inc(s["a_exp"], 1)
            act.wait_ge(s["d_rot"], 2)
            act.activation(k_scale[:, :], rcol[:, 2, :], ACT.Sin).then_inc(s["a_sin"], 1)
            act.activation(rcol[:, 0, :], rcol[:, 3, :], ACT.Sin).then_inc(s["a_sin"], 1)

            def w_scale(raw, scale):
                for o in range(KC):
                    act.activation(raw[:, o, :], raw[:, o, :], ACT.Copy, scale=scale[:, o:o + 1]
                                   ).then_inc(s["a_wsc"], 1)

            def w_hi(dst, sem_hi, sem_t, n, bank0):
                for ic in range(KC):
                    act.wait_ge(s[sem_t], n * KC + ic + 1)
                    act.activation(dst[:, ic, :], ps[:, bank0 + ic, :], ACT.Copy).then_inc(s[sem_hi], 1)

            act.wait_ge(s["ld_w0"], 16)
            act.wait_ge(s["d_rot"], 5)
            w_scale(w_raw[:, 0], q_scale)
            w_hi(wqT_hi, "a_whi", "t_w", 0, 4)
            act.wait_ge(s["ld_w1"], 16)
            w_scale(w_raw[:, 1], k_scale)
            w_hi(wkT_hi, "a_whi", "t_w", 1, 4)

            def turned(n, dst, col):
                act.wait_ge(s["t_tr"], n + 1)
                act.activation(dst[:, :, col:col + 4], ps[:, n % 4, :].rearrange("p (q h) -> p h q", q=4),
                               ACT.Copy).then_inc(s["a_tr"], 1)

            for hf in range(HALVES):
                base = hf * 32
                if hf == 1:
                    act.wait_ge(s["t_mm"], NHB)
                for q in range(16):
                    turned(base + q, rT, 4 * q)
                for c in range(NB):
                    for k in range(2):
                        turned(base + 16 + 2 * c + k, lT, c * NA + 4 * k)
                for hb in range(NHB):
                    n = hf * NHB + hb
                    act.wait_ge(s["t_mm"], n + 1)
                    if n >= 2:
                        act.wait_ge(s_row[n % 2], 16 * (n // 2))
                    for k in range(2):
                        e = act.activation(so[:, n % 2, k * BANK:(k + 1) * BANK], ps[:, 4 + 2 * (n % 2) + k, :], ACT.Copy)
                    e.then_inc(s["a_so"], 1)

            def hi_xT(n, bank, st):
                act.wait_ge(s["t_x"], n + 1)
                act.activation(xT_hi[:, :, st * P:st * P + P], ps[:, bank, :].rearrange("p (k t) -> p k t", k=KC),
                               ACT.Copy).then_inc(s["a_hiT"], 1)

            act.wait_ge(s["t_x"], 1)
            act.activation(xT_hi[:, :, BODY:KPAD], ps[:, 7, 0:KC * NB].rearrange("p (k t) -> p k t", k=KC)[:, :, 0:2],
                           ACT.Copy).then_inc(s["a_hiT"], 1)
            hi_xT(1, 6, 0)
            hi_xT(2, 7, 1)

            def hi_qk(c, m, first=False):
                ci, bank = m // 2, 6 + m % 2
                act.wait_ge(s["t_qk"], c * 2 * KC + m + 1)
                if m % 2 == 0:
                    for j in range(HPC):
                        rows = slice(j * DH, (j + 1) * DH)
                        e = act.activation(q_hi[rows, ci * HPC + j, :], ps[rows, bank, 0:BODY], ACT.Identity,
                                           bias=q_bias[rows, ci:ci + 1])
                    if first:
                        e = act.activation(qcls_hi[:, ci, :], ps[:, bank, BODY:KPAD], ACT.Identity,
                                           bias=q_bias[:, ci:ci + 1])
                else:
                    e = act.activation(k_hi[:, ci, :], ps[:, bank, 0:KPAD], ACT.Identity, bias=k_bias[:, ci:ci + 1])
                e.then_inc(s["a_hiqk"], 1)

            act.wait_ge(s["c_zero"], 2)
            for m in range(2 * KC):
                hi_qk(0, m, True)
            for i, dst in enumerate((wvT_hi, woT_hi)):
                w_hi(dst, "a_wvhi", "t_wv", i, 0)

            def exp_unit(c, j):
                act.wait_ge(s["d_max"], c * NHEAD + j + 1)
                for st in range(HALVES):
                    e = act.activation(prb[:, j % 4, st, 0:KEYS], ps[:, 2 * (j % 2) + st, 0:KEYS], ACT.Exp,
                                       bias=negmax[:, j % 4, st:st + 1], accum_out=rowsum[:, j % 4, st:st + 1])
                e.then_inc(s["a_exps"], 1)

            def keep_pt(c, j):
                act.wait_ge(s["t_tp"], c * NHEAD + j + 1)
                act.activation(pts[:, j % 8, :, 0:BODY], ps[:, 4, :].rearrange("p (t s) -> p t s", t=2),
                               ACT.Copy).then_inc(s["a_pt"], 1)

            def keep_v(c, st):
                act.wait_ge(s["t_v"], c * HALVES + st + 1)
                act.activation(v_sb[:, st, :], ps[:, 7, :], ACT.Copy).then_inc(s["a_v"], 1)

            def hi_ot(c, gr):
                act.wait_ge(s["t_pv"], c * KC + gr + 1)
                act.activation(oT_hi[:, gr, :], ps[:, 5, 0:BODY], ACT.Copy).then_inc(s["a_ot"], 1)

            def body(c, first, last):
                for j in range(NHEAD):
                    if j >= 4 or not first:
                        act.wait_ge(s["t_tp"], c * NHEAD + j - 3)
                        act.wait_ge(s["p_pc"], c * NHEAD + j - 3)
                    for m in QK_SLOT[j - 1] if j >= 1 and not last else ():
                        hi_qk(c + 1, m)
                    for m in QK_SLOT[NHEAD - 1] if j == 0 and not first else ():
                        hi_qk(c, m)
                    if j == 3 and not first:
                        hi_ot(c - 1, 3)
                    if j == 4:
                        keep_v(c, 1)
                    if j in (7, 11, 15):
                        if j == 7 and not first:
                            act.wait_ge(s["t_op"], c * HALVES)
                        hi_ot(c, (j - 7) // 4)
                    if j == 8 and not last:
                        act.wait_ge(s["t_v"], (c + 1) * HALVES)
                        hi_xT((c + 1) * HALVES + 1, 6, 0)
                        hi_xT((c + 1) * HALVES + 2, 7, 1)
                    exp_unit(c, j)
                    if j >= 2:
                        if j == 2 and not first:
                            act.wait_ge(s["t_pv"], c * KC - 1)
                        if j == 10:
                            act.wait_ge(s["t_pv"], c * KC + 1)
                        if j == 14:
                            act.wait_ge(s["t_pv"], c * KC + 2)
                        keep_pt(c, j - 2)
                    elif not first:
                        keep_pt(c - 1, NHEAD - 2 + j)
                    if j == 1:
                        act.wait_ge(s["d_scm"], c + 1)
                        act.activation(pc[:, 0:KEYS], ps[0:NHEAD, 6, 0:KEYS], ACT.Exp, bias=cstat[:, 0:1],
                                       accum_out=cstat[:, 1:2]).then_inc(s["a_expc"], 1)
                    if j == 2:
                        if not first:
                            act.wait_ge(s["t_pv"], c * KC)
                        keep_v(c, 0)


            body(0, True, False)
            with act.Fori(1, NB - 1) as c:
                body(c, False, False)
            body(NB - 1, False, True)
            last = NB - 1
            keep_pt(last, NHEAD - 2)
            keep_pt(last, NHEAD - 1)
            hi_ot(last, 3)
            act.wait_ge(s["d_fin"], 1)
            act.wait_ge(s["ld_router"], 32)
            act.activation(rw_hi[:, :, :], rw[:, :, :], ACT.Copy).then_inc(s["a_rwhi"], 1)

            def hi_xn(t):
                act.wait_ge(s["t_xn"], t + 1)
                act.activation(xnT_hi[:, :, :], ps[:, 4, :].rearrange("p (k t) -> p k t", k=KC), ACT.Copy
                               ).then_inc(s["a_hixn"], 1)

            def route_exp(t):
                act.wait_ge(s["d_route"], t * 8 + 2)
                act.activation(probs[:, :], lg[:, :], ACT.Exp, bias=rstat[:, 0:1], accum_out=rstat[:, 1:2]
                               ).then_inc(s["a_rexp"], 1)

            def hi_expert(e):
                act.wait_ge(ld_ew[e], 16)
                act.activation(ew_hi[:, e, :, :], ew[:, e, :, :], ACT.Copy).then_inc(s["a_ewhi"], 1)

            def gelu(t, e, first):
                act.wait_ge(s["d_pre"], t * NE + e + 1)
                if e >= 2 or not first:
                    act.wait_ge(s["d_comb"], t * NE + e - 1)
                act.activation(act_out[:, e % 2, :], ps[:, e % 4, :], ACT.Gelu_apprx_tanh).then_inc(s["a_gelu"], 1)

            def tile(t, first, last):
                for e in range(NE):
                    if first and e < NE // 2:
                        hi_expert(e + NE // 2)
                    if e == NE - 1 and not last:
                        act.wait_ge(s["t_expert"], (t + 1) * NE)
                        hi_xn(t + 1)
                    gelu(t, e, first)
                act.wait_ge(s["t_comb"], t + 1)
                if not first:
                    act.wait_ge(s["t_out"], t)
                act.activation(combT[:, :, :], ps[:, 5, :].rearrange("p (k t) -> p k t", k=KC), ACT.Copy
                               ).then_inc(s["a_combT"], 1)
                if not last:
                    route_exp(t + 1)

            hi_xn(0)
            route_exp(0)
            for e in range(NE // 2):
                hi_expert(e)
            tile(0, True, False)
            with act.Fori(1, TILES) as t:
                tile(t, False, False)
            tile(TILES, False, True)

        @block.vector
        def _(dve):
            n_par = [0]

            def link(ins):
                n_par[0] += 1
                ins.then_inc(s["d_par"], 1)
                dve.wait_ge(s["d_par"], n_par[0])

            dve.wait_ge(s["ld_rot"], 16 * (4 + HPC))
            for i, (dst, shift) in enumerate(((2, 0.0), (3, 0.25))):
                t = prm[:, 7, 0, i * 16:i * 16 + KC]
                link(dve.tensor_scalar(t, rcol[:, 0, :], 1.0 / (TWO_PI_HI + TWO_PI_LO), shift, ALU.mult, ALU.add))
                link(dve.tensor_scalar(t, t, ROUND_MAGIC, ROUND_MAGIC, ALU.add, ALU.subtract))
                link(dve.scalar_tensor_tensor(out=rcol[:, dst, :], in0=t, scalar=-TWO_PI_HI, in1=rcol[:, 0, :],
                                              op0=ALU.mult, op1=ALU.add))
                link(dve.scalar_tensor_tensor(out=rcol[:, dst, :], in0=t, scalar=-TWO_PI_LO, in1=rcol[:, dst, :],
                                              op0=ALU.mult, op1=ALU.add))
                link(dve.tensor_scalar(rcol[:, dst, :], rcol[:, dst, :], 4 * shift * 1.5707963267948966, None, ALU.add))
                dve.tensor_scalar(rcol[:, dst, :], rcol[:, dst, :], PI_SAFE, -PI_SAFE, ALU.min, ALU.max
                                  ).then_inc(s["d_rot"], 1)
            dve.wait_ge(s["a_sin"], 2)
            link(dve.scalar_tensor_tensor(out=q_scale[:, :], in0=rcol[:, 0, :], scalar=float(DH) ** -0.5,
                                          in1=rcol[:, 1, :], op0=ALU.mult, op1=ALU.mult))
            dve.tensor_tensor(q_bias[:, :], q_bias[:, :], q_scale[:, :], ALU.mult).then_inc(s["d_rot"], 1)
            dve.tensor_tensor(k_bias[:, :], k_bias[:, :], k_scale[:, :], ALU.mult).then_inc(s["d_rot"], 1)
            dve.memset(prm[:, 7, 1, 0:1], 0.0).then_inc(s["d_rot"], 1)

            dve.wait_ge(s["a_exp"], 2)
            link(dve.tensor_scalar(dt2[:, 1, :], dt2[:, 0, :], 0.5, None, ALU.mult))
            e_, q1, v_, inv, t0, t1, om = (prm[:, i, :, :] for i in range(7))
            for hf in range(HALVES):
                dve.tensor_scalar(e_[:, hf, :], e_[:, hf, :], dt2[:, 1, hf:hf + 1], None, ALU.mult).then_inc(s["d_par"], 1)
                dve.tensor_scalar(v_[:, hf, :], aim[:, hf, :], dt2[:, 1, hf:hf + 1], None, ALU.mult).then_inc(s["d_par"], 1)
            n_par[0] += 4
            dve.wait_ge(s["d_par"], n_par[0])
            link(dve.tensor_scalar(q1, e_, 1.0, None, ALU.add))
            link(dve.tensor_scalar(om, e_, -1.0, 1.0, ALU.mult, ALU.add))
            link(dve.tensor_tensor(t0, v_, v_, ALU.mult))
            link(dve.tensor_tensor(t1, q1, q1, ALU.mult))
            link(dve.tensor_tensor(t1, t1, t0, ALU.add))
            link(dve.reciprocal(inv, t1))
            link(dve.tensor_tensor(t1, om, q1, ALU.mult))
            link(dve.tensor_tensor(t1, t1, t0, ALU.subtract))
            link(dve.tensor_tensor(e_, t1, inv, ALU.mult))
            link(dve.scalar_tensor_tensor(out=om, in0=v_, scalar=2.0, in1=inv, op0=ALU.mult, op1=ALU.mult))
            br, bi = b_in[:, :, :, 0], b_in[:, :, :, 1]
            for hf in range(HALVES):
                link(dve.tensor_scalar(inv[:, hf, :], inv[:, hf, :], dt2[:, 0, hf:hf + 1], 2.0, ALU.mult, ALU.mult))
            link(dve.tensor_tensor(t0, br, q1, ALU.mult))
            link(dve.tensor_tensor(t1, bi, v_, ALU.mult))
            link(dve.tensor_tensor(t0, t0, t1, ALU.subtract))
            link(dve.tensor_tensor(g[:, :, 0, :], t0, inv, ALU.mult))
            link(dve.tensor_tensor(t0, br, v_, ALU.mult))
            link(dve.tensor_tensor(t1, bi, q1, ALU.mult))
            link(dve.tensor_tensor(t0, t0, t1, ALU.add))
            dve.tensor_tensor(g[:, :, 1, :], t0, inv, ALU.mult).then_inc(s["d_coef"], 1)

            def w_lo(dst, hi, sem_hi, sem_lo, n, bank0):
                for ic in range(KC):
                    dve.wait_ge(s[sem_hi], n * KC + ic + 1)
                    dve.tensor_tensor(dst[:, ic, :], ps[:, bank0 + ic, :], hi[:, ic, :].bitcast(F32), ALU.subtract
                                      ).then_inc(s[sem_lo], 1)

            n_pow = [0]

            def step(ins):
                n_pow[0] += 1
                ins.then_inc(s["d_pow"], 1)
                dve.wait_ge(s["d_pow"], n_pow[0])

            for hf in range(HALVES):
                step(dve.tensor_copy(zs[:, 0, 0, :], e_[:, hf, :]))
                step(dve.tensor_copy(zs[:, 0, 1, :], om[:, hf, :]))
                for k in range(9):
                    zr, zi = zs[:, k, 0, :], zs[:, k, 1, :]
                    if k < 8:
                        step(dve.tensor_tensor(t0[:, 0, :], zr, zr, ALU.mult))
                        step(dve.tensor_tensor(t1[:, 0, :], zi, zi, ALU.mult))
                        step(dve.scalar_tensor_tensor(out=zs[:, k + 1, 1, :], in0=zr, scalar=2.0, in1=zi,
                                                      op0=ALU.mult, op1=ALU.mult))
                        step(dve.tensor_tensor(zs[:, k + 1, 0, :], t0[:, 0, :], t1[:, 0, :], ALU.subtract))
                    step(dve.tensor_scalar(zt[:, k, 0, :], zi, -1.0, None, ALU.mult))
                    step(dve.tensor_copy(zt[:, k, 1, :], zr))
                if hf == 0:
                    w_lo(wqT_lo, wqT_hi, "a_whi", "d_wlo", 0, 4)
                else:
                    dve.wait_ge(s["t_tr"], 32)

                def doubled(dst, n, k, tmp):
                    shape = [P, n, 2, NS]
                    step(dve.tensor_tensor(dst[:, n:2 * n], bc(dst[:, 0:n, 0:1, :], shape),
                                           bc(zs[:, k, :, :].unsqueeze(1), shape), ALU.mult))
                    step(dve.tensor_tensor(tmp, bc(dst[:, 0:n, 1:2, :], shape),
                                           bc(zt[:, k, :, :].unsqueeze(1), shape), ALU.mult))
                    step(dve.tensor_tensor(dst[:, n:2 * n], dst[:, n:2 * n], tmp, ALU.add))

                ring_flat = ring[:, 0, :, :, :, :].rearrange("p a b s n -> p (a b) s n")
                for dst, k0, levels in ((r_low, 0, 5), (w_pow, 6, 3)):
                    step(dve.memset(dst[:, 0, 0, :], 1.0))
                    step(dve.memset(dst[:, 0, 1, :], 0.0))
                    step(dve.tensor_copy(dst[:, 1, :, :], zs[:, k0, :, :]))
                    for lv in range(1, levels):
                        doubled(dst, 1 << lv, k0 + lv, ring_flat[:, 0:1 << lv])
                    if dst is r_low:
                        dve.memset(t0[:, 0, 0:1], 0.0).then_inc(s["d_rl"], 1)
                step(dve.tensor_scalar(w_b[:, :, 0, :], w_pow[:, :, 1, :], -1.0, None, ALU.mult))
                step(dve.tensor_scalar(w_b[:, :, 1, :], w_pow[:, :, 0, :], -1.0, None, ALU.mult))
                step(dve.tensor_scalar(w_pow[:, :, 1, :], w_pow[:, :, 1, :], -1.0, None, ALU.mult))
                shape = [P, PIECE, 2, NS]
                for q in range(4):
                    n = hf * 12 + q
                    if q >= 2:
                        dve.wait_ge(s["t_tr"], hf * 32 + 8 + 2 * (q - 1))
                    dve.tensor_tensor(ring[:, n % 2, 0], bc(r_low[:, 8 * q:8 * q + 8, 0:1, :], shape),
                                      bc(zs[:, 5, :, :].unsqueeze(1), shape), ALU.mult)
                    dve.tensor_tensor(ring[:, n % 2, 1], bc(r_low[:, 8 * q:8 * q + 8, 1:2, :], shape),
                                      bc(zt[:, 5, :, :].unsqueeze(1), shape), ALU.mult).then_inc(s["d_up"], 1)
                dve.wait_ge(s["p_coef"], hf + 1)
                for c in range(NB):
                    n = hf * 12 + 4 + c
                    dve.wait_ge(s["t_tr"], hf * 32 + 8 + 2 * (4 + c - 1))
                    dve.tensor_tensor(ring[:, n % 2, 0], bc(coef[:, c, 0:1, :].unsqueeze(1), shape), w_pow[:, :, :, :],
                                      ALU.mult)
                    dve.tensor_tensor(ring[:, n % 2, 1], bc(coef[:, c, 1:2, :].unsqueeze(1), shape), w_b[:, :, :, :],
                                      ALU.mult).then_inc(s["d_lp"], 1)
                if hf == 0:
                    w_lo(wkT_lo, wkT_hi, "a_whi", "d_wlo", 1, 4)
            dve.wait_ge(s["m_tok"], 16 * 2 * NB * HALVES)
            dve.wait_ge(s["t_mm"], HALVES * NHB)

            def ln(n, tiles, rows):
                for i, t in enumerate(tiles):
                    dve.bn_stats(lnst[0:rows, i, :], tok[0:rows, t, :]).then_inc(s["d_ln"], 1)
                for i in range(2):
                    dve.wait_ge(s["d_ln"], n * 5 + 2)
                    dve.bn_aggr(lnmv[0:rows, i, :], lnst[0:rows, i, :]).then_inc(s["d_ln"], 1)
                dve.wait_ge(s["d_ln"], n * 5 + 4)
                dve.tensor_scalar(lnr[0:rows, 0, :], lnmv[0:rows, :, 1], EPS, None, ALU.add).then_inc(s["d_ln"], 1)

            def ln_apply(n, tiles, rows):
                dve.wait_ge(s["p_pow"], 12 + n + 1)
                for i, t in enumerate(tiles):
                    dve.tensor_scalar(xhat[0:rows, i, :], tok[0:rows, t, :], lnmv[0:rows, i, 0:1],
                                      lnr[0:rows, 1, i:i + 1], ALU.subtract, ALU.mult).then_inc(s["d_x"], 1)

            dve.wait_ge(s["ld_cls"], 16)
            dve.memset(lnr[:, 0, :], 1.0).then_inc(s["d_qb"], 1)
            dve.wait_ge(s["d_qb"], 1)
            ln(0, (CLS, CLS), NB)
            ln_apply(0, (CLS, CLS), NB)
            dve.wait_ge(s["t_x"], 1)
            ln(1, (0, 1), P)
            ln_apply(1, (0, 1), P)

            def lo_xT(n, bank, st):
                dve.wait_ge(s["a_hiT"], n + 1)
                dve.tensor_tensor(xT_lo[:, :, st * P:st * P + P], ps[:, bank, :].rearrange("p (k t) -> p k t", k=KC),
                                  xT_hi[:, :, st * P:st * P + P].bitcast(F32), ALU.subtract).then_inc(s["d_loT"], 1)

            dve.wait_ge(s["a_hiT"], 1)
            dve.tensor_tensor(xT_lo[:, :, BODY:KPAD],
                              ps[:, 7, 0:KC * NB].rearrange("p (k t) -> p k t", k=KC)[:, :, 0:2],
                              xT_hi[:, :, BODY:KPAD].bitcast(F32), ALU.subtract).then_inc(s["d_loT"], 1)
            lo_xT(1, 6, 0)
            lo_xT(2, 7, 1)

            def lo_qk(c, m, first=False):
                ci, bank = m // 2, 6 + m % 2
                dve.wait_ge(s["a_hiqk"], c * 2 * KC + m + 1)

                def low(dst, src, bias, hi):
                    return dve.scalar_tensor_tensor(out=dst, in0=src, scalar=bias, in1=hi.bitcast(F32),
                                                    op0=ALU.add, op1=ALU.subtract)
                if m % 2 == 0:
                    for j in range(HPC):
                        rows, h = slice(j * DH, (j + 1) * DH), ci * HPC + j
                        e = low(q_lo[rows, h, :], ps[rows, bank, 0:BODY], q_bias[rows, ci:ci + 1], q_hi[rows, h, :])
                    if first:
                        e = low(qcls_lo[:, ci, :], ps[:, bank, BODY:KPAD], q_bias[:, ci:ci + 1], qcls_hi[:, ci, :])
                else:
                    e = low(k_lo[:, ci, :], ps[:, bank, 0:KPAD], k_bias[:, ci:ci + 1], k_hi[:, ci, :])
                e.then_inc(s["d_loqk"], 1)

            for m in range(2 * KC):
                lo_qk(0, m, True)
            dve.wait_ge(s["c_mask"], 1)
            dve.wait_ge(s["d_loqk"], 2 * KC)
            for ci in range(KC):
                dve.tensor_scalar(qblk_hi[:, ci, :], mask[:, ci, :], qcls_hi[:, ci, 0:1].bitcast(F32), None,
                                  ALU.mult).then_inc(s["d_qb"], 1)
                dve.tensor_scalar(qblk_lo[:, ci, :], mask[:, ci, :], qcls_lo[:, ci, 0:1].bitcast(F32), None,
                                  ALU.mult).then_inc(s["d_qb"], 1)
            for i, (dst, hi) in enumerate(((wvT_lo, wvT_hi), (woT_lo, woT_hi))):
                w_lo(dst, hi, "a_wvhi", "d_wvlo", i, 0)
            dve.wait_ge(s["t_vb"], 1)
            for ci in range(KC):
                dve.tensor_scalar(vblk[:, ci, :], mask[:, ci, 0:32], ps[:, 4, 2 * ci:2 * ci + 1], None, ALU.mult
                                  ).then_inc(s["d_vb"], 1)
            dve.wait_ge(s["d_vb"], KC)
            dve.tensor_copy(vblk[:, :, NHEAD:NHEAD + 1], bv_col[:, :].unsqueeze(2)).then_inc(s["d_vb"], 1)
            dve.wait_ge(s["t_u"], 1)
            dve.wait_ge(s["c_fix"], 6)
            dve.tensor_copy(u_sb[0:32, :], ps[0:32, 5, :]).then_inc(s["d_u"], 1)
            dve.wait_ge(s["c_ones"], 4)

            def top(c, j):
                dve.wait_ge(s["t_s"], c * NHEAD + j + 1)
                dve.tensor_reduce(negmax[:, j % 4, :], ps[:, 2 * (j % 2):2 * (j % 2) + 2, 0:KEYS], AX_X, ALU.max,
                                  negate=True).then_inc(s["d_max"], 1)

            def norm(c, j):
                dve.wait_ge(s["a_exps"], c * NHEAD + j + 1)
                dve.reciprocal(rrec[:, j % 4, :], rowsum[:, j % 4, :]).then_inc(s["d_rc"], 1)
                dve.wait_ge(s["d_rc"], c * NHEAD + j + 1)
                for st in range(HALVES):
                    e = dve.tensor_scalar(prb[:, j % 4, st, 0:KEYS], prb[:, j % 4, st, 0:KEYS],
                                          rrec[:, j % 4, st:st + 1], None, ALU.mult)
                e.then_inc(s["d_norm"], 1)

            def lo_ot(c, gr):
                dve.wait_ge(s["a_ot"], c * KC + gr + 1)
                dve.tensor_tensor(oT_lo[:, gr, :], ps[:, 5, 0:BODY], oT_hi[:, gr, :].bitcast(F32), ALU.subtract)
                dve.tensor_copy(ocls[:, gr, bass.ds(c, 1)], ps[:, 5, BODY:BODY + 1]).then_inc(s["d_ot"], 1)

            def residual(c, st, bank):
                dve.wait_ge(s["t_op"], c * HALVES + st + 1)
                t = tok[:, c * HALVES + st, :]
                dve.tensor_tensor(t, ps[:, bank, :], t, ALU.add).then_inc(s["d_res"], 1)

            def tck_copy(c):
                dve.wait_ge(s["t_tck"], c + 1)
                dve.tensor_copy(pclsT[0:NHEAD, :], ps[0:NHEAD, 4, 0:BODY]).then_inc(s["d_tck"], 1)

            def body(c, first, last):
                for j in range(NHEAD):
                    top(c, j)
                    if j >= 1:
                        norm(c, j - 1)
                    elif not first:
                        norm(c - 1, NHEAD - 1)
                        for m in QK_SLOT[NHEAD - 1]:
                            lo_qk(c, m)
                    if j == 1:
                        dve.wait_ge(s["t_sc"], c + 1)
                        dve.tensor_reduce(cstat[:, 0:1], ps[0:NHEAD, 6, 0:KEYS], AX_X, ALU.max, negate=True
                                          ).then_inc(s["d_scm"], 1)
                    if j == 2:
                        dve.wait_ge(s["a_expc"], c + 1)
                        dve.reciprocal(cstat[:, 2:3], cstat[:, 1:2]).then_inc(s["d_scn"], 1)
                        dve.wait_ge(s["d_scn"], 3 * c + 1)
                        dve.tensor_scalar(pc[:, 0:KEYS], pc[:, 0:KEYS], cstat[:, 2:3], None, ALU.mult
                                          ).then_inc(s["d_scn"], 1)
                        dve.wait_ge(s["d_scn"], 3 * c + 2)
                        dve.tensor_copy(pccT[0:NHEAD, bass.ds(c, 1)], pc[:, BODY:BODY + 1]).then_inc(s["d_scn"], 1)
                    if j == 2 and not first:
                        if True:
                            dve.wait_ge(s["t_op"], (c - 1) * HALVES)
                        tck_copy(c - 1)
                    if j == 3:
                        if not first:
                            lo_ot(c - 1, 3)
                        if not last:
                            for i in range(2):
                                dve.bn_stats(lnst[:, i, :], tok[:, (c + 1) * HALVES + i, :]).then_inc(s["d_ln"], 1)
                        dve.wait_ge(s["t_tc"], c + 1)
                        if not first:
                            dve.wait_ge(s["p_ptc"], c * KC)
                        if not last:
                            dve.wait_ge(s["d_ln"], c * 5 + 12)
                        dve.tensor_copy(ptc[:, :, :], ps[:, 6, 0:2 * NHEAD].rearrange("p (t h) -> p t h", t=2)
                                        ).then_inc(s["d_ptc"], 1)
                        if not last:
                            for i in range(2):
                                dve.bn_aggr(lnmv[:, i, :], lnst[:, i, :]).then_inc(s["d_ln"], 1)
                            dve.wait_ge(s["d_ln"], c * 5 + 14)
                            dve.tensor_scalar(lnr[:, 0, :], lnmv[:, :, 1], EPS, None, ALU.add).then_inc(s["d_ln"], 1)
                    if j == 5:
                        if not first:
                            residual(c - 1, 0, 6)
                        if not last:
                            dve.wait_ge(s["p_pow"], c + 15)
                            for i in range(2):
                                dve.tensor_scalar(xhat[:, i, :],
                                                  tok[:, (c + 1) * HALVES + i, :],
                                                  lnmv[:, i, 0:1], lnr[:, 1, i:i + 1], ALU.subtract, ALU.mult
                                                  ).then_inc(s["d_x"], 1)
                    if j == 6 and not first:
                        residual(c - 1, 1, 7)
                    if j == 8 and not last:
                        lo_xT((c + 1) * HALVES + 1, 6, 0)
                        lo_xT((c + 1) * HALVES + 2, 7, 1)
                    if j in (7, 11, 15):
                        lo_ot(c, (j - 7) // 4)
                    for m in QK_SLOT[j - 1] if j >= 1 and not last else ():
                        lo_qk(c + 1, m)

            body(0, True, False)
            with dve.Fori(1, NB - 1) as c:
                body(c, False, False)
            body(NB - 1, False, True)
            last = NB - 1
            norm(last, NHEAD - 1)
            dve.wait_ge(s["t_op"], last * HALVES)
            tck_copy(last)
            lo_ot(last, 3)
            dve.wait_ge(s["d_ot"], NB * KC)
            dve.wait_ge(s["t_sc"], NB)
            dve.memset(oc_hi[:, :, NB:P].bitcast(F32), 0.0).then_inc(s["d_qb"], 1)
            dve.memset(oc_lo[:, :, NB:P].bitcast(F32), 0.0).then_inc(s["d_qb"], 1)
            dve.tensor_copy(oc_hi[:, :, 0:NB], ocls[:, :, :]).then_inc(s["d_qb"], 1)
            dve.wait_ge(s["d_qb"], 12)
            dve.tensor_tensor(oc_lo[:, :, 0:NB], ocls[:, :, :], oc_hi[:, :, 0:NB].bitcast(F32), ALU.subtract
                              ).then_inc(s["d_qb"], 1)
            residual(last, 0, 6)
            residual(last, 1, 7)
            dve.wait_ge(s["t_fin"], 1)
            dve.tensor_tensor(tok[0:NB, CLS, :], ps[0:NB, 6, :], tok[0:NB, CLS, :], ALU.add).then_inc(s["d_fin"], 1)
            dve.wait_ge(s["d_fin"], 1)
            def stats(t):
                dve.bn_stats(st2[:, :], tok[:, t, :]).then_inc(s["d_ln2"], 1)

            def variance(t):
                dve.bn_aggr(mv2[:, :], st2[:, :]).then_inc(s["d_ln2"], 1)
                dve.wait_ge(s["d_ln2"], t * 3 + 2)
                dve.tensor_scalar(rs2[:, 0:1], mv2[:, 1:2], EPS, None, ALU.add).then_inc(s["d_ln2"], 1)

            def normalise(t):
                dve.wait_ge(s["p_rstd"], t + 1)
                dve.tensor_scalar(xn[:, :], tok[:, t, :], mv2[:, 0:1], rs2[:, 1:2], ALU.subtract, ALU.mult
                                  ).then_inc(s["d_xn"], 1)

            def lo_xn(t):
                dve.wait_ge(s["a_hixn"], t + 1)
                dve.tensor_tensor(xnT_lo[:, :, :], ps[:, 4, :].rearrange("p (k t) -> p k t", k=KC),
                                  xnT_hi[:, :, :].bitcast(F32), ALU.subtract).then_inc(s["d_loxn"], 1)

            def residual_out(t):
                dve.wait_ge(s["t_out"], t + 1)
                dve.wait_ge(s["p_outb"], t + 1)
                dve.tensor_tensor(tok[:, t, :], ps[:, 6, :], tok[:, t, :], ALU.add).then_inc(s["d_out"], 1)

            def route(t, finish):
                n = t * 8
                dve.wait_ge(s["t_router"], t + 1)
                dve.tensor_tensor(lg[:, :], ps[:, 7, 0:NE], rb[:, :], ALU.add).then_inc(s["d_route"], 1)
                dve.wait_ge(s["d_route"], n + 1)
                dve.tensor_reduce(rstat[:, 0:1], lg[:, :], AX_X, ALU.max, negate=True).then_inc(s["d_route"], 1)
                dve.wait_ge(s["a_rexp"], t + 1)
                dve.reciprocal(rstat[:, 2:3], rstat[:, 1:2]).then_inc(s["d_route"], 1)
                dve.wait_ge(s["d_route"], n + 3)
                dve.tensor_scalar(probs[:, :], probs[:, :], rstat[:, 2:3], None, ALU.mult).then_inc(s["d_route"], 1)
                dve.wait_ge(s["d_route"], n + 4)
                finish()
                dve.max(top8[:, :], probs[:, :]).then_inc(s["d_route"], 1)
                dve.wait_ge(s["d_route"], n + 5)
                dve.tensor_tensor(rstat[:, 3:4], top8[:, 0:1], top8[:, 1:2], ALU.add).then_inc(s["d_route"], 1)
                dve.max_index(idx8[:, :], top8[:, :], probs[:, :]).then_inc(s["d_route"], 1)
                dve.wait_ge(s["d_route"], n + 6)
                dve.reciprocal(rstat[:, 2:3], rstat[:, 3:4]).then_inc(s["d_route"], 1)
                dve.wait_ge(s["d_route"], n + 8)
                g = t * 5
                dve.tensor_scalar(top8[:, 0:2], top8[:, 0:2], rstat[:, 2:3], None, ALU.mult).then_inc(s["d_gate"], 1)
                dve.tensor_copy(idxf[:, :], idx8[:, 0:2]).then_inc(s["d_gate"], 1)
                dve.wait_ge(s["d_gate"], g + 2)
                for i in range(2):
                    dve.tensor_scalar(gates[:, i, :], iota[:, :], idxf[:, i:i + 1], top8[:, i:i + 1], ALU.is_equal,
                                      ALU.mult).then_inc(s["d_gate"], 1)
                dve.wait_ge(s["d_gate"], g + 4)
                dve.tensor_tensor(gates[:, 0, :], gates[:, 0, :], gates[:, 1, :], ALU.add).then_inc(s["d_gate"], 1)
                dve.wait_ge(s["d_gate"], g + 5)

            def lo_expert(e):
                dve.wait_ge(s["a_ewhi"], e + 1)
                dve.tensor_tensor(ew_lo[:, e, :, :], ew[:, e, :, :], ew_hi[:, e, :, :].bitcast(F32), ALU.subtract
                                  ).then_inc(s["d_ewlo"], 1)

            def add_bias(t, e):
                dve.wait_ge(s["t_expert"], t * NE + e + 1)
                dve.tensor_tensor(ps[:, e % 4, :], ps[:, e % 4, :], eb[:, e, :], ALU.add).then_inc(s["d_pre"], 1)

            def combine(t, e):
                dve.wait_ge(s["a_gelu"], t * NE + e + 1)
                gate = gates[:, 0, e:e + 1]
                if e == 0:
                    dve.tensor_scalar(comb[:, :], act_out[:, 0, :], gate, None, ALU.mult).then_inc(s["d_comb"], 1)
                else:
                    dve.wait_ge(s["d_comb"], t * NE + e)
                    dve.scalar_tensor_tensor(out=comb[:, :], in0=act_out[:, e % 2, :], scalar=gate, in1=comb[:, :],
                                             op0=ALU.mult, op1=ALU.add).then_inc(s["d_comb"], 1)

            def tile(t, first, last):
                for e in range(NE):
                    if first and e < NE // 2:
                        lo_expert(e + NE // 2)
                    if e == 1 and not last:
                        stats(t + 1)
                        dve.wait_ge(s["d_ln2"], (t + 1) * 3 + 1)
                    add_bias(t, e)
                    if e == 1 and not last:
                        variance(t + 1)
                    if e == 3 and not last:
                        normalise(t + 1)
                    if e >= 1:
                        if e == 1:
                            dve.wait_ge(s["t_comb"], t)
                        combine(t, e - 1)
                if not last:
                    lo_xn(t + 1)
                combine(t, NE - 1)
                if not last:
                    route(t + 1, (lambda: residual_out(t - 1)) if not first else
                          (lambda: dve.memset(idxf[:, :], 0.0)))

            dve.wait_ge(s["p_const"], 2)
            stats(0)
            dve.wait_ge(s["d_ln2"], 1)
            variance(0)
            normalise(0)
            dve.wait_ge(s["a_rwhi"], 1)
            dve.tensor_tensor(rw_lo[:, :, :], rw[:, :, :], rw_hi[:, :, :].bitcast(F32), ALU.subtract
                              ).then_inc(s["d_rwlo"], 1)
            lo_xn(0)
            dve.wait_ge(s["ld_router"], 32)
            route(0, lambda: None)
            for e in range(NE // 2):
                lo_expert(e)
            dve.wait_ge(s["ld_bias"], 32)
            tile(0, True, False)
            with dve.Fori(1, TILES) as t:
                tile(t, False, False)
            tile(TILES, False, True)
            residual_out(TILES - 1)
            residual_out(TILES)

        @block.tensor
        def _(pe):
            pe.wait_ge(s["c_ident"], 2)

            def w_turn(raw, sem_t, bank0):
                for ic in range(KC):
                    for o in range(KC):
                        mm = pe.transpose(ps[:, bank0 + ic, o * P:(o + 1) * P], raw[:, o, ic * P:(ic + 1) * P], ident[:, :])
                    mm.then_inc(s[sem_t], 1)

            pe.wait_ge(s["a_wsc"], KC)
            w_turn(w_raw[:, 0], "t_w", 4)
            pe.wait_ge(s["a_wsc"], 2 * KC)
            pe.wait_ge(s["d_wlo"], KC)
            w_turn(w_raw[:, 1], "t_w", 4)

            def turn(n, parts):
                if n >= 4:
                    pe.wait_ge(s["a_tr"], n - 3)
                for k, part in enumerate(parts):
                    for q in range(4):
                        mm = pe.matmul(ps[:, n % 4, q * P:(q + 1) * P], part(q), ident[:, :], is_transpose=True,
                                       start=(k == 0 and q == 0), stop=(k == len(parts) - 1 and q == 3),
                                       skip_group_check=True)
                mm.then_inc(s["t_tr"], 1)

            for hf in range(HALVES):
                base = hf * 32
                pe.wait_ge(s["d_rl"], hf + 1)
                for q in range(8):
                    turn(base + q, [lambda i, q=q: r_low[:, 4 * q + i, :, :].rearrange("p s n -> p (s n)")])
                for n in range(12):
                    if n < 4:
                        pe.wait_ge(s["d_up"], hf * 4 + n + 1)
                    else:
                        pe.wait_ge(s["d_lp"], hf * NB + n - 4 + 1)
                    for k in range(2):
                        turn(base + 8 + 2 * n + k,
                             [lambda i, w=w, n=n, k=k: ring[:, n % 2, w, 4 * k + i, :, :].rearrange("p s n -> p (s n)")
                              for w in range(2)])
                pe.wait_ge(s["a_tr"], base + 32)
                if hf == 0:
                    pe.wait_ge(s["d_wlo"], 2 * KC)
                for hb in range(NHB):
                    n = hf * NHB + hb
                    if n >= 2:
                        pe.wait_ge(s["a_so"], n - 1)
                    for i in range(HB):
                        for hp in range(2):
                            h = hp * 64 + hb * HB + i
                            bank = 4 + 2 * (n % 2) + i // 8
                            mm = pe.matmul(ps[hp * 64:hp * 64 + 64, bank, (i % 8) * NBP:(i % 8 + 1) * NBP],
                                           lT[:, h, :], rT[:, h, :], start=(i % 8 == 0), stop=(i % 8 == 7),
                                           skip_group_check=True)
                    mm.then_inc(s["t_mm"], 1)

            def split3(out_ap, lhs, rhs, start, stop, skip=False):
                (lh, ll), (rh, rl) = lhs, rhs
                for i, (a, b) in enumerate(((lh, rh), (ll, rh), (lh, rl))):
                    mm = pe.matmul(out_ap, a, b, start=start and i == 0, stop=stop and i == 2, skip_group_check=skip)
                return mm

            def x_turn(n, bank, i, rows):
                pe.wait_ge(s["d_x"], 2 * ((n + 1) // 2) + i + 1 if isinstance(n, int) and n == 0 else n + 2)
                w = rows
                for k in range(KC):
                    mm = pe.transpose(ps[:, bank, k * w:(k + 1) * w], xhat[0:rows, i, k * P:(k + 1) * P],
                                      ident[0:rows, 0:rows])
                mm.then_inc(s["t_x"], 1)

            pe.wait_ge(s["a_so"], HALVES * NHB)
            x_turn(0, 7, 0, NB)
            pe.wait_ge(s["d_x"], 2)
            x_turn(1, 6, 0, P)
            pe.wait_ge(s["d_loT"], 1)
            x_turn(2, 7, 1, P)

            def qk(c, m):
                hi, lo = (wqT_hi, wqT_lo) if m % 2 == 0 else (wkT_hi, wkT_lo)
                ci = m // 2
                for ic in range(KC):
                    w = slice(ci * P, (ci + 1) * P)
                    mm = split3(ps[:, 6 + m % 2, 0:KPAD], (hi[:, ic, w], lo[:, ic, w]),
                                (xT_hi[:, ic, :], xT_lo[:, ic, :]), ic == 0, ic == KC - 1)
                mm.then_inc(s["t_qk"], 1)

            def qk_wait(c, m):
                if m == 0:
                    pe.wait_ge(s["d_loT"], c * HALVES + 3)
                elif m >= 2:
                    pe.wait_ge(s["d_loqk"], c * 2 * KC + m - 1)

            for m in range(2 * KC):
                qk_wait(0, m)
                qk(0, m)
            pe.wait_ge(s["ld_wv"], 32)
            for i in range(2):
                if i == 1:
                    pe.wait_ge(s["d_wvlo"], KC)
                w_turn(w_raw2[:, i], "t_wv", 0)
            pe.wait_ge(s["d_wvlo"], KC)
            for ci in range(KC):
                for ic in range(KC):
                    w = slice(ci * P, (ci + 1) * P)
                    mm = split3(ps[:, 4, 2 * ci:2 * ci + 2], (wvT_hi[:, ic, w], wvT_lo[:, ic, w]),
                                (xT_hi[:, ic, BODY:KPAD], xT_lo[:, ic, BODY:KPAD]), ic == 0, ic == KC - 1, True)
            mm.then_inc(s["t_vb"], 1)
            pe.wait_ge(s["d_wvlo"], 2 * KC)
            pe.wait_ge(s["d_vb"], KC + 1)
            pe.wait_ge(s["c_ones"], 4)
            pe.wait_ge(s["ld_bo"], 16)
            for ci in range(KC):
                for part in (woT_hi, woT_lo):
                    pe.matmul(ps[0:32, 5, :], vblk[:, ci, :], part[:, ci, :].bitcast(F32),
                              start=(ci == 0 and part is woT_hi), stop=False)
            pe.matmul(ps[0:32, 5, :], e16[:, :], bo_row[:, :], start=False, stop=True).then_inc(s["t_u"], 1)

            def scores(c, j):
                ci = j // HPC
                if j % HPC == 0:
                    pe.wait_ge(s["d_loqk"], c * 2 * KC + 2 * ci + 2)
                for st in range(HALVES):
                    w = slice(st * P, (st + 1) * P)
                    mm = split3(ps[:, 2 * (j % 2) + st, 0:KPAD], (q_hi[:, j, w], q_lo[:, j, w]),
                                (k_hi[:, ci, :], k_lo[:, ci, :]), True, True)
                mm.then_inc(s["t_s"], 1)

            def turn_p(c, j):
                pe.wait_ge(s["d_norm"], c * NHEAD + j + 1)
                for tt in range(HALVES):
                    for st in range(HALVES):
                        mm = pe.transpose(ps[:, 4, tt * BODY + st * P:tt * BODY + (st + 1) * P],
                                          prb[:, j % 4, st, tt * P:(tt + 1) * P], ident[:, :])
                mm.then_inc(s["t_tp"], 1)

            def pv(c, gr):
                pe.wait_ge(s["a_pt"], c * NHEAD + (gr + 1) * HPC)
                pe.wait_ge(s["p_ptc"], c * KC + gr + 1)
                for tt in range(HALVES):
                    for j in range(HPC):
                        h = gr * HPC + j
                        mm = pe.matmul(ps[j * DH:(j + 1) * DH, 5, 0:KEYS], v_sb[:, tt, h * DH:(h + 1) * DH],
                                       pts[:, h % 8, tt, 0:KEYS], start=(tt == 0), stop=(tt == HALVES - 1))
                mm.then_inc(s["t_pv"], 1)

            def cls_scores(c):
                for ci in range(KC):
                    mm = split3(ps[:, 6, 0:KPAD], (qblk_hi[:, ci, :], qblk_lo[:, ci, :]),
                                (k_hi[:, ci, :], k_lo[:, ci, :]), ci == 0, ci == KC - 1)
                mm.then_inc(s["t_sc"], 1)

            def cls_turn(c):
                for tt in range(HALVES):
                    mm = pe.transpose(ps[:, 6, tt * NHEAD:(tt + 1) * NHEAD], pc[:, tt * P:(tt + 1) * P],
                                      ident[0:NHEAD, 0:NHEAD])
                mm.then_inc(s["t_tc"], 1)

            def values(c, st):
                for ic in range(KC):
                    w = slice(st * P, (st + 1) * P)
                    mm = split3(ps[:, 7, :], (xT_hi[:, ic, w], xT_lo[:, ic, w]),
                                (wvT_hi[:, ic, :], wvT_lo[:, ic, :]), ic == 0, ic == KC - 1)
                mm.then_inc(s["t_v"], 1)

            def key_turn(c):
                pe.wait_ge(s["p_pc"], (c + 1) * NHEAD)
                pe.wait_ge(s["a_pt"], (c + 1) * NHEAD)
                for st in range(HALVES):
                    mm = pe.transpose(ps[0:NHEAD, 4, st * P:(st + 1) * P], pcls[:, st, :], ident[:, :])
                mm.then_inc(s["t_tck"], 1)

            def project(c, st, bank):
                w = slice(st * P, (st + 1) * P)
                pe.matmul(ps[:, bank, :], pclsT[:, w], u_sb[:, :], start=True, stop=False)
                for ic in range(KC):
                    mm = split3(ps[:, bank, :], (oT_hi[:, ic, w], oT_lo[:, ic, w]),
                                (woT_hi[:, ic, :], woT_lo[:, ic, :]), False, ic == KC - 1)
                mm.then_inc(s["t_op"], 1)

            def body(c, first, last):
                for j in range(NHEAD):
                    if j >= 2 or not first:
                        pe.wait_ge(s["a_exps"], c * NHEAD + j - 1)
                    scores(c, j)
                    if j >= 3:
                        pe.wait_ge(s["a_pt"], c * NHEAD + j - 2)
                    elif j == 2:
                        if not first:
                            pe.wait_ge(s["a_pt"], c * NHEAD)
                    elif not first:
                        pe.wait_ge(s["a_pt"], c * NHEAD - 2 + j)
                    if j >= 2:
                        if j == 3 and not first:
                            pe.wait_ge(s["d_tck"], c)
                        if j == 2 and not first:
                            key_turn(c - 1)
                            pe.wait_ge(s["d_tck"], c)
                        turn_p(c, j - 2)
                    elif not first:
                        turn_p(c - 1, NHEAD - 2 + j)
                    if j == 1:
                        pe.wait_ge(s["d_loqk"], (c + 1) * 2 * KC)
                        if first:
                            pe.wait_ge(s["d_qb"], 1 + 2 * KC)
                        cls_scores(c)
                    if j == 1:
                        values(c, 0)
                    if j == 2 and not first:
                        pe.wait_ge(s["d_ot"], c * KC - 1)
                        pv(c - 1, 3)
                    if j == 3:
                        pe.wait_ge(s["d_scn"], 3 * c + 3)
                        pe.wait_ge(s["a_expc"], c + 1)
                        pe.wait_ge(s["a_v"], c * HALVES + 1)
                        values(c, 1)
                        cls_turn(c)
                    if j == 4 and not first:
                        pe.wait_ge(s["d_tck"], c)
                        pe.wait_ge(s["d_ot"], c * KC)
                        pe.wait_ge(s["d_ptc"], c + 1)
                        project(c - 1, 0, 6)
                    if j == 5 and not first:
                        pe.wait_ge(s["a_v"], c * HALVES + 2)
                        project(c - 1, 1, 7)
                    if j == 7 and not last:
                        if first:
                            pe.wait_ge(s["d_u"], 1)
                            pe.wait_ge(s["d_ptc"], c + 1)
                            pe.wait_ge(s["a_v"], c * HALVES + 2)
                        else:
                            pe.wait_ge(s["d_res"], c * HALVES - 1)
                        pe.wait_ge(s["d_x"], (c + 1) * HALVES + 3)
                        x_turn2(c + 1, 0, 6)
                        if not first:
                            pe.wait_ge(s["d_res"], c * HALVES)
                        pe.wait_ge(s["d_x"], (c + 1) * HALVES + 4)
                        x_turn2(c + 1, 1, 7)
                    for m in QK_SLOT[j] if not last else ():
                        qk_wait(c + 1, m)
                        qk(c + 1, m)
                    if j in (6, 10, 14):
                        if j == 6:
                            pe.wait_ge(s["a_v"], (c + 1) * HALVES)
                        if j > 6 or not first:
                            pe.wait_ge(s["d_ot"], c * KC + (j - 6) // 4)
                        pv(c, (j - 6) // 4)

            def x_turn2(c, i, bank):
                for k in range(KC):
                    mm = pe.transpose(ps[:, bank, k * P:(k + 1) * P], xhat[:, i, k * P:(k + 1) * P], ident[:, :])
                mm.then_inc(s["t_x"], 1)

            body(0, True, False)
            with pe.Fori(1, NB - 1) as c:
                body(c, False, False)
            body(NB - 1, False, True)
            last = NB - 1
            pe.wait_ge(s["a_pt"], NB * NHEAD - 2)
            turn_p(last, NHEAD - 2)
            pe.wait_ge(s["a_pt"], NB * NHEAD - 1)
            turn_p(last, NHEAD - 1)
            key_turn(last)
            pe.wait_ge(s["d_ot"], NB * KC - 1)
            pv(last, 3)
            pe.wait_ge(s["d_tck"], NB)
            pe.wait_ge(s["d_ot"], NB * KC)
            project(last, 0, 6)
            project(last, 1, 7)
            pe.wait_ge(s["d_qb"], 13)
            pe.wait_ge(s["d_res"], NB * HALVES - 1)
            pe.matmul(ps[:, 6, :], pccT[:, :], u_sb[:, :], start=True, stop=False)
            for ic in range(KC):
                mm = split3(ps[:, 6, :], (oc_hi[:, ic, :], oc_lo[:, ic, :]), (woT_hi[:, ic, :], woT_lo[:, ic, :]),
                            False, ic == KC - 1)
            mm.then_inc(s["t_fin"], 1)
            pe.wait_ge(s["d_fin"], 1)

            def turn_xn(t):
                pe.wait_ge(s["d_xn"], t + 1)
                for k in range(KC):
                    mm = pe.transpose(ps[:, 4, k * P:(k + 1) * P], xn[:, k * P:(k + 1) * P], ident[:, :])
                mm.then_inc(s["t_xn"], 1)

            def router(t):
                pe.wait_ge(s["d_loxn"], t + 1)
                for k in range(KC):
                    mm = split3(ps[:, 7, 0:NE], (xnT_hi[:, k, :], xnT_lo[:, k, :]), (rw_hi[:, k, :], rw_lo[:, k, :]),
                                k == 0, k == KC - 1)
                mm.then_inc(s["t_router"], 1)

            def expert(t, e, first):
                if first:
                    pe.wait_ge(s["d_ewlo"], e + 1)
                if e >= 4 or not first:
                    pe.wait_ge(s["a_gelu"], t * NE + e - 3)
                for k in range(KC):
                    mm = split3(ps[:, e % 4, :], (xnT_hi[:, k, :], xnT_lo[:, k, :]),
                                (ew_hi[:, e, k, :], ew_lo[:, e, k, :]), k == 0, k == KC - 1)
                mm.then_inc(s["t_expert"], 1)

            def turn_comb(t):
                pe.wait_ge(s["d_comb"], (t + 1) * NE)
                for k in range(KC):
                    mm = pe.transpose(ps[:, 5, k * P:(k + 1) * P], comb[:, k * P:(k + 1) * P], ident[:, :])
                mm.then_inc(s["t_comb"], 1)

            def project_out(t):
                pe.wait_ge(s["a_combT"], t + 1)
                for k in range(KC):
                    mm = pe.matmul(ps[:, 6, :], combT[:, k, :], ow[:, k, :], start=(k == 0), stop=(k == KC - 1))
                mm.then_inc(s["t_out"], 1)

            def tile(t, first, last):
                for e in range(NE):
                    if e == NE - 2 and not last:
                        turn_xn(t + 1)
                    expert(t, e, first)
                if not first:
                    project_out(t - 1)
                if not last:
                    router(t + 1)
                turn_comb(t)

            turn_xn(0)
            pe.wait_ge(s["d_rwlo"], 1)
            router(0)
            tile(0, True, False)
            pe.wait_ge(s["ld_outw"], 16)
            with pe.Fori(1, TILES) as t:
                tile(t, False, False)
            tile(TILES, False, True)
            pe.wait_ge(s["d_out"], TILES)
            project_out(TILES)


_INS = ['x', 'cls_tok', 'L0_tok_log_dt', 'L0_tok_B_ri', 'L0_tok_inv_A_real', 'L0_tok_A_imag', 'L0_attn_Wq',
        'L0_attn_bq', 'L0_attn_Wk', 'L0_attn_bk', 'L0_attn_Wv', 'L0_attn_bv', 'L0_attn_Wo', 'L0_attn_bo',
        'L0_attn_spiral_weight', 'L0_attn_helix_rotation', 'L0_ffn_router_w', 'L0_ffn_router_b',
        'L0_ffn_expert_w', 'L0_ffn_expert_b', 'L0_ffn_out_w', 'L0_ffn_out_b']
_OUTS = [((8, 257, 512), 'float32')]


def kernel(**inputs):
    import numpy as _np
    import concourse.bacc as _bacc
    from concourse import mybir as _mybir
    from concourse.bass_utils import run_bass_kernel_spmd as _run

    nc = _bacc.Bacc("TRN2", target_bir_lowering=False, num_devices=1)
    arrays, args = {}, []
    for name in _INS:
        a = _np.ascontiguousarray(inputs[name])
        arrays[f"in_{name}_dram"] = a
        args.append(nc.dram_tensor(f"in_{name}_dram", a.shape, _mybir.dt.from_np(a.dtype), kind="ExternalInput").ap())
    for i, (shape, dtype) in enumerate(_OUTS):
        dt = _mybir.dt.from_np(_np.dtype(dtype))
        args.append(nc.dram_tensor(f"out_{i}_dram", shape, dt, kind="ExternalOutput").ap())
    vit_tower_kernel(nc, *args)
    r = _run(nc, [arrays], core_ids=[0])
    got = tuple(r.results[0][f"out_{i}_dram"] for i in range(len(_OUTS)))
    return got[0]
```

```python
from contextlib import ExitStack

import concourse.bass as bass
from concourse import mybir

F32 = mybir.dt.float32
F32R = mybir.dt.float32r
ALU = mybir.AluOpType
ACT = mybir.ActivationFunctionType
AX_X = mybir.AxisListType.X

P = 128
BANK = 512
EPS = 1e-5
TWO_PI_HI = 6.28125
TWO_PI_LO = 0.0019353071795864769
PI_SAFE = 3.1415925
ROUND_MAGIC = 12582912.0


def vit_tower_kernel(nc, x, cls_tok, log_dt, B_ri, inv_A_real, A_imag, Wq, bq, Wk, bk, Wv, bv, Wo, bo,
                     spiral, rot, router_w, router_b, expert_w, expert_b, out_w, out_b, out):
    NB, NH_SSM, NS, _ = x.shape
    D = Wq.shape[0]
    NHEAD = spiral.shape[0]
    DH = D // NHEAD
    NE = router_w.shape[1]
    KC = D // P
    HPC = P // DH
    HALVES = NH_SSM // P
    BODY = HALVES * P
    KEYS = BODY + 1
    KPAD = KEYS + 1
    S2 = 2 * NS
    NA = 8
    NBP = D // NA
    NLOW = NBP // 2
    PIECE = 8
    TILES = NB * HALVES
    CLS = TILES
    HB = 16
    NHB = P // 2 // HB
    SEL = 2
    NT = TILES + 1
    COLS = NT * SEL
    SLOTS = (SEL * NB * KEYS + NE * (P - 1)) // P
    LOOPED = NT // 2
    assert SLOTS % 4 == 0 and NT % 2 == 1
    CHAIN = 2 + 9 * 2 + 8 * 5 + 3 + 3 * 5
    FIRST_BANKS = (0, 1, 2, 3, 6, 7, 4, 5)
    QK_SLOT = {j: () for j in range(NHEAD)} | {9: (0,), 10: (1,), 11: (2,), 12: (3,), 13: (4,), 14: (5,), 15: (6, 7)}
    assert S2 == P and NBP * NA == D and NB * NA == 64 and HALVES == 2 and DH == 32

    CHOSEN_STEP, ROUTE_STEPS, AFTER_SLOTS = 12, 44, 6

    with ExitStack() as whole:
        def sb(scope, name, shape, dt=F32):
            return scope.enter_context(nc.sbuf_tensor(name, shape, dt))

        def sem(name):
            return whole.enter_context(nc.semaphore(name))

        ps = whole.enter_context(nc.psum_tensor("ps", [P, 8, BANK], F32))

        ident = sb(whole, "ident", [P, P])
        tok = sb(whole, "tok", [P, TILES + 1, D])
        st2 = sb(whole, "st2", [P, NT, 6])
        mean_var = sb(whole, "mean_var", [P, NT, 2])
        attn = ExitStack()
        wqT_hi = sb(attn, "wqT_hi", [P, KC, D], F32R)
        wqT_lo = sb(attn, "wqT_lo", [P, KC, D], F32R)
        wkT_hi = sb(attn, "wkT_hi", [P, KC, D], F32R)
        wkT_lo = sb(attn, "wkT_lo", [P, KC, D], F32R)
        q_scale = sb(attn, "q_scale", [P, KC])
        k_scale = sb(attn, "k_scale", [P, KC])
        q_bias = sb(attn, "q_bias", [P, KC])
        k_bias = sb(attn, "k_bias", [P, KC])
        bv_col = sb(attn, "bv_col", [P, KC])
        mk = ExitStack()
        ldt = sb(mk, "ldt", [P, HALVES])
        iar = sb(mk, "iar", [P, HALVES, NS])
        aim = sb(mk, "aim", [P, HALVES, NS])
        b_in = sb(mk, "b_in", [P, HALVES, NS, 2])
        x_in = sb(mk, "x_in", [P, NB, NS, 2])
        coef = sb(mk, "coef", [P, NB, 2, NS])
        ctmp = sb(mk, "ctmp", [P, NB, NS])
        g = sb(mk, "g", [P, HALVES, 2, NS])
        prm = sb(mk, "prm", [P, 8, HALVES, NS])
        dt2 = sb(mk, "dt2", [P, 2, HALVES])
        zs = sb(mk, "zs", [P, 9, 2, NS])
        zt = sb(mk, "zt", [P, 9, 2, NS])
        r_low = sb(mk, "r_low", [P, NLOW, 2, NS])
        w_pow = sb(mk, "w_pow", [P, NA, 2, NS])
        w_b = sb(mk, "w_b", [P, NA, 2, NS])
        ring = sb(mk, "ring", [P, 2, 2, PIECE, 2, NS])
        rT = sb(mk, "rT", [P, P, NBP])
        so = sb(mk, "so", [P, 2, HB * NBP])
        rcol = sb(mk, "rcol", [P, 4, KC])
        with ExitStack() as early:
            w_raw = sb(early, "w_raw", [P, 2, KC, D])
        lT = sb(mk, "lT", [P, P, NB * NA])
        mk.close()
        r_low2 = tok[:, NB:2 * NB, :].rearrange("p t d -> p (t d)").rearrange("p (m s n) -> p m s n", s=2, n=NS)
        early_tok = tok[:, 0:NB, :].rearrange("p t d -> p (t d)")
        zs2, zt2 = (early_tok[:, i * 9 * S2:(i + 1) * 9 * S2].rearrange("p (k s n) -> p k s n", s=2, n=NS)
                    for i in range(2))
        ptmp = early_tok[:, 18 * S2:(18 + PIECE) * S2].rearrange("p (m s n) -> p m s n", s=2, n=NS)
        at = attn
        wvT_hi = sb(at, "wvT_hi", [P, KC, D], F32R)
        wvT_lo = sb(at, "wvT_lo", [P, KC, D], F32R)
        woT_hi = sb(at, "woT_hi", [P, KC, D], F32R)
        woT_lo = sb(at, "woT_lo", [P, KC, D], F32R)
        xT_hi = sb(at, "xT_hi", [P, KC, KPAD], F32R)
        xT_lo = sb(at, "xT_lo", [P, KC, KPAD], F32R)
        xhat = sb(at, "xhat", [P, HALVES, D])
        q_hi = sb(at, "q_hi", [P, NHEAD, BODY], F32R)
        q_lo = sb(at, "q_lo", [P, NHEAD, BODY], F32R)
        qcls_hi = sb(at, "qcls_hi", [P, KC, 2], F32R)
        qcls_lo = sb(at, "qcls_lo", [P, KC, 2], F32R)
        k_hi = sb(at, "k_hi", [P, KC, KPAD], F32R)
        k_lo = sb(at, "k_lo", [P, KC, KPAD], F32R)
        v_sb = sb(at, "v_sb", [P, HALVES, D])
        oT_hi = sb(at, "oT_hi", [P, KC, BODY], F32R)
        oT_lo = sb(at, "oT_lo", [P, KC, BODY], F32R)
        u_sb = sb(at, "u_sb", [P, D])
        pclsT = sb(at, "pclsT", [P, BODY])
        pccT = sb(at, "pccT", [P, P])
        pcls = sb(at, "pcls", [P, HALVES, NHEAD])
        pc = sb(at, "pc", [NHEAD, KPAD])
        ptc = sb(at, "ptc", [P, HALVES, NHEAD])
        ocls = sb(at, "ocls", [P, KC, NB])
        negmax = sb(at, "negmax", [P, 4, HALVES])
        rowsum = sb(at, "rowsum", [P, 4, HALVES])
        rrec = sb(at, "rrec", [P, 4, HALVES])
        cstat = sb(at, "cstat", [NHEAD, 4])
        lnst = sb(at, "lnst", [P, HALVES, 6])
        lnmv = sb(at, "lnmv", [P, HALVES, 2])
        lnr = sb(at, "lnr", [P, 2, HALVES])
        mhalf = sb(at, "mhalf", [P, HALVES])
        ones = sb(at, "ones", [P, HALVES, HPC])
        qblk_hi = sb(at, "qblk_hi", [P, KC, P], F32R)
        qblk_lo = sb(at, "qblk_lo", [P, KC, P], F32R)
        zero_row = sb(at, "zero_row", [P, D])
        late = ExitStack()
        prb = sb(late, "prb", [P, 4, HALVES, KPAD])
        pts = sb(late, "pts", [P, 8, HALVES, KPAD])
        late.close()
        setup = ExitStack()
        w_raw2 = sb(setup, "w_raw2", [P, 2, KC, D])
        mask = sb(setup, "mask", [P, KC, P])
        vblk_hi = sb(setup, "vblk_hi", [P, KC, P], F32R)
        vblk_lo = sb(setup, "vblk_lo", [P, KC, P], F32R)
        bo_row = sb(setup, "bo_row", [1, D])
        e16 = sb(setup, "e16", [1, P])
        setup.close()
        oc_hi, oc_lo = qblk_hi, qblk_lo
        attn.close()
        ffn = whole
        with ExitStack() as as_loaded:
            ew = sb(as_loaded, "ew", [P, NE, KC, D])
        with ExitStack() as at_end:
            ow_hi = sb(at_end, "ow_hi", [P, KC, D], F32R)
            ow_lo = sb(at_end, "ow_lo", [P, KC, D], F32R)
            combT_hi = sb(at_end, "combT_hi", [P, 2, KC, P], F32R)
            combT_lo = sb(at_end, "combT_lo", [P, 2, KC, P], F32R)
            comb = sb(at_end, "comb", [P, 2, D])
        ew_lo = sb(ffn, "ew_lo", [P, NE, KC, D], F32R)
        ew_hi = sb(ffn, "ew_hi", [P, NE, KC, D], F32R)
        rw = sb(ffn, "rw", [P, KC, NE])
        rw_parts = sb(ffn, "rw_parts", [P, KC, 2, NE], F32R)
        eb = sb(ffn, "eb", [P, NE, D])
        ob = sb(ffn, "ob", [P, D])
        rb = sb(ffn, "rb", [P, NE])
        rows = sb(ffn, "rows", [P, 4, D])
        rstd = sb(ffn, "rstd", [P, NT])
        gates = sb(ffn, "gates", [P, NT, SEL])
        slot_of = sb(ffn, "slot_of", [P, COLS], mybir.dt.uint32)
        expert_of = sb(ffn, "expert_of", [P, SLOTS], mybir.dt.int32)
        xnT_hi = sb(ffn, "xnT_hi", [P, 2, KC, P], F32R)
        xnT_lo = sb(ffn, "xnT_lo", [P, 2, KC, P], F32R)
        with ExitStack() as at_end:
            ow = sb(at_end, "ow", [P, KC, D])
        rt = ffn
        before = sb(rt, "before", [P, P])
        all_one = sb(rt, "all_one", [P, P])
        iota_e = sb(rt, "iota_e", [P, NE])
        iota_s = sb(rt, "iota_s", [P, SLOTS])
        valid = sb(rt, "valid", [P, 1])
        spare = sb(rt, "spare", [P, SEL])
        mh2 = sb(rt, "mh2", [P, NT])
        probs = sb(rt, "probs", [P, NT, NE])
        rsum = sb(rt, "rsum", [P, 3, NT])
        top8 = sb(rt, "top8", [P, NT, 8])
        idx8 = sb(rt, "idx8", [P, NT, 8], mybir.dt.uint32)
        idxf = sb(rt, "idxf", [P, NT, SEL])
        chosen = sb(rt, "chosen", [P, COLS, NE])
        cum = sb(rt, "cum", [P, 2, COLS, NE])
        cnt = sb(rt, "cnt", [P, NE])
        tile0 = sb(rt, "tile0", [P, NE + 1])
        slotf = sb(rt, "slotf", [P, COLS])
        reached = sb(rt, "reached", [P, SLOTS, NE])

        signals = {
            "pool_cls_zeroed": "the class tile's rows are zero",
            "pool_identity": "the identity matrix",
            "pool_step": "a step of Pool's small chains: coefficients, then 1 / sqrt(variance + eps)",
            "pool_coef": "coefficients of a channel half",
            "pool_power_step": "a step of the second half's powers",
            "pool_q_zeroed": "q's buffers hold zeros outside each head's rows",
            "pool_filled": "a constant's first filling",
            "pool_constants": "a constant of attention",
            "pool_mask_half": "the heads' mask, one bound cut",
            "pool_head_mask": "the heads' mask",
            "pool_key_col": "a head's probabilities of the class key",
            "pool_cls_cols": "the class query's column in four heads' P^T",
            "pool_zero_row": "a row of zeros",
            "pool_routing_const": "a constant of the routing",
            "pool_rstd": "the second norm's 1 / sqrt",
            "pool_out_bias": "a tile with the output bias added",
            "act_exp_params": "exponentials of the parameters",
            "act_sines": "sines of the rotations",
            "act_w_scaled": "a chunk of Wq or Wk scaled",
            "act_w_high": "high part of a chunk of Wq^T, Wk^T",
            "act_table_kept": "a bank of the turned tables",
            "act_tokens_kept": "token values of 32 channels",
            "act_xT_high": "high part of a turned tile",
            "act_wvo_high": "high part of a chunk of Wv^T, Wo^T",
            "act_qk_high": "high part of q or k of a chunk",
            "act_exp": "a head's exponentials and their sums",
            "act_cls_exp": "the class query's",
            "act_pT_kept": "a head's P^T",
            "act_v_kept": "v of a tile",
            "act_oT_high": "high part of four heads' output",
            "act_router_high": "high part of the router's matrix",
            "act_xnT_high": "high part of a turned token tile",
            "act_route_exp": "the router's exponentials",
            "act_expert_high": "high part of an expert's matrix",
            "act_slotT_high": "high part of a turned tile of slots",
            "act_gelu": "results of a tile of slots",
            "act_out_w_high": "high part of the output matrix",
            "act_combT_high": "high part of a turned combined tile",
            "dve_param_step": "a step of the parameters' chain",
            "dve_z_ready": "z and g of both halves",
            "dve_angles": "angles, then the scales and biases of q and k",
            "dve_power_step": "a step of the powers",
            "dve_powers_copied": "the second half's powers are off the tokens' place",
            "dve_r_low": "z^0 .. z^31 of the first half",
            "dve_r_upper": "two products of the table's upper half",
            "dve_l_product": "two products of coefficient and power, for a batch",
            "dve_w_low": "low part of a chunk of Wq^T, Wk^T",
            "dve_ln_step": "a step of the first norm",
            "dve_xhat": "a normed tile",
            "dve_xT_low": "low part of a turned tile",
            "dve_qk_low": "low part of q or k of a chunk",
            "dve_wvo_low": "low part of a chunk of Wv^T, Wo^T",
            "dve_cls_value": "the class value spread over the heads",
            "dve_spread": "the class query spread over the heads, then the class rows' output",
            "dve_u": "the class value and biases through Wo",
            "dve_max": "a head's maxima",
            "dve_recip": "a head's reciprocal sums",
            "dve_normed": "a head's probabilities",
            "dve_cls_max": "the class query's maxima",
            "dve_cls_step": "a step of the class query's probabilities",
            "dve_cls_pT": "the class query's probabilities, keys on partitions",
            "dve_key_probs": "the class key's probabilities, heads on partitions",
            "dve_oT_low": "low part of four heads' output",
            "dve_residual": "a tile after attention",
            "dve_attn_done": "the class rows after attention: all of it is done",
            "dve_stats2": "a step of the second norm's statistics",
            "dve_router_low": "low part of the router's matrix",
            "dve_xn": "a token tile after the second norm",
            "dve_xnT_low": "low part of a turned token tile",
            "dve_route_step": "a step of the routing",
            "dve_row_ready": "a token tile's rows for the slots",
            "dve_expert_low": "low part of an expert's matrix",
            "dve_slotT_low": "low part of a turned tile of slots",
            "dve_bias_added": "an expert's bias added",
            "dve_out_w_low": "low part of the output matrix",
            "dve_combined": "a step of gating and adding: two a tile",
            "dve_combT_low": "low part of a turned combined tile",
            "dve_out": "a finished tile",
            "pe_w_turned": "a chunk of Wq^T, Wk^T",
            "pe_table_turned": "a bank of turned tables",
            "pe_tokens": "token values of 32 channels",
            "pe_x_turned": "a turned tile",
            "pe_qk": "q or k of a chunk",
            "pe_wvo_turned": "a chunk of Wv^T, Wo^T",
            "pe_cls_value": "the class value",
            "pe_u": "the class value and biases through Wo",
            "pe_scores": "a head's scores",
            "pe_cls_scores": "the class query's scores",
            "pe_cls_turned": "the class query's probabilities turned",
            "pe_values": "v of a tile",
            "pe_p_turned": "a head's P^T",
            "pe_key_turned": "the class key's probabilities turned",
            "pe_pv": "four heads' output",
            "pe_projected": "a tile through Wo",
            "pe_cls_projected": "the class rows through Wo",
            "pe_xn_turned": "a turned token tile",
            "pe_logits": "a tile's logits",
            "pe_ranks": "rows before each row, and rows in each column",
            "pe_slot_turned": "a turned tile of slots",
            "pe_expert": "a tile of slots through its expert",
            "pe_comb_turned": "a turned combined tile",
            "pe_out": "a tile through the output matrix",
            "loaded_ssm": "parameters of the state space model",
            "loaded_x0": "x of the first channel half",
            "loaded_x1": "x of the second",
            "loaded_vectors": "rotations, spirals and biases",
            "loaded_wq": "Wq",
            "loaded_wk": "Wk",
            "loaded_wv": "Wv",
            "loaded_wo": "Wo",
            "loaded_bo": "bo",
            "loaded_cls": "the class token",
            "loaded_tokens0": "the first batch's tokens",
            "loaded_tokens": "the other batches'",
            "loaded_router": "the router",
            "loaded_biases": "the experts' and the output bias",
            "loaded_out_w": "the output matrix",
            "stored_zeros": "zeros in all slots",
            "stored_out": "finished rows",
        }
        s = {name: sem(name) for name in signals}
        sent = [sem(f"sent{i}") for i in range(4)]
        ld_xs = [sem(f"ld_xs{i}") for i in range(2)]
        st_y = [sem(f"st_y{i}") for i in range(2)]
        got_y = [sem(f"got_y{i}") for i in range(2)]
        ld_ew = [sem(f"loaded_expert{e}") for e in range(NE)]
        s_row = [sem(f"stored_rows{i}") for i in range(2)]
        tok_dram = nc.dram_tensor("tok_dram", [HALVES, P, 64, NBP], F32).ap()

        x_slots = nc.dram_tensor("x_slots", [(SLOTS + SEL) * P, D], F32).ap()
        y_slots = nc.dram_tensor("y_slots", [(SLOTS + SEL) * P, D], F32).ap()

        def tiles_in_pairs(engine, step):
            step(0, 0, True)
            step(1, 1, True)
            with engine.Fori(1, LOOPED) as pair:
                step(2 * pair, 0, False)
                step(2 * pair + 1, 1, False)
            step(NT - 1, 0, False)

        block = whole.enter_context(nc.Block())
        bc = lambda ap, shape: ap.broadcast_to(shape)

        @block.sync
        def _(sp):
            whole.enter_context(nc.allow_non_contiguous_dma(reason="a few hundred words of parameters"))
            sp.dma_start(ldt[:, :], log_dt.rearrange("(f p) -> p f", p=P)).then_inc(s["loaded_ssm"], 16)
            sp.dma_start(iar[:, :, :], inv_A_real.rearrange("(f p) n -> p f n", p=P)).then_inc(s["loaded_ssm"], 16)
            sp.dma_start(aim[:, :, :], A_imag.rearrange("(f p) n -> p f n", p=P)).then_inc(s["loaded_ssm"], 16)
            sp.dma_start(b_in[:, :, :, :], B_ri.rearrange("(f p) n r -> p f n r", p=P)).then_inc(s["loaded_ssm"], 16)
            sp.dma_start(x_in[:, :, :, :], x[:, 0:P].rearrange("c p n r -> p c n r")).then_inc(s["loaded_x0"], 16)
            sp.dma_start(rcol[:, 0, :], rot.rearrange("(k p) -> p k", p=P)).then_inc(s["loaded_vectors"], 16)
            for j in range(HPC):
                sp.dma_start(rcol[j * DH:(j + 1) * DH, 1, :],
                             spiral.rearrange("(k j) -> j k", j=HPC)[j:j + 1, :].broadcast_to([DH, KC])
                             ).then_inc(s["loaded_vectors"], 16)
            sp.dma_start(q_bias[:, :], bq.rearrange("(k p) -> p k", p=P)).then_inc(s["loaded_vectors"], 16)
            sp.dma_start(k_bias[:, :], bk.rearrange("(k p) -> p k", p=P)).then_inc(s["loaded_vectors"], 16)
            sp.dma_start(w_raw[:, 0, :, :], Wq.rearrange("(o p) i -> p o i", p=P)).then_inc(s["loaded_wq"], 16)
            sp.dma_start(w_raw[:, 1, :, :], Wk.rearrange("(o p) i -> p o i", p=P)).then_inc(s["loaded_wk"], 16)
            sp.dma_start(bv_col[:, :], bv.rearrange("(k p) -> p k", p=P)).then_inc(s["loaded_vectors"], 16)
            sp.wait_ge(s["pool_cls_zeroed"], 1)
            sp.dma_start(tok[0:NB, CLS, :], cls_tok[0, :, :].broadcast_to([NB, D])).then_inc(s["loaded_cls"], 16)
            sp.wait_ge(s["pool_coef"], 1)
            sp.dma_start(x_in[:, :, :, :], x[:, P:2 * P].rearrange("c p n r -> p c n r")).then_inc(s["loaded_x1"], 16)
            for hf in range(HALVES):
                for hb in range(NHB):
                    n = hf * NHB + hb
                    sp.wait_ge(s["act_tokens_kept"], n + 1)
                    sp.dma_start(tok_dram[hf, :, hb * HB:(hb + 1) * HB, :],
                                 so[:, n % 2, :].rearrange("r (h b) -> r h b", h=HB)).then_inc(s_row[n % 2], 16)
                for row in s_row:
                    sp.wait_ge(row, 16 * NHB // 2 * (hf + 1))
                if hf == HALVES - 1:
                    sp.wait_ge(s["pe_tokens"], HALVES * NHB)
                    sp.dma_start(w_raw2[:, 0, :, :], Wv.rearrange("(o p) i -> p o i", p=P)).then_inc(s["loaded_wv"], 16)
                    sp.dma_start(w_raw2[:, 1, :, :], Wo.rearrange("(o p) i -> p o i", p=P)).then_inc(s["loaded_wo"], 16)
                    sp.dma_start(bo_row[:, :], bo.rearrange("(a d) -> a d", a=1)).then_inc(s["loaded_bo"], 16)
                if hf == 0:
                    sp.wait_ge(s["dve_powers_copied"], 1)
                for c in range(NB):
                    for hp in range(2):
                        r0 = hp * 64 + c * NA
                        sp.dma_start(
                            tok[hp * 64:hp * 64 + 64, hf * NB + c, :].rearrange("h (a b) -> h a b", a=NA),
                            tok_dram[hf, r0:r0 + NA, :, :].rearrange("a h b -> h a b")
                            ).then_inc(s["loaded_tokens0" if c == 0 else "loaded_tokens"], 16)

            def load_expert(e):
                sp.dma_start(ew[:, e, :, :], expert_w[e].rearrange("(k p) d -> p k d", p=P)
                             ).then_inc(ld_ew[e], 16)

            sp.wait_ge(s["pool_zero_row"], 1)
            sp.dma_start(x_slots.rearrange("(i p) d -> p i d", p=P),
                         zero_row[:, :].unsqueeze(1).broadcast_to([P, SLOTS + SEL, D])).then_inc(s["stored_zeros"], 16)
            sp.dma_start(y_slots[SLOTS * P:, :].rearrange("(i p) d -> p i d", p=P),
                         zero_row[:, :].unsqueeze(1).broadcast_to([P, SEL, D])).then_inc(s["stored_zeros"], 16)
            sp.wait_ge(s["pe_qk"], NB * 2 * KC)
            for e in range(NE // 2):
                load_expert(e)
            sp.wait_ge(s["dve_attn_done"], 1)
            sp.dma_start(rw[:, :, :], router_w.rearrange("(k p) e -> p k e", p=P)
                         ).then_inc(s["loaded_router"], 16)
            sp.dma_start(rb[:, :], router_b.rearrange("(a n) -> a n", a=1).broadcast_to([P, NE])
                         ).then_inc(s["loaded_router"], 16)
            sp.dma_start(ob[:, :], out_b.rearrange("(a n) -> a n", a=1).broadcast_to([P, D])).then_inc(s["loaded_biases"], 16)
            sp.dma_start(eb[:, :, :].rearrange("p e d -> p (e d)"),
                         expert_b.rearrange("e d -> (e d)").rearrange("(a n) -> a n", a=1).broadcast_to([P, NE * D])
                         ).then_inc(s["loaded_biases"], 16)
            for e in range(NE // 2, NE):
                load_expert(e)
            for i, done in enumerate(sent):
                sp.wait_ge(done, 16 * SEL * len(range(i, NT, 4)))
            sp.dma_start(ow[:, :, :], out_w.rearrange("(k p) d -> p k d", p=P)).then_inc(s["loaded_out_w"], 16)

            def load_slots(i, u, first):
                if not first:
                    sp.wait_ge(s["pe_slot_turned"], i - 1)
                sp.dma_start(rows[:, u % 2, :], x_slots.rearrange("(i p) d -> i p d", p=P)[i]).then_inc(ld_xs[u % 2], 16)

            load_slots(0, 0, True)
            load_slots(1, 1, True)
            with sp.Fori(1, SLOTS // 2) as k:
                for u in range(2):
                    load_slots(2 * k + u, u, False)
            for t in range(TILES + 1):
                sp.wait_ge(s["dve_out"], t + 1)
                if t < TILES:
                    st = t // NB
                    sp.dma_start(out[t % NB, 1 + st * P:1 + st * P + P, :], tok[:, t, :]).then_inc(s["stored_out"], 16)
                else:
                    sp.dma_start(out[:, 0, :], tok[0:NB, CLS, :]).then_inc(s["stored_out"], 16)
            sp.wait_ge(s["stored_out"], (TILES + 1) * 16)

        @block.gpsimd
        def _(pool):
            pool.memset(tok[:, CLS, :], 0.0).then_inc(s["pool_cls_zeroed"], 1)
            nc.gpsimd.memset(ident[:, :], 0.0).then_inc(s["pool_identity"], 1)
            pool.wait_ge(s["pool_identity"], 1)
            nc.gpsimd.affine_select(out=ident[:, :], in_=ident[:, :], compare_op=ALU.not_equal, fill=1.0, base=0,
                                    pattern=[[-1, P]], channel_multiplier=1).then_inc(s["pool_identity"], 1)
            n_chain = [0]

            def put(ins):
                n_chain[0] += 1
                ins.then_inc(s["pool_power_step"], 1)

            def settle():
                pool.wait_ge(s["pool_power_step"], n_chain[0])

            def pool_powers():
                tre, tim = prm[:, 4, 1, :], prm[:, 5, 1, :]
                put(pool.tensor_copy(zs2[:, 0, 0, :], prm[:, 0, 1, :]))
                put(pool.tensor_copy(zs2[:, 0, 1, :], prm[:, 6, 1, :]))
                for k in range(9):
                    zr, zi = zs2[:, k, 0, :], zs2[:, k, 1, :]
                    settle()
                    put(pool.tensor_scalar(zt2[:, k, 0, :], zi, -1.0, None, ALU.mult))
                    put(pool.tensor_copy(zt2[:, k, 1, :], zr))
                    if k < 8:
                        put(pool.tensor_tensor(zs2[:, k + 1, 1, :], zr, zi, ALU.mult))
                        put(pool.tensor_tensor(tre, zr, zr, ALU.mult))
                        put(pool.tensor_tensor(tim, zi, zi, ALU.mult))
                        settle()
                        put(pool.tensor_tensor(zs2[:, k + 1, 1, :], zs2[:, k + 1, 1, :], zs2[:, k + 1, 1, :], ALU.add))
                        put(pool.tensor_tensor(zs2[:, k + 1, 0, :], tre, tim, ALU.subtract))
                put(pool.memset(r_low2[:, 0, 0, :], 1.0))
                put(pool.memset(r_low2[:, 0, 1, :], 0.0))
                put(pool.tensor_copy(r_low2[:, 1, :, :], zs2[:, 0, :, :]))
                for lv in range(1, 5):
                    n = 1 << lv
                    for m0 in range(0, n, PIECE):
                        m = min(n, PIECE)
                        shape = [P, m, 2, NS]
                        new = r_low2[:, n + m0:n + m0 + m]
                        settle()
                        put(pool.tensor_tensor(new, bc(r_low2[:, m0:m0 + m, 0:1, :], shape),
                                               bc(zs2[:, lv, :, :].unsqueeze(1), shape), ALU.mult))
                        put(pool.tensor_tensor(ptmp[:, 0:m], bc(r_low2[:, m0:m0 + m, 1:2, :], shape),
                                               bc(zt2[:, lv, :, :].unsqueeze(1), shape), ALU.mult))
                        settle()
                        put(pool.tensor_tensor(new, new, ptmp[:, 0:m], ALU.add))
                assert n_chain[0] == CHAIN

            for hf in range(HALVES):
                pool.wait_ge(s["loaded_x0" if hf == 0 else "loaded_x1"], 16)
                if hf == 0:
                    pool.wait_ge(s["dve_z_ready"], 1)
                else:
                    pool.wait_ge(s["dve_l_product"], NB)
                xr, xi = x_in[:, :, :, 0], x_in[:, :, :, 1]
                gr = bc(g[:, hf, 0, :].unsqueeze(1), [P, NB, NS])
                gi = bc(g[:, hf, 1, :].unsqueeze(1), [P, NB, NS])
                base = 6 * hf
                cr, cim = coef[:, :, 0, :], coef[:, :, 1, :]
                pool.tensor_tensor(ctmp[:, :, :], xi, gi, ALU.mult).then_inc(s["pool_step"], 1)
                pool.tensor_tensor(cr, xr, gr, ALU.mult).then_inc(s["pool_step"], 1)
                pool.wait_ge(s["pool_step"], base + 2)
                pool.tensor_tensor(cr, cr, ctmp[:, :, :], ALU.subtract).then_inc(s["pool_step"], 1)
                pool.wait_ge(s["pool_step"], base + 3)
                pool.tensor_tensor(ctmp[:, :, :], xi, gr, ALU.mult).then_inc(s["pool_step"], 1)
                pool.tensor_tensor(cim, xr, gi, ALU.mult).then_inc(s["pool_step"], 1)
                pool.wait_ge(s["pool_step"], base + 5)
                pool.tensor_tensor(cim, cim, ctmp[:, :, :], ALU.add).then_inc(s["pool_step"], 1)
                pool.wait_ge(s["pool_step"], base + 6)
                pool.tensor_copy(ctmp[:, 0, 0:1], ident[:, 0:1]).then_inc(s["pool_coef"], 1)

                if hf == 0:
                    pool_powers()

            pool.wait_ge(s["pe_tokens"], HALVES * NHB)
            for row in s_row:
                pool.wait_ge(row, 16 * NHB // 2 * HALVES)
            pool.memset(mhalf[:, :], -0.5).then_inc(s["pool_constants"], 1)
            def ln_pow(n):
                pool.wait_ge(s["dve_ln_step"], n * 5 + 5)
                pool.tensor_tensor(lnr[:, 1, :], lnr[:, 0, :], mhalf[:, :], ALU.pow).then_inc(s["pool_step"], 1)

            pool.wait_ge(s["pool_constants"], 1)
            ln_pow(0)
            pool.memset(ones[:, :, :], 1.0).then_inc(s["pool_filled"], 1)
            pool.memset(mask[:, :, :], 1.0).then_inc(s["pool_filled"], 1)
            pool.memset(pclsT[:, :], 0.0).then_inc(s["pool_filled"], 1)
            pool.memset(pccT[:, :], 0.0).then_inc(s["pool_filled"], 1)
            pool.memset(e16[:, :], 0.0).then_inc(s["pool_filled"], 1)
            pool.memset(u_sb[:, :], 0.0).then_inc(s["pool_filled"], 1)
            pool.wait_ge(s["pool_filled"], 6)
            pool.affine_select(out=mask[:, :, :], in_=mask[:, :, :], compare_op=ALU.is_ge, fill=0.0, base=0,
                               pattern=[[P, KC], [-DH, P]], channel_multiplier=1).then_inc(s["pool_mask_half"], 1)
            for t, n in ((pclsT, BODY), (pccT, P)):
                pool.affine_select(out=t[:, :], in_=t[:, :], compare_op=ALU.not_equal, fill=1.0, base=-NHEAD,
                                   pattern=[[0, n]], channel_multiplier=1).then_inc(s["pool_constants"], 1)
            pool.memset(e16[:, NHEAD:NHEAD + 1], 1.0).then_inc(s["pool_constants"], 1)
            pool.wait_ge(s["pool_mask_half"], 1)
            pool.affine_select(out=mask[:, :, :], in_=mask[:, :, :], compare_op=ALU.is_ge, fill=0.0, base=DH - 1,
                               pattern=[[-P, KC], [DH, P]], channel_multiplier=-1).then_inc(s["pool_head_mask"], 1)

            for part in (q_hi, q_lo):
                pool.memset(part[:, :, :].bitcast(F32), 0.0).then_inc(s["pool_q_zeroed"], 1)
            ln_pow(1)
            pool.memset(zero_row[:, :], 0.0).then_inc(s["pool_zero_row"], 1)

            def keep_cls(c, j):
                pool.wait_ge(s["dve_normed"], c * NHEAD + j + 1)
                column = prb[:, j % 4, :, BODY]
                pool.tensor_tensor(pcls[:, :, j], column, ones[:, :, 0], ALU.mult).then_inc(s["pool_key_col"], 1)

            def cls_cols(c, gr):
                if gr == 0:
                    pool.wait_ge(s["dve_cls_pT"], c + 1)
                column = ptc[:, :, gr * HPC:(gr + 1) * HPC].rearrange("p t h -> p h t")
                pool.tensor_tensor(pts[:, (gr * HPC) % 8:(gr * HPC) % 8 + HPC, :, BODY], column, ones[:, :, :].rearrange("p t h -> p h t"), ALU.mult
                                   ).then_inc(s["pool_cls_cols"], 1)

            def body(c, first, last):
                for j in range(NHEAD):
                    if j == 1:
                        if not first:
                            pool.wait_ge(s["pe_key_turned"], c)
                    if j >= 1:
                        keep_cls(c, j - 1)
                    if j == 4:
                        if not first:
                            pool.wait_ge(s["pe_pv"], c * KC)
                        cls_cols(c, 0)
                        cls_cols(c, 1)
                        if not last:
                            ln_pow(c + 2)
                    if j == 11:
                        pool.wait_ge(s["pe_pv"], c * KC + 1)
                        cls_cols(c, 2)
                    if j == 15:
                        pool.wait_ge(s["pe_pv"], c * KC + 2)
                        cls_cols(c, 3)
                keep_cls(c, NHEAD - 1)

            body(0, True, False)
            with pool.Fori(1, NB - 1) as c:
                body(c, False, False)
            body(NB - 1, False, True)
            pool.wait_ge(s["dve_attn_done"], 1)
            pool.memset(mh2[:, :], -0.5).then_inc(s["pool_routing_const"], 1)
            for table, step, n in ((iota_e, 1, NE), (iota_s, 1, SLOTS)):
                pool.iota(table[:, :], pattern=[[step, n]], base=0, channel_multiplier=0,
                          allow_small_or_imprecise_dtypes=True).then_inc(s["pool_routing_const"], 1)
            pool.iota(spare[:, :], pattern=[[P, SEL]], base=SLOTS * P, channel_multiplier=1,
                      allow_small_or_imprecise_dtypes=True).then_inc(s["pool_routing_const"], 1)
            for table in (before, all_one, valid):
                pool.memset(table[:, :], 1.0).then_inc(s["pool_routing_const"], 1)
            pool.wait_ge(s["pool_routing_const"], 7)
            pool.affine_select(out=before[:, :], in_=before[:, :], compare_op=ALU.is_ge, fill=0.0, base=-1,
                               pattern=[[1, P]], channel_multiplier=-1).then_inc(s["pool_routing_const"], 1)
            pool.affine_select(out=valid[:, :], in_=valid[:, :], compare_op=ALU.is_ge, fill=0.0, base=NB - 1,
                               pattern=[[0, 1]], channel_multiplier=-1).then_inc(s["pool_routing_const"], 1)
            pool.affine_select(out=spare[:, :], in_=spare[:, :], compare_op=ALU.is_ge, fill=0.0, base=-NB,
                               pattern=[[0, SEL]], channel_multiplier=1).then_inc(s["pool_routing_const"], 1)
            pool.wait_ge(s["dve_stats2"], 2 * NT + 1)
            pool.tensor_tensor(rstd[:, :], rstd[:, :], mh2[:, :], ALU.pow).then_inc(s["pool_rstd"], 1)
            pool.wait_ge(s["stored_zeros"], 32)
            pool.wait_ge(s["dve_route_step"], ROUTE_STEPS)
            for t in range(NT):
                pool.wait_ge(s["dve_row_ready"], t + 1)
                for k in range(SEL):
                    pool.indirect_dma_start(
                        out=x_slots,
                        out_offset=bass.IndirectOffsetOnAxis(ap=slot_of[:, SEL * t + k:SEL * t + k + 1], axis=0),
                        in_=rows[:, t % 4, :], in_offset=None).then_inc(sent[t % 4], 16)
            pool.wait_ge(s["loaded_biases"], 32)
            with pool.Fori(0, NT) as t:
                pool.tensor_tensor(tok[:, t, :], tok[:, t, :], ob[:, :], ALU.add).then_inc(s["pool_out_bias"], 1)
            for done in st_y:
                pool.wait_ge(done, 16 * SLOTS // 2)
            for t in range(NT):
                if t >= 2:
                    pool.wait_ge(s["dve_combined"], 2 * (t - 1))
                for k in range(SEL):
                    pool.indirect_dma_start(
                        out=rows[:, 2 * (t % 2) + k, :], out_offset=None, in_=y_slots,
                        in_offset=bass.IndirectOffsetOnAxis(ap=slot_of[:, SEL * t + k:SEL * t + k + 1], axis=0)
                        ).then_inc(got_y[t % 2], 16)

        @block.scalar
        def _(act):
            act.wait_ge(s["loaded_ssm"], 64)
            act.activation(prm[:, 0, :, :], iar[:, :, :], ACT.Exp).then_inc(s["act_exp_params"], 1)
            act.activation(dt2[:, 0, :], ldt[:, :], ACT.Exp).then_inc(s["act_exp_params"], 1)
            act.wait_ge(s["dve_angles"], 2)
            act.activation(k_scale[:, :], rcol[:, 2, :], ACT.Sin).then_inc(s["act_sines"], 1)
            act.activation(rcol[:, 0, :], rcol[:, 3, :], ACT.Sin).then_inc(s["act_sines"], 1)

            def w_scale(raw, scale):
                for o in range(KC):
                    act.activation(raw[:, o, :], raw[:, o, :], ACT.Copy, scale=scale[:, o:o + 1]
                                   ).then_inc(s["act_w_scaled"], 1)

            def w_hi(dst, sem_hi, sem_t, n, bank0):
                for ic in range(KC):
                    act.wait_ge(s[sem_t], n * KC + ic + 1)
                    act.activation(dst[:, ic, :], ps[:, bank0 + ic, :], ACT.Copy).then_inc(s[sem_hi], 1)

            act.wait_ge(s["loaded_wq"], 16)
            act.wait_ge(s["dve_angles"], 4)
            w_scale(w_raw[:, 0], q_scale)
            w_hi(wqT_hi, "act_w_high", "pe_w_turned", 0, 4)
            act.wait_ge(s["loaded_wk"], 16)
            w_scale(w_raw[:, 1], k_scale)
            w_hi(wkT_hi, "act_w_high", "pe_w_turned", 1, 4)

            def turned(n, dst, col):
                act.wait_ge(s["pe_table_turned"], n + 1)
                act.activation(dst[:, :, col:col + 4], ps[:, n % 4, :].rearrange("p (q h) -> p h q", q=4),
                               ACT.Copy).then_inc(s["act_table_kept"], 1)

            for hf in range(HALVES):
                base = hf * 32
                if hf == 1:
                    act.wait_ge(s["pe_tokens"], NHB)
                for q in range(16):
                    turned(base + q, rT, 4 * q)
                for c in range(NB):
                    for k in range(2):
                        turned(base + 16 + 2 * c + k, lT, c * NA + 4 * k)
                for hb in range(NHB):
                    n = hf * NHB + hb
                    act.wait_ge(s["pe_tokens"], n + 1)
                    if n >= 2:
                        act.wait_ge(s_row[n % 2], 16 * (n // 2))
                    for k in range(2):
                        e = act.activation(so[:, n % 2, k * BANK:(k + 1) * BANK], ps[:, 4 + 2 * (n % 2) + k, :], ACT.Copy)
                    e.then_inc(s["act_tokens_kept"], 1)

            def hi_xT(n, bank, st):
                act.wait_ge(s["pe_x_turned"], n + 1)
                act.activation(xT_hi[:, :, st * P:st * P + P], ps[:, bank, :].rearrange("p (k t) -> p k t", k=KC),
                               ACT.Copy).then_inc(s["act_xT_high"], 1)

            for row in s_row:
                act.wait_ge(row, 16 * NHB // 2 * HALVES)
            act.wait_ge(s["pe_x_turned"], 1)
            act.activation(xT_hi[:, :, BODY:KPAD], ps[:, 7, 0:KC * NB].rearrange("p (k t) -> p k t", k=KC)[:, :, 0:2],
                           ACT.Copy).then_inc(s["act_xT_high"], 1)
            for i, dst in enumerate((wvT_hi, woT_hi)):
                w_hi(dst, "act_wvo_high", "pe_wvo_turned", i, 0)
            hi_xT(1, 6, 0)
            hi_xT(2, 7, 1)

            def hi_qk(c, m, first=False):
                ci, bank = m // 2, FIRST_BANKS[m] if first else 6 + m % 2
                act.wait_ge(s["pe_qk"], c * 2 * KC + m + 1)
                if m % 2 == 0:
                    for j in range(HPC):
                        rows = slice(j * DH, (j + 1) * DH)
                        e = act.activation(q_hi[rows, ci * HPC + j, :], ps[rows, bank, 0:BODY], ACT.Identity,
                                           bias=q_bias[rows, ci:ci + 1])
                    if first:
                        e = act.activation(qcls_hi[:, ci, :], ps[:, bank, BODY:KPAD], ACT.Identity,
                                           bias=q_bias[:, ci:ci + 1])
                else:
                    e = act.activation(k_hi[:, ci, :], ps[:, bank, 0:KPAD], ACT.Identity, bias=k_bias[:, ci:ci + 1])
                e.then_inc(s["act_qk_high"], 1)

            act.wait_ge(s["pool_q_zeroed"], 2)
            for m in range(2 * KC):
                hi_qk(0, m, True)
            def exp_unit(c, j):
                act.wait_ge(s["dve_max"], c * NHEAD + j + 1)
                for st in range(HALVES):
                    e = act.activation(prb[:, j % 4, st, 0:KEYS], ps[:, 2 * (j % 2) + st, 0:KEYS], ACT.Exp,
                                       bias=negmax[:, j % 4, st:st + 1], accum_out=rowsum[:, j % 4, st:st + 1])
                e.then_inc(s["act_exp"], 1)

            def keep_pt(c, j):
                act.wait_ge(s["pe_p_turned"], c * NHEAD + j + 1)
                act.activation(pts[:, j % 8, :, 0:BODY], ps[:, 4, :].rearrange("p (t s) -> p t s", t=2),
                               ACT.Copy).then_inc(s["act_pT_kept"], 1)

            def keep_v(c, st):
                act.wait_ge(s["pe_values"], c * HALVES + st + 1)
                act.activation(v_sb[:, st, :], ps[:, 7, :], ACT.Copy).then_inc(s["act_v_kept"], 1)

            def hi_ot(c, gr):
                act.wait_ge(s["pe_pv"], c * KC + gr + 1)
                act.activation(oT_hi[:, gr, :], ps[:, 5, 0:BODY], ACT.Copy).then_inc(s["act_oT_high"], 1)

            def body(c, first, last):
                for j in range(NHEAD):
                    if j >= 4 or not first:
                        act.wait_ge(s["pe_p_turned"], c * NHEAD + j - 3)
                        act.wait_ge(s["pool_key_col"], c * NHEAD + j - 3)
                    for m in QK_SLOT[j - 1] if j >= 1 and not last else ():
                        hi_qk(c + 1, m)
                    for m in QK_SLOT[NHEAD - 1] if j == 0 and not first else ():
                        hi_qk(c, m)
                    if j == 3 and not first:
                        hi_ot(c - 1, 3)
                    if j == 4:
                        keep_v(c, 1)
                    if j in (7, 11, 15):
                        if j == 7 and not first:
                            act.wait_ge(s["pe_projected"], c * HALVES)
                        hi_ot(c, (j - 7) // 4)
                    exp_unit(c, j)
                    if j >= 2:
                        if j == 2 and not first:
                            act.wait_ge(s["pe_pv"], c * KC - 1)
                        if j == 10:
                            act.wait_ge(s["pe_pv"], c * KC + 1)
                        if j == 14:
                            act.wait_ge(s["pe_pv"], c * KC + 2)
                        keep_pt(c, j - 2)
                    elif not first:
                        keep_pt(c - 1, NHEAD - 2 + j)
                    if j == 8 and not last:
                        act.wait_ge(s["pe_values"], (c + 1) * HALVES)
                        hi_xT((c + 1) * HALVES + 1, 6, 0)
                        hi_xT((c + 1) * HALVES + 2, 7, 1)
                    if j == 1:
                        act.wait_ge(s["dve_cls_max"], c + 1)
                        act.activation(pc[:, 0:KEYS], ps[0:NHEAD, 6, 0:KEYS], ACT.Exp, bias=cstat[:, 0:1],
                                       accum_out=cstat[:, 1:2]).then_inc(s["act_cls_exp"], 1)
                    if j == 2:
                        if not first:
                            act.wait_ge(s["pe_pv"], c * KC)
                        keep_v(c, 0)


            body(0, True, False)
            with act.Fori(1, NB - 1) as c:
                body(c, False, False)
            body(NB - 1, False, True)
            last = NB - 1
            keep_pt(last, NHEAD - 2)
            keep_pt(last, NHEAD - 1)
            hi_ot(last, 3)
            act.wait_ge(s["dve_attn_done"], 1)
            act.wait_ge(s["loaded_router"], 32)
            act.activation(rw_parts[:, :, 0, :], rw[:, :, :], ACT.Copy).then_inc(s["act_router_high"], 1)

            def hi_expert(e):
                act.wait_ge(ld_ew[e], 16)
                act.activation(ew_hi[:, e, :, :], ew[:, e, :, :], ACT.Copy).then_inc(s["act_expert_high"], 1)

            def hi_turned(bank, u, done):
                act.activation(xnT_hi[:, u, :, :], ps[:, bank, :].rearrange("p (k t) -> p k t", k=KC), ACT.Copy
                               ).then_inc(s[done], 1)

            def hi_xn(t, u, first):
                act.wait_ge(s["pe_xn_turned"], t + 1)
                if not first:
                    act.wait_ge(s["pe_logits"], t - 1)
                hi_turned(4 + u, u, "act_xnT_high")

            tiles_in_pairs(act, hi_xn)
            act.wait_ge(s["dve_route_step"], 4)
            act.activation(probs[:, :, :], probs[:, :, :], ACT.Exp).then_inc(s["act_route_exp"], 1)
            for e in range(NE):
                hi_expert(e)

            def hi_xs(i, u, first):
                act.wait_ge(s["pe_slot_turned"], i + 1)
                if not first:
                    act.wait_ge(s["pe_expert"], i - 1)
                hi_turned(4 + u % 2, u % 2, "act_slotT_high")

            def gelu(i, u, first):
                act.wait_ge(s["dve_bias_added"], i + 1)
                if not first:
                    act.wait_ge(st_y[u % 2], 8 * (i - u))
                act.activation(rows[:, 2 + u % 2, :], ps[:, u, :], ACT.Gelu_apprx_tanh).then_inc(s["act_gelu"], 1)

            def store_slots(i, u):
                act.wait_ge(s["act_gelu"], i + 1)
                act.dma_start(y_slots.rearrange("(i p) d -> i p d", p=P)[i], rows[:, 2 + u % 2, :]
                              ).then_inc(st_y[u % 2], 16)

            hi_xs(0, 0, True)
            hi_xs(1, 1, True)
            gelu(0, 0, True)
            hi_xs(2, 0, False)
            store_slots(0, 0)
            gelu(1, 1, True)
            with act.Fori(1, SLOTS // 2 - 1) as k:
                for u in range(2):
                    hi_xs(2 * k + u + 1, u + 1, False)
                    store_slots(2 * k + u - 1, u + 1)
                    gelu(2 * k + u, u, False)
            hi_xs(SLOTS - 1, 1, False)
            store_slots(SLOTS - 3, 1)
            gelu(SLOTS - 2, 0, False)
            store_slots(SLOTS - 2, 0)
            gelu(SLOTS - 1, 1, False)
            store_slots(SLOTS - 1, 1)
            act.wait_ge(s["loaded_out_w"], 16)
            act.wait_ge(s["pe_expert"], SLOTS)
            act.activation(ow_hi[:, :, :], ow[:, :, :], ACT.Copy).then_inc(s["act_out_w_high"], 1)

            def keep_combT(t, u, first):
                act.wait_ge(s["pe_comb_turned"], t + 1)
                if not first:
                    act.wait_ge(s["pe_out"], t - 1)
                act.activation(combT_hi[:, u, :, :], ps[:, 4 + u, :].rearrange("p (k t) -> p k t", k=KC), ACT.Copy
                               ).then_inc(s["act_combT_high"], 1)

            tiles_in_pairs(act, keep_combT)

        @block.vector
        def _(dve):
            n_par = [0]

            def link(ins):
                n_par[0] += 1
                ins.then_inc(s["dve_param_step"], 1)
                dve.wait_ge(s["dve_param_step"], n_par[0])

            dve.wait_ge(s["act_exp_params"], 2)
            link(dve.tensor_scalar(dt2[:, 1, :], dt2[:, 0, :], 0.5, None, ALU.mult))
            e_, q1, v_, inv, t0, t1, om = (prm[:, i, :, :] for i in range(7))
            for hf in range(HALVES):
                dve.tensor_scalar(e_[:, hf, :], e_[:, hf, :], dt2[:, 1, hf:hf + 1], None, ALU.mult).then_inc(s["dve_param_step"], 1)
                dve.tensor_scalar(v_[:, hf, :], aim[:, hf, :], dt2[:, 1, hf:hf + 1], None, ALU.mult).then_inc(s["dve_param_step"], 1)
            n_par[0] += 4
            dve.wait_ge(s["dve_param_step"], n_par[0])
            link(dve.tensor_scalar(q1, e_, 1.0, None, ALU.add))
            link(dve.tensor_scalar(om, e_, -1.0, 1.0, ALU.mult, ALU.add))
            link(dve.tensor_tensor(t0, v_, v_, ALU.mult))
            link(dve.tensor_tensor(t1, q1, q1, ALU.mult))
            link(dve.tensor_tensor(t1, t1, t0, ALU.add))
            link(dve.reciprocal(inv, t1))
            link(dve.tensor_tensor(t1, om, q1, ALU.mult))
            link(dve.tensor_tensor(t1, t1, t0, ALU.subtract))
            link(dve.tensor_tensor(e_, t1, inv, ALU.mult))
            link(dve.scalar_tensor_tensor(out=om, in0=v_, scalar=2.0, in1=inv, op0=ALU.mult, op1=ALU.mult))
            br, bi = b_in[:, :, :, 0], b_in[:, :, :, 1]
            for hf in range(HALVES):
                link(dve.tensor_scalar(inv[:, hf, :], inv[:, hf, :], dt2[:, 0, hf:hf + 1], 2.0, ALU.mult, ALU.mult))
            link(dve.tensor_tensor(t0, br, q1, ALU.mult))
            link(dve.tensor_tensor(t1, bi, v_, ALU.mult))
            link(dve.tensor_tensor(t0, t0, t1, ALU.subtract))
            link(dve.tensor_tensor(g[:, :, 0, :], t0, inv, ALU.mult))
            link(dve.tensor_tensor(t0, br, v_, ALU.mult))
            link(dve.tensor_tensor(t1, bi, q1, ALU.mult))
            link(dve.tensor_tensor(t0, t0, t1, ALU.add))
            dve.tensor_tensor(g[:, :, 1, :], t0, inv, ALU.mult).then_inc(s["dve_z_ready"], 1)

            dve.wait_ge(s["loaded_vectors"], 16 * (4 + HPC))
            for i, (dst, shift) in enumerate(((2, 0.0), (3, 0.25))):
                t = prm[:, 7, 0, i * 16:i * 16 + KC]
                link(dve.tensor_scalar(t, rcol[:, 0, :], 1.0 / (TWO_PI_HI + TWO_PI_LO), shift, ALU.mult, ALU.add))
                link(dve.tensor_scalar(t, t, ROUND_MAGIC, ROUND_MAGIC, ALU.add, ALU.subtract))
                link(dve.scalar_tensor_tensor(out=rcol[:, dst, :], in0=t, scalar=-TWO_PI_HI, in1=rcol[:, 0, :],
                                              op0=ALU.mult, op1=ALU.add))
                link(dve.scalar_tensor_tensor(out=rcol[:, dst, :], in0=t, scalar=-TWO_PI_LO, in1=rcol[:, dst, :],
                                              op0=ALU.mult, op1=ALU.add))
                link(dve.tensor_scalar(rcol[:, dst, :], rcol[:, dst, :], 4 * shift * 1.5707963267948966, None, ALU.add))
                dve.tensor_scalar(rcol[:, dst, :], rcol[:, dst, :], PI_SAFE, -PI_SAFE, ALU.min, ALU.max
                                  ).then_inc(s["dve_angles"], 1)
            dve.wait_ge(s["act_sines"], 2)
            link(dve.scalar_tensor_tensor(out=q_scale[:, :], in0=rcol[:, 0, :], scalar=float(DH) ** -0.5,
                                          in1=rcol[:, 1, :], op0=ALU.mult, op1=ALU.mult))
            dve.tensor_tensor(q_bias[:, :], q_bias[:, :], q_scale[:, :], ALU.mult).then_inc(s["dve_angles"], 1)
            dve.tensor_tensor(k_bias[:, :], k_bias[:, :], k_scale[:, :], ALU.mult).then_inc(s["dve_angles"], 1)

            def w_lo(dst, hi, sem_hi, sem_lo, n, bank0):
                for ic in range(KC):
                    dve.wait_ge(s[sem_hi], n * KC + ic + 1)
                    dve.tensor_tensor(dst[:, ic, :], ps[:, bank0 + ic, :], hi[:, ic, :].bitcast(F32), ALU.subtract
                                      ).then_inc(s[sem_lo], 1)

            n_pow = [0]

            def put(ins):
                n_pow[0] += 1
                ins.then_inc(s["dve_power_step"], 1)

            def settle():
                dve.wait_ge(s["dve_power_step"], n_pow[0])

            for hf in range(HALVES):
                low = r_low if hf == 0 else r_low2
                if hf == 0:
                    put(dve.tensor_copy(zs[:, 0, 0, :], e_[:, hf, :]))
                    put(dve.tensor_copy(zs[:, 0, 1, :], om[:, hf, :]))
                    for k in range(9):
                        zr, zi = zs[:, k, 0, :], zs[:, k, 1, :]
                        settle()
                        if k < 8:
                            put(dve.tensor_tensor(t0[:, 0, :], zr, zr, ALU.mult))
                            put(dve.tensor_tensor(t1[:, 0, :], zi, zi, ALU.mult))
                            put(dve.scalar_tensor_tensor(out=zs[:, k + 1, 1, :], in0=zr, scalar=2.0, in1=zi,
                                                         op0=ALU.mult, op1=ALU.mult))
                        put(dve.tensor_scalar(zt[:, k, 0, :], zi, -1.0, None, ALU.mult))
                        put(dve.tensor_copy(zt[:, k, 1, :], zr))
                        if k < 8:
                            dve.wait_ge(s["dve_power_step"], n_pow[0] - 3)
                            put(dve.tensor_tensor(zs[:, k + 1, 0, :], t0[:, 0, :], t1[:, 0, :], ALU.subtract))
                    settle()
                    w_lo(wqT_lo, wqT_hi, "act_w_high", "dve_w_low", 0, 4)
                else:
                    dve.wait_ge(s["pool_power_step"], CHAIN)
                    settle()
                    put(dve.tensor_copy(zs[:, :, :, :], zs2))
                    put(dve.tensor_copy(zt[:, :, :, :], zt2))
                    settle()
                    dve.memset(t0[:, 0, 0:1], 0.0).then_inc(s["dve_powers_copied"], 1)

                def doubled(dst, n, k, tmp):
                    shape = [P, n, 2, NS]
                    put(dve.tensor_tensor(dst[:, n:2 * n], bc(dst[:, 0:n, 0:1, :], shape),
                                          bc(zs[:, k, :, :].unsqueeze(1), shape), ALU.mult))
                    put(dve.tensor_tensor(tmp, bc(dst[:, 0:n, 1:2, :], shape),
                                          bc(zt[:, k, :, :].unsqueeze(1), shape), ALU.mult))
                    settle()
                    put(dve.tensor_tensor(dst[:, n:2 * n], dst[:, n:2 * n], tmp, ALU.add))
                    settle()

                if hf == 1:
                    dve.wait_ge(s["pe_table_turned"], 32)
                ring_flat = ring[:, 0, :, :, :, :].rearrange("p a b s n -> p (a b) s n")
                for dst, k0, levels in ((r_low, 0, 5), (w_pow, 6, 3))[hf:]:
                    put(dve.memset(dst[:, 0, 0, :], 1.0))
                    put(dve.memset(dst[:, 0, 1, :], 0.0))
                    put(dve.tensor_copy(dst[:, 1, :, :], zs[:, k0, :, :]))
                    settle()
                    for lv in range(1, levels):
                        doubled(dst, 1 << lv, k0 + lv, ring_flat[:, 0:1 << lv])
                    if dst is r_low:
                        dve.memset(t0[:, 0, 0:1], 0.0).then_inc(s["dve_r_low"], 1)
                put(dve.tensor_scalar(w_b[:, :, 0, :], w_pow[:, :, 1, :], -1.0, None, ALU.mult))
                put(dve.tensor_scalar(w_b[:, :, 1, :], w_pow[:, :, 0, :], -1.0, None, ALU.mult))
                settle()
                put(dve.tensor_scalar(w_pow[:, :, 1, :], w_pow[:, :, 1, :], -1.0, None, ALU.mult))
                settle()
                shape = [P, PIECE, 2, NS]
                for q in range(4):
                    n = hf * 12 + q
                    if q >= 2:
                        dve.wait_ge(s["pe_table_turned"], hf * 32 + 8 + 2 * (q - 1))
                    dve.tensor_tensor(ring[:, n % 2, 0], bc(low[:, 8 * q:8 * q + 8, 0:1, :], shape),
                                      bc(zs[:, 5, :, :].unsqueeze(1), shape), ALU.mult)
                    dve.tensor_tensor(ring[:, n % 2, 1], bc(low[:, 8 * q:8 * q + 8, 1:2, :], shape),
                                      bc(zt[:, 5, :, :].unsqueeze(1), shape), ALU.mult).then_inc(s["dve_r_upper"], 1)
                dve.wait_ge(s["pool_coef"], hf + 1)
                for c in range(NB):
                    n = hf * 12 + 4 + c
                    dve.wait_ge(s["pe_table_turned"], hf * 32 + 8 + 2 * (4 + c - 1))
                    dve.tensor_tensor(ring[:, n % 2, 0], bc(coef[:, c, 0:1, :].unsqueeze(1), shape), w_pow[:, :, :, :],
                                      ALU.mult)
                    dve.tensor_tensor(ring[:, n % 2, 1], bc(coef[:, c, 1:2, :].unsqueeze(1), shape), w_b[:, :, :, :],
                                      ALU.mult).then_inc(s["dve_l_product"], 1)
                if hf == 0:
                    w_lo(wkT_lo, wkT_hi, "act_w_high", "dve_w_low", 1, 4)
            for row in s_row:
                dve.wait_ge(row, 16 * NHB // 2 * HALVES)
            dve.wait_ge(s["pe_tokens"], HALVES * NHB)

            def ln(n, tiles, rows):
                for i, t in enumerate(tiles):
                    dve.bn_stats(lnst[0:rows, i, :], tok[0:rows, t, :]).then_inc(s["dve_ln_step"], 1)
                for i in range(2):
                    dve.wait_ge(s["dve_ln_step"], n * 5 + 2)
                    dve.bn_aggr(lnmv[0:rows, i, :], lnst[0:rows, i, :]).then_inc(s["dve_ln_step"], 1)
                dve.wait_ge(s["dve_ln_step"], n * 5 + 4)
                dve.tensor_scalar(lnr[0:rows, 0, :], lnmv[0:rows, :, 1], EPS, None, ALU.add).then_inc(s["dve_ln_step"], 1)

            def ln_apply(n, tiles, rows):
                dve.wait_ge(s["pool_step"], 12 + n + 1)
                for i, t in enumerate(tiles):
                    dve.tensor_scalar(xhat[0:rows, i, :], tok[0:rows, t, :], lnmv[0:rows, i, 0:1],
                                      lnr[0:rows, 1, i:i + 1], ALU.subtract, ALU.mult).then_inc(s["dve_xhat"], 1)

            dve.wait_ge(s["loaded_cls"], 16)
            dve.memset(lnr[:, 0, :], 1.0).then_inc(s["dve_spread"], 1)
            dve.wait_ge(s["dve_spread"], 1)
            ln(0, (CLS, CLS), NB)
            ln_apply(0, (CLS, CLS), NB)
            dve.wait_ge(s["act_xT_high"], 1)
            dve.tensor_tensor(xT_lo[:, :, BODY:KPAD],
                              ps[:, 7, 0:KC * NB].rearrange("p (k t) -> p k t", k=KC)[:, :, 0:2],
                              xT_hi[:, :, BODY:KPAD].bitcast(F32), ALU.subtract).then_inc(s["dve_xT_low"], 1)
            for i, (dst, hi) in enumerate(((wvT_lo, wvT_hi), (woT_lo, woT_hi))):
                w_lo(dst, hi, "act_wvo_high", "dve_wvo_low", i, 0)
            dve.wait_ge(s["pool_head_mask"], 1)
            dve.wait_ge(s["pe_cls_value"], 1)
            for ci in range(KC):
                dve.tensor_scalar(vblk_hi[:, ci, :], mask[:, ci, :], ps[:, 4, 2 * ci:2 * ci + 1], None, ALU.mult
                                  ).then_inc(s["dve_cls_value"], 1)
            dve.wait_ge(s["dve_cls_value"], KC)
            for ci in range(KC):
                dve.scalar_tensor_tensor(out=vblk_lo[:, ci, :], in0=mask[:, ci, :], scalar=ps[:, 4, 2 * ci:2 * ci + 1],
                                         in1=vblk_hi[:, ci, :].bitcast(F32), op0=ALU.mult, op1=ALU.subtract
                                         ).then_inc(s["dve_cls_value"], 1)
            dve.wait_ge(s["dve_cls_value"], 2 * KC)
            bias_hi, bias_lo = (part[:, :, NHEAD:NHEAD + 1] for part in (vblk_hi, vblk_lo))
            dve.tensor_copy(bias_hi, bv_col[:, :].unsqueeze(2)).then_inc(s["dve_cls_value"], 1)
            dve.wait_ge(s["dve_cls_value"], 2 * KC + 1)
            dve.tensor_tensor(bias_lo, bv_col[:, :].unsqueeze(2), bias_hi.bitcast(F32), ALU.subtract
                              ).then_inc(s["dve_cls_value"], 1)
            dve.wait_ge(s["loaded_tokens0"], 16 * 2 * HALVES)
            dve.wait_ge(s["pe_x_turned"], 1)
            ln(1, (0, NB), P)
            ln_apply(1, (0, NB), P)

            def lo_xT(n, bank, st):
                dve.wait_ge(s["act_xT_high"], n + 1)
                dve.tensor_tensor(xT_lo[:, :, st * P:st * P + P], ps[:, bank, :].rearrange("p (k t) -> p k t", k=KC),
                                  xT_hi[:, :, st * P:st * P + P].bitcast(F32), ALU.subtract).then_inc(s["dve_xT_low"], 1)

            lo_xT(1, 6, 0)
            lo_xT(2, 7, 1)

            def lo_qk(c, m, first=False):
                ci, bank = m // 2, FIRST_BANKS[m] if first else 6 + m % 2
                dve.wait_ge(s["act_qk_high"], c * 2 * KC + m + 1)

                def low(dst, src, bias, hi):
                    return dve.scalar_tensor_tensor(out=dst, in0=src, scalar=bias, in1=hi.bitcast(F32),
                                                    op0=ALU.add, op1=ALU.subtract)
                if m % 2 == 0:
                    for j in range(HPC):
                        rows, h = slice(j * DH, (j + 1) * DH), ci * HPC + j
                        e = low(q_lo[rows, h, :], ps[rows, bank, 0:BODY], q_bias[rows, ci:ci + 1], q_hi[rows, h, :])
                    if first:
                        e = low(qcls_lo[:, ci, :], ps[:, bank, BODY:KPAD], q_bias[:, ci:ci + 1], qcls_hi[:, ci, :])
                else:
                    e = low(k_lo[:, ci, :], ps[:, bank, 0:KPAD], k_bias[:, ci:ci + 1], k_hi[:, ci, :])
                e.then_inc(s["dve_qk_low"], 1)

            for m in range(2 * KC):
                lo_qk(0, m, True)
            dve.wait_ge(s["pool_head_mask"], 1)
            dve.wait_ge(s["dve_qk_low"], 2 * KC)
            for ci in range(KC):
                dve.tensor_scalar(qblk_hi[:, ci, :], mask[:, ci, :], qcls_hi[:, ci, 0:1].bitcast(F32), None,
                                  ALU.mult).then_inc(s["dve_spread"], 1)
                dve.tensor_scalar(qblk_lo[:, ci, :], mask[:, ci, :], qcls_lo[:, ci, 0:1].bitcast(F32), None,
                                  ALU.mult).then_inc(s["dve_spread"], 1)
            dve.wait_ge(s["pe_u"], 1)
            dve.wait_ge(s["pool_filled"], 6)
            dve.tensor_copy(u_sb[0:32, :], ps[0:32, 5, :]).then_inc(s["dve_u"], 1)
            dve.wait_ge(s["pool_constants"], 4)

            def top(c, j):
                dve.wait_ge(s["pe_scores"], c * NHEAD + j + 1)
                dve.tensor_reduce(negmax[:, j % 4, :], ps[:, 2 * (j % 2):2 * (j % 2) + 2, 0:KEYS], AX_X, ALU.max,
                                  negate=True).then_inc(s["dve_max"], 1)

            def norm(c, j):
                dve.wait_ge(s["act_exp"], c * NHEAD + j + 1)
                dve.reciprocal(rrec[:, j % 4, :], rowsum[:, j % 4, :]).then_inc(s["dve_recip"], 1)
                dve.wait_ge(s["dve_recip"], c * NHEAD + j + 1)
                for st in range(HALVES):
                    e = dve.tensor_scalar(prb[:, j % 4, st, 0:KEYS], prb[:, j % 4, st, 0:KEYS],
                                          rrec[:, j % 4, st:st + 1], None, ALU.mult)
                e.then_inc(s["dve_normed"], 1)

            def lo_ot(c, gr):
                dve.wait_ge(s["act_oT_high"], c * KC + gr + 1)
                dve.tensor_tensor(oT_lo[:, gr, :], ps[:, 5, 0:BODY], oT_hi[:, gr, :].bitcast(F32), ALU.subtract)
                dve.tensor_copy(ocls[:, gr, bass.ds(c, 1)], ps[:, 5, BODY:BODY + 1]).then_inc(s["dve_oT_low"], 1)

            def residual(c, st, bank):
                dve.wait_ge(s["pe_projected"], c * HALVES + st + 1)
                t = tok[:, st * NB + c, :]
                dve.tensor_tensor(t, ps[:, bank, :], t, ALU.add).then_inc(s["dve_residual"], 1)
                dve.wait_ge(s["dve_residual"], c * HALVES + st + 1)
                dve.bn_stats(st2[:, st * NB + c, :], t).then_inc(s["dve_stats2"], 1)

            def tck_copy(c):
                dve.wait_ge(s["pe_key_turned"], c + 1)
                dve.tensor_copy(pclsT[0:NHEAD, :], ps[0:NHEAD, 4, 0:BODY]).then_inc(s["dve_key_probs"], 1)

            def body(c, first, last):
                for j in range(NHEAD):
                    top(c, j)
                    if j == 2 and not first:
                        dve.wait_ge(s["pe_projected"], (c - 1) * HALVES)
                        tck_copy(c - 1)
                    if j >= 1:
                        norm(c, j - 1)
                    elif not first:
                        norm(c - 1, NHEAD - 1)
                        for m in QK_SLOT[NHEAD - 1]:
                            lo_qk(c, m)
                    if j == 1:
                        dve.wait_ge(s["pe_cls_scores"], c + 1)
                        dve.tensor_reduce(cstat[:, 0:1], ps[0:NHEAD, 6, 0:KEYS], AX_X, ALU.max, negate=True
                                          ).then_inc(s["dve_cls_max"], 1)
                    if j == 2:
                        dve.wait_ge(s["act_cls_exp"], c + 1)
                        dve.reciprocal(cstat[:, 2:3], cstat[:, 1:2]).then_inc(s["dve_cls_step"], 1)
                        dve.wait_ge(s["dve_cls_step"], 3 * c + 1)
                        dve.tensor_scalar(pc[:, 0:KEYS], pc[:, 0:KEYS], cstat[:, 2:3], None, ALU.mult
                                          ).then_inc(s["dve_cls_step"], 1)
                        dve.wait_ge(s["dve_cls_step"], 3 * c + 2)
                        dve.tensor_copy(pccT[0:NHEAD, bass.ds(c, 1)], pc[:, BODY:BODY + 1]).then_inc(s["dve_cls_step"], 1)
                    if j == 3:
                        if not first:
                            lo_ot(c - 1, 3)
                        if first:
                            dve.wait_ge(s["loaded_tokens"], 16 * 2 * (NB - 1) * HALVES)
                        if not last:
                            for i in range(2):
                                dve.bn_stats(lnst[:, i, :], tok[:, i * NB + c + 1, :]).then_inc(s["dve_ln_step"], 1)
                        dve.wait_ge(s["pe_cls_turned"], c + 1)
                        if not first:
                            dve.wait_ge(s["pool_cls_cols"], c * KC)
                        if not last:
                            dve.wait_ge(s["dve_ln_step"], c * 5 + 12)
                        dve.tensor_copy(ptc[:, :, :], ps[:, 6, 0:2 * NHEAD].rearrange("p (t h) -> p t h", t=2)
                                        ).then_inc(s["dve_cls_pT"], 1)
                        if not last:
                            for i in range(2):
                                dve.bn_aggr(lnmv[:, i, :], lnst[:, i, :]).then_inc(s["dve_ln_step"], 1)
                            dve.wait_ge(s["dve_ln_step"], c * 5 + 14)
                            dve.tensor_scalar(lnr[:, 0, :], lnmv[:, :, 1], EPS, None, ALU.add).then_inc(s["dve_ln_step"], 1)
                    if j == 5:
                        if not first:
                            residual(c - 1, 0, 6)
                        if not last:
                            dve.wait_ge(s["pool_step"], c + 15)
                            for i in range(2):
                                dve.tensor_scalar(xhat[:, i, :],
                                                  tok[:, i * NB + c + 1, :],
                                                  lnmv[:, i, 0:1], lnr[:, 1, i:i + 1], ALU.subtract, ALU.mult
                                                  ).then_inc(s["dve_xhat"], 1)
                    if j == 6 and not first:
                        residual(c - 1, 1, 7)
                    if j == 8 and not last:
                        lo_xT((c + 1) * HALVES + 1, 6, 0)
                        lo_xT((c + 1) * HALVES + 2, 7, 1)
                    if j in (7, 11, 15):
                        lo_ot(c, (j - 7) // 4)
                    for m in QK_SLOT[j - 1] if j >= 1 and not last else ():
                        lo_qk(c + 1, m)

            body(0, True, False)
            with dve.Fori(1, NB - 1) as c:
                body(c, False, False)
            body(NB - 1, False, True)
            last = NB - 1
            norm(last, NHEAD - 1)
            dve.wait_ge(s["pe_projected"], last * HALVES)
            tck_copy(last)
            lo_ot(last, 3)
            dve.wait_ge(s["dve_oT_low"], NB * KC)
            dve.wait_ge(s["pe_cls_scores"], NB)
            dve.memset(oc_hi[:, :, NB:P].bitcast(F32), 0.0).then_inc(s["dve_spread"], 1)
            dve.memset(oc_lo[:, :, NB:P].bitcast(F32), 0.0).then_inc(s["dve_spread"], 1)
            dve.tensor_copy(oc_hi[:, :, 0:NB], ocls[:, :, :]).then_inc(s["dve_spread"], 1)
            dve.wait_ge(s["dve_spread"], 12)
            dve.tensor_tensor(oc_lo[:, :, 0:NB], ocls[:, :, :], oc_hi[:, :, 0:NB].bitcast(F32), ALU.subtract
                              ).then_inc(s["dve_spread"], 1)
            residual(last, 0, 6)
            residual(last, 1, 7)
            dve.wait_ge(s["pe_cls_projected"], 1)
            dve.tensor_tensor(tok[0:NB, CLS, :], ps[0:NB, 6, :], tok[0:NB, CLS, :], ALU.add).then_inc(s["dve_attn_done"], 1)
            dve.wait_ge(s["dve_attn_done"], 1)
            dve.bn_stats(st2[:, CLS, :], tok[:, CLS, :]).then_inc(s["dve_stats2"], 1)
            dve.wait_ge(s["dve_stats2"], NT)
            for t in range(NT):
                dve.bn_aggr(mean_var[:, t, :], st2[:, t, :]).then_inc(s["dve_stats2"], 1)
            dve.wait_ge(s["dve_stats2"], 2 * NT)
            dve.tensor_scalar(rstd[:, :], mean_var[:, :, 1], EPS, None, ALU.add).then_inc(s["dve_stats2"], 1)
            dve.wait_ge(s["act_router_high"], 1)
            dve.tensor_tensor(rw_parts[:, :, 1, :], rw[:, :, :], rw_parts[:, :, 0, :].bitcast(F32), ALU.subtract
                              ).then_inc(s["dve_router_low"], 1)
            dve.wait_ge(s["pool_rstd"], 1)

            def normalise(t, buffer, done):
                dve.tensor_scalar(rows[:, buffer, :], tok[:, t, :], mean_var[:, t, 0:1], rstd[:, bass.ds(t, 1)],
                                  ALU.subtract, ALU.mult).then_inc(s[done], 1)

            def lo_turned(bank, u, done):
                dve.tensor_tensor(xnT_lo[:, u, :, :], ps[:, bank, :].rearrange("p (k t) -> p k t", k=KC),
                                  xnT_hi[:, u, :, :].bitcast(F32), ALU.subtract).then_inc(s[done], 1)

            def front(t, u, first):
                if not first:
                    dve.wait_ge(s["pe_xn_turned"], t - 1)
                normalise(t, u, "dve_xn")
                if not (first and u == 0):
                    dve.wait_ge(s["act_xnT_high"], t)
                    lo_turned(4 + (u + 1) % 2, (u + 1) % 2, "dve_xnT_low")

            tiles_in_pairs(dve, front)
            dve.wait_ge(s["act_xnT_high"], NT)
            lo_turned(4, 0, "dve_xnT_low")

            n_route = [0]

            def then(ins):
                n_route[0] += 1
                ins.then_inc(s["dve_route_step"], 1)
                dve.wait_ge(s["dve_route_step"], n_route[0])

            per_tile = lambda ap: bc(ap.unsqueeze(2), [P, NT, NE])
            dve.wait_ge(s["pe_logits"], NT)
            dve.wait_ge(s["loaded_router"], 32)
            dve.wait_ge(s["pool_routing_const"], 10)
            of_tile = ps[:, 7, 0:NT * 2 * NE].rearrange("p (t e) -> p t e", e=2 * NE)
            then(dve.tensor_tensor(probs[:, :, :], of_tile[:, :, 0:NE], bc(rb[:, :].unsqueeze(1), [P, NT, NE]),
                                   ALU.add))
            then(dve.tensor_tensor(probs[:, :, :], probs[:, :, :], of_tile[:, :, NE:2 * NE], ALU.add))
            then(dve.tensor_reduce(rsum[:, 0, :], probs[:, :, :], AX_X, ALU.max))
            then(dve.tensor_tensor(probs[:, :, :], probs[:, :, :], per_tile(rsum[:, 0, :]), ALU.subtract))
            dve.wait_ge(s["act_route_exp"], 1)
            then(dve.tensor_reduce(rsum[:, 1, :], probs[:, :, :], AX_X, ALU.add))
            then(dve.reciprocal(rsum[:, 2, :], rsum[:, 1, :]))
            then(dve.tensor_tensor(probs[:, :, :], probs[:, :, :], per_tile(rsum[:, 2, :]), ALU.mult))
            for t in range(NT):
                e = dve.max(top8[:, t, :], probs[:, t, :])
            then(e)
            for t in range(NT):
                e = dve.max_index(idx8[:, t, :], top8[:, t, :], probs[:, t, :])
            then(e)
            then(dve.tensor_copy(idxf[:, :, :], idx8[:, :, 0:SEL]))
            then(dve.tensor_tensor(chosen[:, :, :], bc(iota_e[:, :].unsqueeze(1), [P, COLS, NE]),
                                   bc(idxf[:, :, :].rearrange("p t k -> p (t k)").unsqueeze(2), [P, COLS, NE]),
                                   ALU.is_equal))
            last_tile = chosen[:, COLS - SEL:COLS, :]
            then(dve.tensor_scalar(last_tile, last_tile, valid[:, 0:1], None, ALU.mult))
            n_chosen = n_route[0]
            assert n_chosen == CHOSEN_STEP
            dve.wait_ge(s["pe_xn_turned"], NT)
            for t in range(4):
                normalise(t, t, "dve_row_ready")
            dve.wait_ge(s["pe_ranks"], 1)
            in_column = ps[:, 0, 0:COLS * NE].rearrange("p (c e) -> p c e", e=NE)
            of_column = ps[:, 1, 0:COLS * NE].rearrange("p (c e) -> p c e", e=NE)
            then(dve.tensor_copy(cum[:, 0, :, :], of_column))
            level, a = 1, 0
            while level < COLS:
                then(dve.tensor_copy(cum[:, 1 - a, 0:level, :], cum[:, a, 0:level, :]))
                then(dve.tensor_tensor(cum[:, 1 - a, level:, :], cum[:, a, level:, :], cum[:, a, 0:COLS - level, :],
                                       ALU.add))
                level, a = 2 * level, 1 - a
            then(dve.tensor_scalar(cnt[:, :], cum[:, a, COLS - 1, :], P / 2 - 0.5, 1.0 / P, ALU.add, ALU.mult))
            then(dve.tensor_scalar(cnt[:, :], cnt[:, :], ROUND_MAGIC, ROUND_MAGIC, ALU.add, ALU.subtract))
            then(dve.memset(tile0[:, 0:1], 0.0))
            for e in range(NE):
                then(dve.tensor_tensor(tile0[:, e + 1:e + 2], tile0[:, e:e + 1], cnt[:, e:e + 1], ALU.add))
            total, z = cum[:, a, :, :], cum[:, 1 - a, :, :]
            then(dve.tensor_tensor(z, total, of_column, ALU.subtract))
            then(dve.tensor_tensor(z, z, in_column, ALU.add))
            then(dve.tensor_scalar(cnt[:, :], tile0[:, 0:NE], float(P), None, ALU.mult))
            then(dve.tensor_tensor(z, z, bc(cnt[:, :].unsqueeze(1), [P, COLS, NE]), ALU.add))
            then(dve.tensor_tensor(z, z, chosen[:, :, :], ALU.mult))
            then(dve.tensor_reduce(slotf[:, :], z, AX_X, ALU.add))
            then(dve.tensor_tensor(slotf[:, COLS - SEL:COLS], slotf[:, COLS - SEL:COLS], spare[:, :], ALU.add))
            then(dve.tensor_copy(slot_of[:, :], slotf[:, :]))
            assert n_route[0] == ROUTE_STEPS, n_route[0]
            then(dve.tensor_tensor(rsum[:, 0, :], top8[:, :, 0], top8[:, :, 1], ALU.add))
            then(dve.reciprocal(rsum[:, 1, :], rsum[:, 0, :]))
            then(dve.tensor_tensor(gates[:, :, :], top8[:, :, 0:SEL], bc(rsum[:, 1, :].unsqueeze(2), [P, NT, SEL]),
                                   ALU.mult))
            then(dve.tensor_tensor(reached[:, :, 0:NE - 1], bc(iota_s[:, :].unsqueeze(2), [P, SLOTS, NE - 1]),
                                   bc(tile0[:, 1:NE].unsqueeze(1), [P, SLOTS, NE - 1]), ALU.is_ge))
            then(dve.tensor_reduce(iota_s[:, :], reached[:, :, 0:NE - 1], AX_X, ALU.add))
            then(dve.tensor_copy(expert_of[:, :], iota_s[:, :]))
            assert n_route[0] == ROUTE_STEPS + AFTER_SLOTS
            def lo_expert(e):
                dve.wait_ge(s["act_expert_high"], e + 1)
                dve.tensor_tensor(ew_lo[:, e, :, :], ew[:, e, :, :], ew_hi[:, e, :, :].bitcast(F32), ALU.subtract
                                  ).then_inc(s["dve_expert_low"], 1)

            for t in range(4, NT):
                dve.wait_ge(sent[t % 4], 16 * SEL * (t // 4))
                normalise(t, t % 4, "dve_row_ready")
                if t % 2 == 1 and t // 2 - 2 < NE:
                    lo_expert(t // 2 - 2)
            for e in range((NT - 1) // 2 - 2, NE):
                lo_expert(e)

            def lo_xs(i, u):
                dve.wait_ge(s["act_slotT_high"], i + 1)
                lo_turned(4 + u % 2, u % 2, "dve_slotT_low")

            def add_bias(i, u):
                e = dve.value_load(expert_of[0:1, bass.ds(i, 1)], min_val=0, max_val=NE - 1)
                dve.wait_ge(s["pe_expert"], i + 1)
                dve.tensor_tensor(ps[:, u, :], ps[:, u, :], eb[:, e, :], ALU.add).then_inc(s["dve_bias_added"], 1)

            dve.wait_ge(s["loaded_biases"], 32)
            lo_xs(0, 0)
            with dve.Fori(0, SLOTS // 2 - 1) as k:
                for u in range(2):
                    lo_xs(2 * k + u + 1, u + 1)
                    add_bias(2 * k + u, u)
            lo_xs(SLOTS - 1, 1)
            add_bias(SLOTS - 2, 0)
            add_bias(SLOTS - 1, 1)

            dve.wait_ge(s["act_out_w_high"], 1)
            dve.tensor_tensor(ow_lo[:, :, :], ow[:, :, :], ow_hi[:, :, :].bitcast(F32), ALU.subtract
                              ).then_inc(s["dve_out_w_low"], 1)

            def lo_combT(t, u):
                dve.wait_ge(s["act_combT_high"], t + 1)
                dve.tensor_tensor(combT_lo[:, u, :, :], ps[:, 4 + u, :].rearrange("p (k t) -> p k t", k=KC),
                                  combT_hi[:, u, :, :].bitcast(F32), ALU.subtract).then_inc(s["dve_combT_low"], 1)

            def combine(t, u, first):
                dve.wait_ge(got_y[u], 16 * (t - u) + 32)
                if not first:
                    dve.wait_ge(s["pe_comb_turned"], t - 1)
                dve.tensor_scalar(comb[:, u, :], rows[:, 2 * u, :], gates[:, t, 0:1], None, ALU.mult
                                  ).then_inc(s["dve_combined"], 1)
                dve.wait_ge(s["dve_combined"], 2 * t + 1)
                dve.scalar_tensor_tensor(out=comb[:, u, :], in0=rows[:, 2 * u + 1, :], scalar=gates[:, t, 1:2],
                                         in1=comb[:, u, :], op0=ALU.mult, op1=ALU.add).then_inc(s["dve_combined"], 1)
                if not (first and u == 0):
                    lo_combT(t - 1, (u + 1) % 2)
                if not first:
                    residual_out(t - 2, u)

            def residual_out(t, u):
                dve.wait_ge(s["pe_out"], t + 1)
                dve.tensor_tensor(tok[:, t, :], ps[:, 6 + u, :], tok[:, t, :], ALU.add).then_inc(s["dve_out"], 1)

            dve.wait_ge(s["pool_out_bias"], NT)
            tiles_in_pairs(dve, combine)
            lo_combT(NT - 1, 0)
            residual_out(NT - 2, 1)
            residual_out(NT - 1, 0)

        @block.tensor
        def _(pe):
            pe.wait_ge(s["pool_identity"], 2)

            def w_turn(raw, sem_t, bank0):
                for ic in range(KC):
                    for o in range(KC):
                        mm = pe.transpose(ps[:, bank0 + ic, o * P:(o + 1) * P], raw[:, o, ic * P:(ic + 1) * P], ident[:, :])
                    mm.then_inc(s[sem_t], 1)

            pe.wait_ge(s["act_w_scaled"], KC)
            w_turn(w_raw[:, 0], "pe_w_turned", 4)
            pe.wait_ge(s["act_w_scaled"], 2 * KC)
            pe.wait_ge(s["dve_w_low"], KC)
            w_turn(w_raw[:, 1], "pe_w_turned", 4)

            def turn(n, parts):
                if n >= 4:
                    pe.wait_ge(s["act_table_kept"], n - 3)
                for k, part in enumerate(parts):
                    for q in range(4):
                        mm = pe.matmul(ps[:, n % 4, q * P:(q + 1) * P], part(q), ident[:, :], is_transpose=True,
                                       start=(k == 0 and q == 0), stop=(k == len(parts) - 1 and q == 3),
                                       skip_group_check=True)
                mm.then_inc(s["pe_table_turned"], 1)

            for hf in range(HALVES):
                base = hf * 32
                if hf == 0:
                    low = r_low
                    pe.wait_ge(s["dve_r_low"], 1)
                else:
                    low = r_low2
                    pe.wait_ge(s["pool_power_step"], CHAIN)
                for q in range(8):
                    turn(base + q, [lambda i, q=q, low=low: low[:, 4 * q + i, :, :].rearrange("p s n -> p (s n)")])
                for n in range(12):
                    if n < 4:
                        pe.wait_ge(s["dve_r_upper"], hf * 4 + n + 1)
                    else:
                        pe.wait_ge(s["dve_l_product"], hf * NB + n - 4 + 1)
                    for k in range(2):
                        turn(base + 8 + 2 * n + k,
                             [lambda i, w=w, n=n, k=k: ring[:, n % 2, w, 4 * k + i, :, :].rearrange("p s n -> p (s n)")
                              for w in range(2)])
                pe.wait_ge(s["act_table_kept"], base + 32)
                if hf == 0:
                    pe.wait_ge(s["dve_w_low"], 2 * KC)
                for hb in range(NHB):
                    n = hf * NHB + hb
                    if n >= 2:
                        pe.wait_ge(s["act_tokens_kept"], n - 1)
                    for i in range(HB):
                        for hp in range(2):
                            h = hp * 64 + hb * HB + i
                            bank = 4 + 2 * (n % 2) + i // 8
                            mm = pe.matmul(ps[hp * 64:hp * 64 + 64, bank, (i % 8) * NBP:(i % 8 + 1) * NBP],
                                           lT[:, h, :], rT[:, h, :], start=(i % 8 == 0), stop=(i % 8 == 7),
                                           skip_group_check=True)
                    mm.then_inc(s["pe_tokens"], 1)

            def split3(out_ap, lhs, rhs, start, stop, skip=False):
                (lh, ll), (rh, rl) = lhs, rhs
                for i, (a, b) in enumerate(((lh, rh), (ll, rh), (lh, rl))):
                    mm = pe.matmul(out_ap, a, b, start=start and i == 0, stop=stop and i == 2, skip_group_check=skip)
                return mm

            def x_turn(bank, i, rows=P):
                for k in range(KC):
                    mm = pe.transpose(ps[:, bank, k * rows:(k + 1) * rows], xhat[0:rows, i, k * P:(k + 1) * P],
                                      ident[0:rows, 0:rows])
                mm.then_inc(s["pe_x_turned"], 1)

            pe.wait_ge(s["act_tokens_kept"], HALVES * NHB)
            pe.wait_ge(s["dve_xhat"], 1)
            x_turn(7, 0, NB)
            for i in range(2):
                pe.wait_ge(s["loaded_wo" if i else "loaded_wv"], 16)
                if i == 1:
                    pe.wait_ge(s["dve_wvo_low"], KC)
                w_turn(w_raw2[:, i], "pe_wvo_turned", 0)
            pe.wait_ge(s["dve_wvo_low"], KC)
            pe.wait_ge(s["dve_xT_low"], 1)
            for ci in range(KC):
                for ic in range(KC):
                    w = slice(ci * P, (ci + 1) * P)
                    mm = split3(ps[:, 4, 2 * ci:2 * ci + 2], (wvT_hi[:, ic, w], wvT_lo[:, ic, w]),
                                (xT_hi[:, ic, BODY:KPAD], xT_lo[:, ic, BODY:KPAD]), ic == 0, ic == KC - 1, True)
            mm.then_inc(s["pe_cls_value"], 1)
            pe.wait_ge(s["dve_xhat"], 3)
            x_turn(6, 0)
            pe.wait_ge(s["dve_xhat"], 4)
            x_turn(7, 1)

            def qk(c, m, bank):
                hi, lo = (wqT_hi, wqT_lo) if m % 2 == 0 else (wkT_hi, wkT_lo)
                ci = m // 2
                for ic in range(KC):
                    w = slice(ci * P, (ci + 1) * P)
                    mm = split3(ps[:, bank, 0:KPAD], (hi[:, ic, w], lo[:, ic, w]),
                                (xT_hi[:, ic, :], xT_lo[:, ic, :]), ic == 0, ic == KC - 1)
                mm.then_inc(s["pe_qk"], 1)

            def qk_wait(c, m):
                if m == 0:
                    pe.wait_ge(s["dve_xT_low"], c * HALVES + 3)
                elif m >= 2:
                    pe.wait_ge(s["dve_qk_low"], c * 2 * KC + m - 1)

            pe.wait_ge(s["dve_xT_low"], 3)
            pe.wait_ge(s["dve_wvo_low"], 2 * KC)
            pe.wait_ge(s["dve_cls_value"], 2 * KC)
            for m in range(2 * KC):
                qk(0, m, FIRST_BANKS[m])
            pe.wait_ge(s["dve_qk_low"], 2 * KC)
            pe.wait_ge(s["pool_constants"], 4)
            pe.wait_ge(s["loaded_bo"], 16)
            for ci in range(KC):
                split3(ps[:, 5, :], (vblk_hi[:, ci, :], vblk_lo[:, ci, :]), (woT_hi[:, ci, :], woT_lo[:, ci, :]),
                       ci == 0, False)
            pe.matmul(ps[:, 5, :], e16[:, :], bo_row[:, :], start=False, stop=True).then_inc(s["pe_u"], 1)

            def scores(c, j):
                ci = j // HPC
                if j % HPC == 0:
                    pe.wait_ge(s["dve_qk_low"], c * 2 * KC + 2 * ci + 2)
                for st in range(HALVES):
                    w = slice(st * P, (st + 1) * P)
                    mm = split3(ps[:, 2 * (j % 2) + st, 0:KPAD], (q_hi[:, j, w], q_lo[:, j, w]),
                                (k_hi[:, ci, :], k_lo[:, ci, :]), True, True)
                mm.then_inc(s["pe_scores"], 1)

            def turn_p(c, j):
                pe.wait_ge(s["dve_normed"], c * NHEAD + j + 1)
                for tt in range(HALVES):
                    for st in range(HALVES):
                        mm = pe.transpose(ps[:, 4, tt * BODY + st * P:tt * BODY + (st + 1) * P],
                                          prb[:, j % 4, st, tt * P:(tt + 1) * P], ident[:, :])
                mm.then_inc(s["pe_p_turned"], 1)

            def pv(c, gr):
                pe.wait_ge(s["act_pT_kept"], c * NHEAD + (gr + 1) * HPC)
                pe.wait_ge(s["pool_cls_cols"], c * KC + gr + 1)
                for tt in range(HALVES):
                    for j in range(HPC):
                        h = gr * HPC + j
                        mm = pe.matmul(ps[j * DH:(j + 1) * DH, 5, 0:KEYS], v_sb[:, tt, h * DH:(h + 1) * DH],
                                       pts[:, h % 8, tt, 0:KEYS], start=(tt == 0), stop=(tt == HALVES - 1))
                mm.then_inc(s["pe_pv"], 1)

            def cls_scores(c):
                for ci in range(KC):
                    mm = split3(ps[:, 6, 0:KPAD], (qblk_hi[:, ci, :], qblk_lo[:, ci, :]),
                                (k_hi[:, ci, :], k_lo[:, ci, :]), ci == 0, ci == KC - 1)
                mm.then_inc(s["pe_cls_scores"], 1)

            def cls_turn(c):
                for tt in range(HALVES):
                    mm = pe.transpose(ps[:, 6, tt * NHEAD:(tt + 1) * NHEAD], pc[:, tt * P:(tt + 1) * P],
                                      ident[0:NHEAD, 0:NHEAD])
                mm.then_inc(s["pe_cls_turned"], 1)

            def values(c, st):
                for ic in range(KC):
                    w = slice(st * P, (st + 1) * P)
                    mm = split3(ps[:, 7, :], (xT_hi[:, ic, w], xT_lo[:, ic, w]),
                                (wvT_hi[:, ic, :], wvT_lo[:, ic, :]), ic == 0, ic == KC - 1)
                mm.then_inc(s["pe_values"], 1)

            def key_turn(c):
                pe.wait_ge(s["pool_key_col"], (c + 1) * NHEAD)
                pe.wait_ge(s["act_pT_kept"], (c + 1) * NHEAD)
                for st in range(HALVES):
                    mm = pe.transpose(ps[0:NHEAD, 4, st * P:(st + 1) * P], pcls[:, st, :], ident[:, :])
                mm.then_inc(s["pe_key_turned"], 1)

            def project(c, st, bank):
                w = slice(st * P, (st + 1) * P)
                pe.matmul(ps[:, bank, :], pclsT[:, w], u_sb[:, :], start=True, stop=False)
                for ic in range(KC):
                    mm = split3(ps[:, bank, :], (oT_hi[:, ic, w], oT_lo[:, ic, w]),
                                (woT_hi[:, ic, :], woT_lo[:, ic, :]), False, ic == KC - 1)
                mm.then_inc(s["pe_projected"], 1)

            def body(c, first, last):
                for j in range(NHEAD):
                    if j >= 2 or not first:
                        pe.wait_ge(s["act_exp"], c * NHEAD + j - 1)
                    scores(c, j)
                    if j >= 3:
                        pe.wait_ge(s["act_pT_kept"], c * NHEAD + j - 2)
                    elif j == 2:
                        if not first:
                            pe.wait_ge(s["act_pT_kept"], c * NHEAD)
                    elif not first:
                        pe.wait_ge(s["act_pT_kept"], c * NHEAD - 2 + j)
                    if j >= 2:
                        if j == 3 and not first:
                            pe.wait_ge(s["dve_key_probs"], c)
                        if j == 2 and not first:
                            key_turn(c - 1)
                            pe.wait_ge(s["dve_oT_low"], c * KC - 1)
                            pv(c - 1, 3)
                            pe.wait_ge(s["dve_key_probs"], c)
                        turn_p(c, j - 2)
                    elif not first:
                        turn_p(c - 1, NHEAD - 2 + j)
                    if j == 1:
                        pe.wait_ge(s["dve_qk_low"], (c + 1) * 2 * KC)
                        if first:
                            pe.wait_ge(s["dve_spread"], 1 + 2 * KC)
                        cls_scores(c)
                    if j == 1:
                        values(c, 0)
                    if j == 3:
                        pe.wait_ge(s["dve_cls_step"], 3 * c + 3)
                        pe.wait_ge(s["act_cls_exp"], c + 1)
                        pe.wait_ge(s["act_v_kept"], c * HALVES + 1)
                        values(c, 1)
                        cls_turn(c)
                    if j == 4 and not first:
                        pe.wait_ge(s["dve_key_probs"], c)
                        pe.wait_ge(s["dve_oT_low"], c * KC)
                        pe.wait_ge(s["dve_cls_pT"], c + 1)
                        project(c - 1, 0, 6)
                    if j == 5 and not first:
                        pe.wait_ge(s["act_v_kept"], c * HALVES + 2)
                        project(c - 1, 1, 7)
                    if j == 7 and not last:
                        if first:
                            pe.wait_ge(s["dve_u"], 1)
                            pe.wait_ge(s["dve_cls_pT"], c + 1)
                            pe.wait_ge(s["act_v_kept"], c * HALVES + 2)
                        else:
                            pe.wait_ge(s["dve_residual"], c * HALVES - 1)
                        pe.wait_ge(s["dve_xhat"], (c + 1) * HALVES + 3)
                        x_turn(6, 0)
                        if not first:
                            pe.wait_ge(s["dve_residual"], c * HALVES)
                        pe.wait_ge(s["dve_xhat"], (c + 1) * HALVES + 4)
                        x_turn(7, 1)
                    for m in QK_SLOT[j] if not last else ():
                        qk_wait(c + 1, m)
                        qk(c + 1, m, 6 + m % 2)
                    if j in (6, 10, 14):
                        if j == 6:
                            pe.wait_ge(s["act_v_kept"], (c + 1) * HALVES)
                        if j > 6 or not first:
                            pe.wait_ge(s["dve_oT_low"], c * KC + (j - 6) // 4)
                        pv(c, (j - 6) // 4)

            body(0, True, False)
            with pe.Fori(1, NB - 1) as c:
                body(c, False, False)
            body(NB - 1, False, True)
            last = NB - 1
            pe.wait_ge(s["act_pT_kept"], NB * NHEAD - 2)
            turn_p(last, NHEAD - 2)
            pe.wait_ge(s["act_pT_kept"], NB * NHEAD - 1)
            turn_p(last, NHEAD - 1)
            key_turn(last)
            pe.wait_ge(s["dve_oT_low"], NB * KC - 1)
            pv(last, 3)
            pe.wait_ge(s["dve_key_probs"], NB)
            pe.wait_ge(s["dve_oT_low"], NB * KC)
            project(last, 0, 6)
            project(last, 1, 7)
            pe.wait_ge(s["dve_spread"], 13)
            pe.wait_ge(s["dve_residual"], NB * HALVES - 1)
            pe.matmul(ps[:, 6, :], pccT[:, :], u_sb[:, :], start=True, stop=False)
            for ic in range(KC):
                mm = split3(ps[:, 6, :], (oc_hi[:, ic, :], oc_lo[:, ic, :]), (woT_hi[:, ic, :], woT_lo[:, ic, :]),
                            False, ic == KC - 1)
            mm.then_inc(s["pe_cls_projected"], 1)
            pe.wait_ge(s["dve_attn_done"], 1)

            def turn(src, bank):
                for k in range(KC):
                    mm = pe.transpose(ps[:, bank, k * P:(k + 1) * P], src[:, k * P:(k + 1) * P], ident[:, :])
                return mm

            def route(t, u):
                pe.wait_ge(s["dve_xnT_low"], t + 1)
                for k in range(KC):
                    pe.matmul(ps[:, 7, bass.ds(t * 2 * NE, 2 * NE)], xnT_hi[:, u, k, :], rw_parts[:, k, :, :],
                              start=(k == 0), stop=False)
                    mm = pe.matmul(ps[:, 7, bass.ds(t * 2 * NE, NE)], xnT_lo[:, u, k, :], rw_parts[:, k, 0, :],
                                   start=False, stop=(k == KC - 1))
                mm.then_inc(s["pe_logits"], 1)

            def front(t, u, first):
                pe.wait_ge(s["dve_xn"], t + 1)
                turn(rows[:, u], 4 + u).then_inc(s["pe_xn_turned"], 1)
                if not (first and u == 0):
                    route(t - 1, (u + 1) % 2)

            pe.wait_ge(s["dve_router_low"], 1)
            tiles_in_pairs(pe, front)
            route(NT - 1, 0)
            pe.wait_ge(s["dve_route_step"], CHOSEN_STEP)
            flat = chosen[:, :, :].rearrange("p c e -> p (c e)")
            pe.matmul(ps[:, 0, 0:COLS * NE], before[:, :], flat, start=True, stop=True)
            pe.matmul(ps[:, 1, 0:COLS * NE], all_one[:, :], flat, start=True, stop=True).then_inc(s["pe_ranks"], 1)

            def turn_xs(i, u):
                pe.wait_ge(ld_xs[u % 2], 8 * (i - u % 2) + 16)
                turn(rows[:, u % 2], 4 + u % 2).then_inc(s["pe_slot_turned"], 1)

            def expert(i, u, first):
                e = pe.value_load(expert_of[0:1, bass.ds(i, 1)], min_val=0, max_val=NE - 1)
                pe.wait_ge(s["dve_slotT_low"], i + 1)
                if not first:
                    pe.wait_ge(s["act_gelu"], i - 1)
                for k in range(KC):
                    mm = split3(ps[:, u, :], (xnT_hi[:, u, k, :], xnT_lo[:, u, k, :]),
                                (ew_hi[:, e, k, :], ew_lo[:, e, k, :]), k == 0, k == KC - 1)
                mm.then_inc(s["pe_expert"], 1)

            pe.wait_ge(s["dve_route_step"], ROUTE_STEPS + AFTER_SLOTS)
            pe.wait_ge(s["dve_expert_low"], NE)
            turn_xs(0, 0)
            turn_xs(1, 1)
            expert(0, 0, True)
            turn_xs(2, 0)
            expert(1, 1, True)
            with pe.Fori(1, SLOTS // 2 - 1) as k:
                for u in range(2):
                    turn_xs(2 * k + u + 1, u + 1)
                    expert(2 * k + u, u, False)
            turn_xs(SLOTS - 1, 1)
            expert(SLOTS - 2, 0, False)
            expert(SLOTS - 1, 1, False)

            def project_out(t, u):
                pe.wait_ge(s["dve_combT_low"], t + 1)
                for k in range(KC):
                    mm = split3(ps[:, 6 + u, :], (combT_hi[:, u, k, :], combT_lo[:, u, k, :]),
                                (ow_hi[:, k, :], ow_lo[:, k, :]), k == 0, k == KC - 1)
                mm.then_inc(s["pe_out"], 1)

            def back(t, u, first):
                pe.wait_ge(s["dve_combined"], 2 * t + 2)
                turn(comb[:, u], 4 + u).then_inc(s["pe_comb_turned"], 1)
                if not (first and u == 0):
                    project_out(t - 1, (u + 1) % 2)

            pe.wait_ge(s["dve_out_w_low"], 1)
            tiles_in_pairs(pe, back)
            pe.wait_ge(s["dve_out"], NT - 2)
            project_out(NT - 1, 0)


_INS = ['x', 'cls_tok', 'L0_tok_log_dt', 'L0_tok_B_ri', 'L0_tok_inv_A_real', 'L0_tok_A_imag', 'L0_attn_Wq',
        'L0_attn_bq', 'L0_attn_Wk', 'L0_attn_bk', 'L0_attn_Wv', 'L0_attn_bv', 'L0_attn_Wo', 'L0_attn_bo',
        'L0_attn_spiral_weight', 'L0_attn_helix_rotation', 'L0_ffn_router_w', 'L0_ffn_router_b',
        'L0_ffn_expert_w', 'L0_ffn_expert_b', 'L0_ffn_out_w', 'L0_ffn_out_b']
_OUTS = [((8, 257, 512), 'float32')]


def kernel(**inputs):
    import numpy as _np
    import concourse.bacc as _bacc
    from concourse import mybir as _mybir
    from concourse.bass_utils import run_bass_kernel_spmd as _run

    nc = _bacc.Bacc("TRN2", target_bir_lowering=False, num_devices=1)
    arrays, args = {}, []
    for name in _INS:
        a = _np.ascontiguousarray(inputs[name])
        arrays[f"in_{name}_dram"] = a
        args.append(nc.dram_tensor(f"in_{name}_dram", a.shape, _mybir.dt.from_np(a.dtype), kind="ExternalInput").ap())
    for i, (shape, dtype) in enumerate(_OUTS):
        dt = _mybir.dt.from_np(_np.dtype(dtype))
        args.append(nc.dram_tensor(f"out_{i}_dram", shape, dt, kind="ExternalOutput").ap())
    vit_tower_kernel(nc, *args)
    r = _run(nc, [arrays], core_ids=[0])
    got = tuple(r.results[0][f"out_{i}_dram"] for i in range(len(_OUTS)))
    return got[0]
```
